# Optimizing a Trainium2 kernel written in Bass

```python
import numpy as np
import jax
import jax.numpy as jnp

def _softmax(x, axis=-1):
    return jax.nn.softmax(x, axis=axis)

def _gelu(x):
    return jax.nn.gelu(x, approximate=True)

def _silu(x):
    return jax.nn.silu(x)

def _sigmoid(x):
    return jax.nn.sigmoid(x)

def _layernorm(x, axis=-1, eps=1e-05):
    m = jnp.mean(x, axis=axis, keepdims=True)
    v = jnp.var(x, axis=axis, keepdims=True)
    return (x - m) / jnp.sqrt(v + eps)

def _scatter_add(tgt, idx, src, axis=0):
    return tgt.at[idx].add(src)

def _segment_sum(src, seg, n):
    return jax.ops.segment_sum(src, seg, n)
kernel_name = 'mk_gnn_preln_d4_gnn_r32_7f8534'

def setup_inputs(seed: int=0):
    np.random.seed(seed)
    _w = jnp.asarray

    def _rec_inputs():
        import jax
        import jax.numpy as jnp
        _gk = jax.random.key(seed)
        x = -0.0002117 + 1 * jax.random.normal(jax.random.fold_in(_gk, 1), (3125, 256), jnp.float32)
        src = jax.random.randint(jax.random.fold_in(_gk, 2), (50000,), 0, 3125, jnp.int32)
        dst = jax.random.randint(jax.random.fold_in(_gk, 3), (50000,), 0, 3125, jnp.int32)
        _o = jnp.argsort(dst, stable=True)
        src = src[_o]
        dst = dst[_o]
        edge_weight = jax.random.uniform(jax.random.fold_in(_gk, 15), (50000,), jnp.float32, 0.0, 1)
        return (x, src, dst, edge_weight)
    x, src, dst, edge_weight = _rec_inputs()

    def _L0_gnn_setup():
        import jax, jax.numpy as jnp
        import numpy as np
        N = 3125
        E = 100000
        DI = 256
        DO = 256
        BN_EPS = 1e-05

        def _bn_relu(h, gamma, beta):
            mean = jnp.mean(h, axis=0)
            var = jnp.var(h, axis=0)
            hn = (h - mean) * jax.lax.rsqrt(var + BN_EPS)
            return jax.nn.relu(hn * gamma + beta)
        key = jax.random.key(seed)
        ks = jax.random.split(key, 6)
        x = jax.random.normal(ks[0], (N, DI), dtype=jnp.float32)
        edge_row = jax.random.randint(ks[1], (E,), 0, N, dtype=jnp.int32)
        edge_col = jax.random.randint(ks[2], (E,), 0, N, dtype=jnp.int32)
        edge_vals = jnp.ones((E,), dtype=jnp.float32)
        eps = jnp.zeros((1,), dtype=jnp.float32)
        W1 = jax.random.normal(ks[3], (DI, DO), dtype=jnp.float32) * 0.05
        b1 = jnp.zeros((DO,), dtype=jnp.float32)
        g1 = jnp.ones((DO,), dtype=jnp.float32)
        be1 = jnp.zeros((DO,), dtype=jnp.float32)
        W2 = jax.random.normal(ks[4], (DO, DO), dtype=jnp.float32) * 0.05
        b2 = jnp.zeros((DO,), dtype=jnp.float32)
        g2 = jnp.ones((DO,), dtype=jnp.float32)
        be2 = jnp.zeros((DO,), dtype=jnp.float32)
        return {'x': x, 'edge_row': edge_row, 'edge_col': edge_col, 'edge_vals': edge_vals, 'eps': eps, 'W1': W1, 'b1': b1, 'g1': g1, 'be1': be1, 'W2': W2, 'b2': b2, 'g2': g2, 'be2': be2}
    _L0_gnn_all = _L0_gnn_setup()
    _L0_gnn_in = {k: v for k, v in _L0_gnn_all.items() if k in ('eps', 'W1', 'b1', 'g1', 'be1', 'W2', 'b2', 'g2', 'be2')}
    del _L0_gnn_all

    def _L1_gnn_setup():
        import jax, jax.numpy as jnp
        import numpy as np
        NEG_SLOPE = 0.01

        def _leaky(x):
            return jnp.where(x >= 0, x, NEG_SLOPE * x)

        def _gcn(x, W, b, src, dst, w, n):
            h = x @ W
            agg = jax.ops.segment_sum(w[:, None] * h[src], dst, num_segments=n)
            return agg + b
        key = jax.random.key(seed)
        ks = jax.random.split(key, 10)
        N, E, IN, HID, OUT, B = (3125, 9375, 256, 256, 256, 128)
        features = jax.random.normal(ks[0], (N, IN), dtype=jnp.float32)
        values = jax.random.uniform(ks[1], (E,), dtype=jnp.float32)
        s = 1.0 / np.sqrt(IN)
        W1 = jax.random.normal(ks[2], (IN, HID), dtype=jnp.float32) * s
        b1 = jnp.zeros((HID,), dtype=jnp.float32)
        W2 = jax.random.normal(ks[3], (HID + IN, OUT), dtype=jnp.float32) * (1.0 / np.sqrt(HID + IN))
        b2 = jnp.zeros((OUT,), dtype=jnp.float32)
        Wl = jax.random.normal(ks[4], (HID + OUT, IN), dtype=jnp.float32) * (1.0 / np.sqrt(HID + OUT))
        bl = jnp.zeros((IN,), dtype=jnp.float32)
        adjs = jax.random.randint(ks[5], (2, E), 0, N, dtype=jnp.int64)
        batch = jnp.sort(jax.random.randint(ks[6], (N,), 0, B, dtype=jnp.int64))
        root_idx = jax.random.randint(ks[7], (B,), 0, N, dtype=jnp.int64)
        return {'features': features, 'values': values, 'W1': W1, 'b1': b1, 'W2': W2, 'b2': b2, 'Wl': Wl, 'bl': bl, 'adjs': adjs, 'batch': batch, 'root_idx': root_idx}
    _L1_gnn_all = _L1_gnn_setup()
    _L1_gnn_in = {k: v for k, v in _L1_gnn_all.items() if k in ('W1', 'b1', 'W2', 'b2', 'Wl', 'bl', 'root_idx')}
    del _L1_gnn_all

    def _L2_gnn_setup():
        import jax, jax.numpy as jnp
        import numpy as np
        N_NODES = 3125
        N_EDGES = 50000
        IN_FEATS = 256
        OUT_FEATS = 256
        key = jax.random.key(seed)
        k1, k2, k3, k4, k5, k6 = jax.random.split(key, 6)
        h = jax.random.normal(k1, (N_NODES, IN_FEATS), dtype=jnp.float32)
        norm = jax.random.uniform(k2, (N_NODES, 1), dtype=jnp.float32)
        W = jax.random.normal(k3, (OUT_FEATS, IN_FEATS), dtype=jnp.float32) * (1.0 / np.sqrt(IN_FEATS))
        b = jax.random.normal(k4, (OUT_FEATS,), dtype=jnp.float32) * 0.01
        src = jax.random.randint(k5, (N_EDGES,), 0, N_NODES, dtype=jnp.int32)
        dst = jax.random.randint(k6, (N_EDGES,), 0, N_NODES, dtype=jnp.int32)
        return {'h': h, 'norm': norm, 'W': W, 'b': b, 'src': src, 'dst': dst}
    _L2_gnn_all = _L2_gnn_setup()
    _L2_gnn_in = {k: v for k, v in _L2_gnn_all.items() if k in ('W', 'b')}
    del _L2_gnn_all

    def _L3_gnn_setup():
        import jax, jax.numpy as jnp
        import numpy as np
        N_NODES = 10000
        N_EDGES = 5000
        F_IN = 256
        HEADS = 4
        F_OUT = 256
        NEG_SLOPE = 0.2
        EPS = 1e-05

        def gat_conv(x, src, dst, W, a_src, a_dst, bias, concat):
            N = x.shape[0]
            H, C = a_src.shape
            h = (x @ W).reshape(N, H, C)
            al_s = jnp.einsum('nhc,hc->nh', h, a_src)
            al_d = jnp.einsum('nhc,hc->nh', h, a_dst)
            e = jax.nn.leaky_relu(al_s[src] + al_d[dst], NEG_SLOPE)
            m = jax.ops.segment_max(e, dst, num_segments=N)
            ex = jnp.exp(e - m[dst])
            denom = jax.ops.segment_sum(ex, dst, num_segments=N)
            alpha = ex / denom[dst]
            out = jax.ops.segment_sum(h[src] * alpha[:, :, None], dst, num_segments=N)
            out = out.reshape(N, H * C) if concat else out.mean(axis=1)
            return out + bias

        def graph_norm(x, w, b, ms):
            mean = x.mean(axis=0, keepdims=True)
            sh = x - ms * mean
            var = (sh * sh).mean(axis=0, keepdims=True)
            return w * sh / jnp.sqrt(var + EPS) + b
        key = jax.random.key(seed)
        ks = jax.random.split(key, 12)
        H1 = HEADS * F_IN
        s = 0.05
        return {'x': jax.random.normal(ks[0], (N_NODES, F_IN), jnp.float32), 'edge_index': jax.random.randint(ks[1], (2, N_EDGES), 0, N_NODES, jnp.int64), 'W1': jax.random.normal(ks[2], (F_IN, HEADS * F_IN), jnp.float32) * s, 'att_src1': jax.random.normal(ks[3], (HEADS, F_IN), jnp.float32) * s, 'att_dst1': jax.random.normal(ks[4], (HEADS, F_IN), jnp.float32) * s, 'b1': jnp.zeros((H1,), jnp.float32), 'gn_w': jnp.ones((H1,), jnp.float32), 'gn_b': jnp.zeros((H1,), jnp.float32), 'gn_ms': jnp.ones((H1,), jnp.float32), 'W2': jax.random.normal(ks[5], (H1, F_OUT), jnp.float32) * s, 'att_src2': jax.random.normal(ks[6], (1, F_OUT), jnp.float32) * s, 'att_dst2': jax.random.normal(ks[7], (1, F_OUT), jnp.float32) * s, 'b2': jnp.zeros((F_OUT,), jnp.float32)}
    _L3_gnn_all = _L3_gnn_setup()
    _L3_gnn_in = {k: v for k, v in _L3_gnn_all.items() if k in ('W1', 'att_src1', 'att_dst1', 'b1', 'gn_w', 'gn_b', 'gn_ms', 'W2', 'att_src2', 'att_dst2', 'b2')}
    del _L3_gnn_all
    return {'x': x, 'src': src, 'dst': dst, 'edge_weight': edge_weight, 'L0_gnn_eps': _L0_gnn_in['eps'], 'L0_gnn_W1': _L0_gnn_in['W1'], 'L0_gnn_b1': _L0_gnn_in['b1'], 'L0_gnn_g1': _L0_gnn_in['g1'], 'L0_gnn_be1': _L0_gnn_in['be1'], 'L0_gnn_W2': _L0_gnn_in['W2'], 'L0_gnn_b2': _L0_gnn_in['b2'], 'L0_gnn_g2': _L0_gnn_in['g2'], 'L0_gnn_be2': _L0_gnn_in['be2'], 'L1_gnn_W1': _L1_gnn_in['W1'], 'L1_gnn_b1': _L1_gnn_in['b1'], 'L1_gnn_W2': _L1_gnn_in['W2'], 'L1_gnn_b2': _L1_gnn_in['b2'], 'L1_gnn_Wl': _L1_gnn_in['Wl'], 'L1_gnn_bl': _L1_gnn_in['bl'], 'L1_gnn_root_idx': _L1_gnn_in['root_idx'], 'L2_gnn_W': _L2_gnn_in['W'], 'L2_gnn_b': _L2_gnn_in['b'], 'L3_gnn_W1': _L3_gnn_in['W1'], 'L3_gnn_att_src1': _L3_gnn_in['att_src1'], 'L3_gnn_att_dst1': _L3_gnn_in['att_dst1'], 'L3_gnn_b1': _L3_gnn_in['b1'], 'L3_gnn_gn_w': _L3_gnn_in['gn_w'], 'L3_gnn_gn_b': _L3_gnn_in['gn_b'], 'L3_gnn_gn_ms': _L3_gnn_in['gn_ms'], 'L3_gnn_W2': _L3_gnn_in['W2'], 'L3_gnn_att_src2': _L3_gnn_in['att_src2'], 'L3_gnn_att_dst2': _L3_gnn_in['att_dst2'], 'L3_gnn_b2': _L3_gnn_in['b2']}

def reference(x, src, dst, edge_weight, L0_gnn_eps, L0_gnn_W1, L0_gnn_b1, L0_gnn_g1, L0_gnn_be1, L0_gnn_W2, L0_gnn_b2, L0_gnn_g2, L0_gnn_be2, L1_gnn_W1, L1_gnn_b1, L1_gnn_W2, L1_gnn_b2, L1_gnn_Wl, L1_gnn_bl, L1_gnn_root_idx, L2_gnn_W, L2_gnn_b, L3_gnn_W1, L3_gnn_att_src1, L3_gnn_att_dst1, L3_gnn_b1, L3_gnn_gn_w, L3_gnn_gn_b, L3_gnn_gn_ms, L3_gnn_W2, L3_gnn_att_src2, L3_gnn_att_dst2, L3_gnn_b2):
    import jax
    import jax.numpy as jnp

    def _L0_gnn_ref(x, edge_row, edge_col, edge_vals, eps, W1, b1, g1, be1, W2, b2, g2, be2):
        import jax, jax.numpy as jnp
        import numpy as np
        N = 3125
        E = 100000
        DI = 256
        DO = 256
        BN_EPS = 1e-05

        def _bn_relu(h, gamma, beta):
            mean = jnp.mean(h, axis=0)
            var = jnp.var(h, axis=0)
            hn = (h - mean) * jax.lax.rsqrt(var + BN_EPS)
            return jax.nn.relu(hn * gamma + beta)
        n = x.shape[0]
        msgs = edge_vals[:, None] * x[edge_col]
        agg = jax.ops.segment_sum(msgs, edge_row, num_segments=n)
        h = (1.0 + eps[0]) * x + agg
        h = _bn_relu(h @ W1 + b1, g1, be1)
        h = _bn_relu(h @ W2 + b2, g2, be2)
        return h

    def _L1_gnn_ref(features, values, W1, b1, W2, b2, Wl, bl, adjs, batch, root_idx):
        import jax, jax.numpy as jnp
        import numpy as np
        NEG_SLOPE = 0.01

        def _leaky(x):
            return jnp.where(x >= 0, x, NEG_SLOPE * x)

        def _gcn(x, W, b, src, dst, w, n):
            h = x @ W
            agg = jax.ops.segment_sum(w[:, None] * h[src], dst, num_segments=n)
            return agg + b
        N = features.shape[0]
        src, dst = (adjs[0], adjs[1])
        f1 = features
        h = _gcn(f1, W1, b1, src, dst, values, N)
        f2 = h
        root1 = f1[root_idx[batch]]
        x = _leaky(jnp.concatenate([h, root1], axis=1))
        x = _gcn(x, W2, b2, src, dst, values, N)
        x = _leaky(x)
        root2 = f2[root_idx[batch]]
        x = jnp.concatenate([x, root2], axis=1)
        return _leaky(x @ Wl + bl)

    def _L2_gnn_ref(h, norm, W, b, src, dst):
        import jax, jax.numpy as jnp
        import numpy as np
        N_NODES = 3125
        N_EDGES = 50000
        IN_FEATS = 256
        OUT_FEATS = 256
        x = h @ W.T + b
        x = norm * x
        msg = x[src]
        agg = jax.ops.segment_sum(msg, dst, num_segments=h.shape[0])
        return agg * norm

    def _L3_gnn_ref(x, edge_index, W1, att_src1, att_dst1, b1, gn_w, gn_b, gn_ms, W2, att_src2, att_dst2, b2):
        import jax, jax.numpy as jnp
        import numpy as np
        N_NODES = 10000
        N_EDGES = 5000
        F_IN = 256
        HEADS = 4
        F_OUT = 256
        NEG_SLOPE = 0.2
        EPS = 1e-05

        def gat_conv(x, src, dst, W, a_src, a_dst, bias, concat):
            N = x.shape[0]
            H, C = a_src.shape
            h = (x @ W).reshape(N, H, C)
            al_s = jnp.einsum('nhc,hc->nh', h, a_src)
            al_d = jnp.einsum('nhc,hc->nh', h, a_dst)
            e = jax.nn.leaky_relu(al_s[src] + al_d[dst], NEG_SLOPE)
            m = jax.ops.segment_max(e, dst, num_segments=N)
            ex = jnp.exp(e - m[dst])
            denom = jax.ops.segment_sum(ex, dst, num_segments=N)
            alpha = ex / denom[dst]
            out = jax.ops.segment_sum(h[src] * alpha[:, :, None], dst, num_segments=N)
            out = out.reshape(N, H * C) if concat else out.mean(axis=1)
            return out + bias

        def graph_norm(x, w, b, ms):
            mean = x.mean(axis=0, keepdims=True)
            sh = x - ms * mean
            var = (sh * sh).mean(axis=0, keepdims=True)
            return w * sh / jnp.sqrt(var + EPS) + b
        N = x.shape[0]
        loop = jnp.arange(N, dtype=edge_index.dtype)
        src = jnp.concatenate([edge_index[0], loop])
        dst = jnp.concatenate([edge_index[1], loop])
        h = gat_conv(x, src, dst, W1, att_src1, att_dst1, b1, concat=True)
        h = graph_norm(h, gn_w, gn_b, gn_ms)
        h = jax.nn.relu(h)
        out = gat_conv(h, src, dst, W2, att_src2, att_dst2, b2, concat=False)
        return out
    edge_index = jnp.stack([src, dst])
    deg = jnp.maximum(jax.ops.segment_sum(jnp.ones(dst.shape, jnp.float32), dst, num_segments=3125), 1.0)
    deg_isqrt = deg ** (-0.5)
    batch0 = jnp.zeros((3125,), jnp.int32)
    h = jnp.maximum(_layernorm(x, axis=-1), 0.0)
    x = x + _L0_gnn_ref(h, src, dst, edge_weight, L0_gnn_eps, L0_gnn_W1, L0_gnn_b1, L0_gnn_g1, L0_gnn_be1, L0_gnn_W2, L0_gnn_b2, L0_gnn_g2, L0_gnn_be2)
    h = jnp.maximum(_layernorm(x, axis=-1), 0.0)
    x = x + _L1_gnn_ref(h, edge_weight, L1_gnn_W1, L1_gnn_b1, L1_gnn_W2, L1_gnn_b2, L1_gnn_Wl, L1_gnn_bl, edge_index, batch0, L1_gnn_root_idx)
    h = jnp.maximum(_layernorm(x, axis=-1), 0.0)
    x = x + _L2_gnn_ref(h, deg_isqrt[:, None], L2_gnn_W, L2_gnn_b, src, dst)
    h = jnp.maximum(_layernorm(x, axis=-1), 0.0)
    x = x + _L3_gnn_ref(h, edge_index, L3_gnn_W1, L3_gnn_att_src1, L3_gnn_att_dst1, L3_gnn_b1, L3_gnn_gn_w, L3_gnn_gn_b, L3_gnn_gn_ms, L3_gnn_W2, L3_gnn_att_src2, L3_gnn_att_dst2, L3_gnn_b2)
    return x

_drawn_inputs = setup_inputs


def setup_inputs(seed=0):
    import zlib

    import numpy as np

    out = dict(_drawn_inputs(seed))
    spreads = {'L0_gnn_b1': (0.0, 2.0),
     'L0_gnn_g1': (1.0, 0.2),
     'L0_gnn_be1': (0.0, 0.376),
     'L0_gnn_b2': (0.0, 2.0),
     'L0_gnn_g2': (1.0, 0.2),
     'L0_gnn_be2': (0.0, 0.1),
     'L1_gnn_b1': (0.0, 0.306),
     'L1_gnn_b2': (0.0, 0.8),
     'L1_gnn_bl': (0.0, 0.562),
     'L3_gnn_b1': (0.0, 0.342),
     'L3_gnn_gn_w': (1.0, 0.2),
     'L3_gnn_gn_b': (0.0, 0.428),
     'L3_gnn_gn_ms': (1.0, 0.2),
     'L3_gnn_b2': (0.0, 0.43)}
    factors = {'L2_gnn_b': 29.615,
     'L3_gnn_att_src1': 8.0,
     'L3_gnn_att_dst1': 8.0,
     'L3_gnn_att_src2': 3.937,
     'L3_gnn_att_dst2': 6.054}
    for name, (base, spread) in spreads.items():
        noise = np.random.default_rng([zlib.crc32(name.encode()), seed]).standard_normal(out[name].shape)
        drawn = base * np.exp(spread * noise) if base else spread * noise
        out[name] = jnp.asarray(drawn.astype(out[name].dtype))
    for name, factor in factors.items():
        out[name] = (out[name] * factor).astype(out[name].dtype)
    return out
```

```python
from contextlib import ExitStack

import concourse.bass as bass
from concourse import mybir

ALU = mybir.AluOpType
ACT = mybir.ActivationFunctionType
F32 = mybir.dt.float32
I32 = mybir.dt.int32
U32 = mybir.dt.uint32
AX_X = mybir.AxisListType.X

N = 3125
Q = 125
NB = N // Q
D = 256
KT = D // 128
E = 50000
EC = E // Q
HEADS = 4
WIDE = HEADS * D
CT = WIDE // 128
ROWS = NB * 128
SC = 4
NSC = EC // SC
TRASH = ROWS * N
GB = 5
NG = NB // GB
HALF = [(0, 13), (13, 12)]
LN_EPS = 1e-5
BN_EPS = 1e-5
NEG = -1.0e30
TINY = 1.0e-18
MARK = 1024.0
ROUND = 12582912.0
CREDIT_TR = 2 * NG
CREDIT = 2


class Chain:

    def __init__(self, eng, sem):
        self.eng, self.sem, self.n, self.iv, self.per = eng, sem, 0, None, 0

    def value(self):
        return self.n if self.iv is None else self.iv * self.per + self.n

    def mark(self, ins):
        self.n += 1
        ins.then_inc(self.sem, 1)

    def join(self, but=0):
        self.eng.wait_ge(self.sem, self.value() - but)

    def __call__(self, ins):
        self.mark(ins)
        self.join()

    def loop(self, trips, per):
        with self.eng.Fori(0, trips) as iv:
            n0 = self.n
            self.iv, self.per = iv, per
            yield iv
            assert self.n - n0 == per, (self.n - n0, per)
        self.iv = None
        self.n = n0 + per * trips


def gnn_stack(nc, x, src, dst, edge_weight, eps0, W01, b01, g01, be01, W02, b02, g02, be02,
              W11, b11, W12, b12, Wl1, bl1, root_idx, W2, b2, W31, as31, ad31, b31, gnw, gnb, gnms,
              W32, as32, ad32, b32, out):
    with ExitStack() as ctx:
        sems = {}

        def S(name):
            if name not in sems:
                sems[name] = ctx.enter_context(nc.semaphore(name))
            return sems[name]

        def sb(name, shape, dt=F32):
            return ctx.enter_context(nc.sbuf_tensor(name, shape, dt))

        pairs = nc.dram_tensor("pairs", (TRASH + SC * 128, 2), F32, kind="Internal").ap()
        lnc_d = nc.dram_tensor("lnc_d", (NB, 128, N), F32, kind="Internal").ap()
        rows_d = nc.dram_tensor("rows_d", (2 * HEADS, N), F32, kind="Internal").ap()
        wide_d = nc.dram_tensor("wide_d", (128, CT, N), F32, kind="Internal").ap()
        row2_d = nc.dram_tensor("row2_d", (2, N), F32, kind="Internal").ap()
        pair_rows = pairs[0:TRASH, :].rearrange("(i p c) t -> i p c t", p=128, c=N)

        X = sb("X", [128, NB, D])
        H = sb("H", [128, NB, D])
        B = sb("B", [128, NB * D])
        Fb = sb("Fb", [128, KT * N])
        R = sb("R", [128, 4 * N])
        PT = sb("PT", [128, 2, GB * Q])
        Bn = B[:, :].rearrange("p (j f) -> p j f", f=D)
        F = Fb[:, :].rearrange("p (k n) -> p k n", k=KT)
        G = R[:, 0:2 * N].rearrange("p (k n) -> p k n", k=KT)
        Rp = [R[:, s * 2 * N:(s + 1) * 2 * N].rearrange("p (n t) -> p n t", t=2) for s in range(2)]
        lncR = [R[:, s * N:(s + 1) * N] for s in range(2)]
        scr = [R[:, (2 + s) * N:(3 + s) * N] for s in range(2)]
        lncW = [Fb[:, s * N:(s + 1) * N] for s in range(2)]
        als = [B[:, 0:N], B[:, N:2 * N], Fb[:, 0:N], Fb[:, N:2 * N]]

        wA = sb("wA", [128, 5 * KT * D])
        w01, w02, w11 = [wA[:, k * KT * D:(k + 1) * KT * D].rearrange("p (k n) -> p k n", k=KT) for k in range(3)]
        w12 = wA[:, 3 * KT * D:5 * KT * D].rearrange("p (k n) -> p k n", k=2 * KT)
        wl1 = sb("wl1", [128, 2 * KT, D])
        w2 = sb("w2", [128, KT, D])
        w2T = sb("w2T", [128, KT, D])
        w31 = sb("w31", [128, KT, WIDE])
        w32 = sb("w32", [128, CT, D + 2])
        va = sb("va", [128, KT, 2 * HEADS])
        cols = sb("cols", [128, 6, KT])
        colw = sb("colw", [128, 4, CT])
        bcs = sb("bcs", [128, 5, D])
        ident = sb("ident", [128, 128])
        ones = sb("ones", [128, 128])
        small = sb("small", [128, 40])
        st = sb("st", [128, NB, 6])
        lns = sb("lns", [128, 6, NB])
        node = sb("node", [128, NB])
        pick = sb("pick", [128, NB])
        norm = sb("norm", [128, NB])
        rootc = sb("rootc", [128, KT])
        rootb = sb("rootb", [128, KT, Q])
        rootr = sb("rootr", [128, D])
        ald = sb("ald", [128, NB, HEADS])
        bst = sb("bst", [128, KT, 7, 6])
        gst = sb("gst", [128, CT, NB * 6])
        mv = sb("mv", [128, CT, 2])
        aff = sb("aff", [128, 6, CT])
        mx = sb("mx", [128, 8])
        ag = sb("ag", [128, 2, D])
        agT = sb("agT", [128, KT, Q])
        yT = wA[:, 0:2 * CT * Q].rearrange("p (s t q) -> p s t q", s=2, t=CT)
        idx_i = sb("idx_i", [128, 4], I32)
        stage_k = sb("stage_k", [128, 2, SC], U32)
        stage_v = sb("stage_v", [128, 2, SC, 2])
        trash = sb("trash", [128, SC])
        trash_i = sb("trash_i", [128, SC], I32)

        src_i = Fb[0:Q, 0:EC].bitcast(I32)
        dst_i = Fb[0:Q, EC:2 * EC].bitcast(I32)
        wgt = Fb[0:Q, 2 * EC:3 * EC]
        key = Fb[0:Q, 3 * EC:4 * EC]
        e1 = Fb[0:Q, 4 * EC:5 * EC]
        e2 = Fb[0:Q, 5 * EC:6 * EC]
        key_u = Fb[:, 6 * EC:7 * EC].bitcast(U32)
        val = Fb[:, 7 * EC:9 * EC].rearrange("p (c t) -> p c t", t=2)
        M0 = 2 * N
        W = SC * Q
        tri = R[0:Q, M0:M0 + SC * W].rearrange("p (i w) -> p i w", i=SC)
        dgk = [R[0:Q, M0 + (4 + s) * W:M0 + (5 + s) * W].rearrange("p (i q) -> p i q", q=Q) for s in range(2)]
        dgw = [R[0:Q, M0 + (6 + s) * W:M0 + (7 + s) * W].rearrange("p (i q) -> p i q", q=Q) for s in range(2)]
        wrow = [R[0:Q, M0 + (8 + s) * W:M0 + (9 + s) * W] for s in range(2)]
        junk = [R[0:Q, M0 + (10 + s) * W:M0 + (11 + s) * W] for s in range(2)]
        att1 = [B[:, 0:WIDE], B[:, WIDE:2 * WIDE]]
        att2 = [B[:, 2 * WIDE:2 * WIDE + D], B[:, 2 * WIDE + D:2 * WIDE + 2 * D]]
        att_junk = B[:, 2 * WIDE + 2 * D:2 * WIDE + 3 * D]

        ps = ctx.enter_context(nc.psum_tensor("ps", [128, 8, 512], F32))
        psflat = ps[:, :, :].rearrange("p b c -> p (b c)")
        acc = [ps[0:Q, 4 + s, 0:D] for s in range(2)]
        tps = [psflat[:, 1024 * s:1024 * s + 128 * GB].rearrange("p (b q) -> p b q", q=128) for s in range(2)]

        block = ctx.enter_context(nc.Block())

        NCH = [(n0, min(4 * Q, N - n0)) for n0 in range(0, N, 4 * Q)]
        JP = [(j, min(2, NB - j)) for j in range(0, NB, 2)]
        QG = [(k, j, min(4, NB - j)) for k in range(KT) for j in range(0, NB, 4)]
        PAIRS = (NB - 1) // 2

        base, total = {}, 0
        for stage_name, groups in (("z", len(QG)), ("y1", KT * len(NCH)), ("y2", KT * len(NCH)), ("l0", len(JP)),
                                   ("h1", len(QG)), ("t1", len(JP)), ("h2", len(QG)), ("t2", len(JP)),
                                   ("h3", len(QG)), ("t3", len(JP)), ("h4", len(QG)), ("t4", len(JP)),
                                   ("h5", len(QG)), ("alsrow", len(NCH)), ("z3", NB)):
            base[stage_name] = total
            total += groups

        def ring_wait(eng, name, n):
            if n >= 4 or (n == 0 and base[name]):
                eng.wait_ge(S("ring_ev"), base[name] + max(n - 3, 0))

        @block.sync
        def _(sp):
            sp.dma_start(src_i, src.rearrange("(p c) -> p c", c=EC)).then_inc(S("edges_in"), 16)
            sp.dma_start(dst_i, dst.rearrange("(p c) -> p c", c=EC)).then_inc(S("edges_in"), 16)
            sp.dma_start(wgt, edge_weight.rearrange("(p c) -> p c", c=EC)).then_inc(S("edges_in"), 16)
            sp.wait_ge(S("zero_made"), 1)
            flat = pairs[0:TRASH, :].rearrange("(i p c) t -> i p (c t)", p=128, c=N)
            with sp.Fori(0, NB) as i:
                sp.dma_start(flat[bass.ds(i, 1)].rearrange("o p c -> (o p) c"), R[:, 0:2 * N]).then_inc(S("zeroed"), 16)
            sp.dma_start(pairs[TRASH:TRASH + SC * 128, :].rearrange("(p c) t -> p (c t)", p=128),
                         R[:, 0:2 * SC]).then_inc(S("zeroed"), 16)
            sp.dma_start(X[0:Q, :, :], x.rearrange("(p j) f -> p j f", j=NB)).then_inc(S("x_in"), 16)
            w_in = S("w_in")
            nw = 0
            for t, w in ((w01, W01), (w02, W02), (w11, W11), (w12, W12), (wl1, Wl1), (w2, W2), (w31, W31)):
                sp.dma_start(t[:, :, :], w.rearrange("(k p) n -> p k n", p=128)).then_inc(w_in, 16)
                nw += 1
            sp.dma_start(w32[:, :, 0:D], W32.rearrange("(k p) n -> p k n", p=128)).then_inc(w_in, 16)
            for k, a in enumerate((as31, ad31)):
                sp.dma_start(att1[k], a.rearrange("h c -> (h c)").partition_broadcast(128)).then_inc(w_in, 16)
            for k, a in enumerate((as32, ad32)):
                sp.dma_start(att2[k], a.rearrange("h c -> (h c)").partition_broadcast(128)).then_inc(w_in, 16)
            for k, v in enumerate((b11, b12, bl1, b2, b32)):
                sp.dma_start(bcs[:, k, :], v.partition_broadcast(128)).then_inc(w_in, 16)
            sp.dma_start(idx_i[:, 0:1], root_idx[0:1].partition_broadcast(128)).then_inc(w_in, 16)
            sp.dma_start(small[:, 0:1], eps0.partition_broadcast(128)).then_inc(w_in, 16)
            with nc.allow_non_contiguous_dma(reason="a few hundred per-feature values"):
                for k, v in enumerate((b01, g01, be01, b02, g02, be02)):
                    sp.dma_start(cols[:, k, :], v.rearrange("(k p) -> p k", p=128)).then_inc(w_in, 16)
                for k, v in enumerate((b31, gnw, gnb, gnms)):
                    sp.dma_start(colw[:, k, :], v.rearrange("(k p) -> p k", p=128)).then_inc(w_in, 16)

            sp.wait_ge(S("scattered"), 16 * EC)
            for h, (j0, nj) in enumerate(HALF):
                def half_rows(i, s, k):
                    sp.wait_ge(S(f"L0used{h}"), k)
                    r = pair_rows[bass.ds(i, 1)].rearrange("o p c t -> (o p) c t")[:, j0 * Q:(j0 + nj) * Q, :]
                    sp.dma_start(Rp[s][:, 0:nj * Q, :], r).then_inc(S(f"L0rows{h}_{s}"), 16)
                if h:
                    sp.wait_ge(S("L0used0"), NB + CREDIT)
                with sp.Fori(0, PAIRS) as v:
                    half_rows(v * 2, 0, v * 2 + 1)
                    half_rows(v * 2 + 1, 1, v * 2 + 2)
                half_rows(NB - 1, 0, NB)

            def pair_pass(name, extra=None):
                def load(i, s, k):
                    sp.wait_ge(S(name + "tr"), k * NG)
                    if extra:
                        sp.wait_ge(S(extra), k)
                    sp.dma_start(Rp[s], pair_rows[bass.ds(i, 1)].rearrange("o p c t -> (o p) c t"))\
                        .then_inc(S(f"{name}rows{s}"), 16)

                def store(i, s, k):
                    sp.wait_ge(S("lnc_read"), k + CREDIT)
                    sp.dma_start(lnc_d[bass.ds(i, 1)].rearrange("o p c -> (o p) c"), lncW[s])\
                        .then_inc(S(f"lnc_out{s}"), 16)

                if not extra:
                    with sp.Fori(0, PAIRS) as v:
                        load(v * 2, 0, v * 2 + 1)
                        load(v * 2 + 1, 1, v * 2 + 2)
                    load(NB - 1, 0, NB)
                    return
                load(0, 0, 1)
                load(1, 1, 2)
                with sp.Fori(0, PAIRS - 1) as v:
                    store(v * 2, 0, v * 2 + 1)
                    load(v * 2 + 2, 0, v * 2 + 3)
                    store(v * 2 + 1, 1, v * 2 + 2)
                    load(v * 2 + 3, 1, v * 2 + 4)
                store(NB - 3, 0, NB - 2)
                load(NB - 1, 0, NB)
                store(NB - 2, 1, NB - 1)
                store(NB - 1, 0, NB)

            sp.wait_ge(S("r_free_L1a"), 1)
            pair_pass("L1a", "lnc_read")
            sp.wait_ge(S("L1a_done"), 1)
            pair_pass("L1b")
            sp.wait_ge(S("L1b_done"), 1)
            pair_pass("L2")

            sp.wait_ge(S("alsrow_made"), 1)
            sp.dma_start(rows_d[:, :], R[0:2 * HEADS, 0:N]).then_inc(S("alsrow_out"), 16)
            sp.wait_ge(S("alsrow_out"), 16)
            sp.wait_ge(S("ald_mm"), 1)
            for h in range(HEADS):
                sp.dma_start(als[h], rows_d[h, :].partition_broadcast(128)).then_inc(S("als_in"), 16)

            def lnc_load(name, i, s, k):
                sp.wait_ge(S(name + "lnc_used"), k)
                sp.dma_start(lncR[s], lnc_d[bass.ds(i, 1)].rearrange("o p c -> (o p) c"))\
                    .then_inc(S(f"{name}lnc{s}"), 16)

            def wide_store(i, s, k, ks):
                sp.wait_ge(S("y_made"), k)
                with nc.allow_non_contiguous_dma(reason="rows of a block"):
                    sp.dma_start(wide_d[:, :, bass.ds(i * Q, Q)], yT[:, s, :, :]).then_inc(S(f"y_out{s}"), 16)
                sp.wait_ge(S(f"y_out{s}"), ks)
                sp.sem_inc(S("y_free"), 1)

            sp.sem_inc(S("y_free"), CREDIT)
            lnc_load("L3a", 0, 0, 1)
            lnc_load("L3a", 1, 1, 2)
            with sp.Fori(0, PAIRS - 1) as v:
                lnc_load("L3a", v * 2 + 2, 0, v * 2 + 3)
                wide_store(v * 2, 0, v * 2 + 1, (v + 1) * 16)
                lnc_load("L3a", v * 2 + 3, 1, v * 2 + 4)
                wide_store(v * 2 + 1, 1, v * 2 + 2, (v + 1) * 16)
            lnc_load("L3a", NB - 1, 0, NB)
            wide_store(NB - 3, 0, NB - 2, PAIRS * 16)
            wide_store(NB - 2, 1, NB - 1, PAIRS * 16)
            wide_store(NB - 1, 0, NB, (PAIRS + 1) * 16)
            for c, (n0, nn) in enumerate(NCH):
                if c >= 2:
                    sp.wait_ge(S("wide_used"), c - 1)
                slot = R[:, (c % 2) * 4096:(c % 2) * 4096 + CT * nn].rearrange("p (t n) -> p t n", t=CT)
                sp.dma_start(slot, wide_d[:, :, n0:n0 + nn]).then_inc(S(f"wide_in{c % 2}"), 16)
            sp.wait_ge(S("row2_made"), 1)
            sp.dma_start(row2_d[:, :], R[0:2, 8192:8192 + N]).then_inc(S("row2_out"), 16)
            sp.wait_ge(S("row2_out"), 16)
            sp.dma_start(als[2], row2_d[0, :].partition_broadcast(128)).then_inc(S("als2_in"), 16)
            sp.wait_ge(S("als2_in"), 16)
            with sp.Fori(0, PAIRS) as v:
                lnc_load("L3b", v * 2, 0, v * 2 + 1)
                lnc_load("L3b", v * 2 + 1, 1, v * 2 + 2)
            lnc_load("L3b", NB - 1, 0, NB)
            sp.wait_ge(S("L3bout"), NB + CREDIT)
            sp.dma_start(out.rearrange("(p j) f -> p j f", j=NB), X[0:Q, :, :]).then_inc(S("stored"), 16)
            sp.wait_ge(S("stored"), 16)
            sp.wait_ge(S("lnc_out0"), 16 * (PAIRS + 1))
            sp.wait_ge(S("lnc_out1"), 16 * PAIRS)

        @block.gpsimd
        def _(pool):
            g = nc.gpsimd
            link = Chain(pool, S("pool_chain"))
            link(g.memset(ident[:, :], 0.0))
            g.affine_select(out=ident[:, :], in_=ident[:, :], compare_op=ALU.not_equal, fill=1.0, base=0,
                            pattern=[[-1, 128]], channel_multiplier=1).then_inc(S("pool_consts"), 1)
            link(g.memset(tri, 1.0))
            for i in range(SC):
                g.affine_select(out=tri[:, i, :], in_=tri[:, i, :], compare_op=ALU.is_ge, fill=1.0 + MARK,
                                base=-i * Q, pattern=[[1, W]], channel_multiplier=-1).then_inc(S("pool_consts"), 1)
            g.iota(trash_i[:, :], pattern=[[128, SC]], base=TRASH, channel_multiplier=1).then_inc(S("pool_consts"), 1)
            g.iota(node[:, :], pattern=[[1, NB]], base=0, channel_multiplier=NB,
                   allow_small_or_imprecise_dtypes=True).then_inc(S("pool_consts"), 1)

            def stage(t, s, k):
                pool.wait_ge(S("merged"), k)
                link.mark(g.tensor_copy(stage_k[:, s, :], key_u[:, bass.ds(t * SC, SC)]))
                link(g.tensor_copy(stage_v[:, s, :, :], val[:, bass.ds(t * SC, SC), :]))

            def scatter(s):
                pool.sem_inc(S("rounds_begun"), 1)
                for i in range(SC):
                    pool.indirect_dma_start(pairs, bass.IndirectOffsetOnAxis(ap=stage_k[:, s, i:i + 1], axis=0),
                                            stage_v[:, s, i, :], None, compute_op=ALU.add).then_inc(S("scattered"), 16)

            stage(0, 0, 1)
            pool.wait_ge(S("zeroed"), 16 * (NB + 1))
            for v in link.loop(NSC // 2 - 1, 4):
                scatter(0)
                stage(v * 2 + 1, 1, v + 1)
                pool.wait_ge(S("scattered"), (v * 2 + 1) * (16 * SC))
                scatter(1)
                stage(v * 2 + 2, 0, v + 2)
                pool.wait_ge(S("scattered"), (v * 2 + 2) * (16 * SC))
            scatter(0)
            stage(NSC - 1, 1, NSC // 2)
            pool.wait_ge(S("scattered"), (NSC - 1) * (16 * SC))
            scatter(1)

        @block.tensor
        def _(pe):
            mm = nc.tensor.matmul

            def to_features(name, node_major, gate=None):
                for n, (k, j, nj) in enumerate(QG):
                    if gate is not None:
                        pe.wait_ge(S("ln_done"), gate * NB + min(NB, j + nj))
                    ring_wait(pe, name, n)
                    for m in range(nj):
                        last = nc.tensor.transpose(ps[:, n % 4, m * Q:(m + 1) * Q],
                                                   node_major[0:Q, j + m, k * 128:(k + 1) * 128], ident[0:Q, 0:Q])
                    last.then_inc(S("ring_pe"), 1)

            def feature_product(name, w, inp):
                n = 0
                for c in range(KT):
                    for n0, nn in NCH:
                        ring_wait(pe, name, n)
                        for k in range(KT):
                            last = mm(ps[:, n % 4, 0:nn], w[:, k, c * 128:(c + 1) * 128], inp[:, k, n0:n0 + nn],
                                      start=k == 0, stop=k == KT - 1)
                        last.then_inc(S("ring_pe"), 1)
                        n += 1

            def node_product(name, w, inp):
                for n, (j, nj) in enumerate(JP):
                    ring_wait(pe, name, n)
                    for m in range(nj):
                        for k in range(KT):
                            last = mm(ps[0:Q, n % 4, m * D:(m + 1) * D], inp[:, k, (j + m) * Q:(j + m + 1) * Q],
                                      w[:, k, :], start=k == 0, stop=k == KT - 1)
                    last.then_inc(S("ring_pe"), 1)

            def to_nodes(name, feat):
                for n, (j, nj) in enumerate(JP):
                    ring_wait(pe, name, n)
                    for m in range(nj):
                        for k in range(KT):
                            last = nc.tensor.transpose(ps[0:Q, n % 4, m * D + k * 128:m * D + (k + 1) * 128],
                                                       feat[:, k, (j + m) * Q:(j + m + 1) * Q], ident[:, :])
                    last.then_inc(S("ring_pe"), 1)

            def row_slot(s, plane):
                return (lambda j: scr[s][0:Q, j * Q:(j + 1) * Q]) if plane is None else \
                       (lambda j: Rp[s][0:Q, j * Q:(j + 1) * Q, plane])

            pe.wait_ge(S("ones_made"), 1)

            def broadcast(s, k):
                pe.wait_ge(S("diag_made"), k)
                pe.wait_ge(S("keyrow_free"), k)
                pe.wait_ge(S("wrow_out"), k)
                mm(ps[0:Q, s, 0:W], ones[0:Q, 0:Q], dgk[s].rearrange("p i q -> p (i q)"), start=True, stop=True)
                mm(ps[0:Q, 2 + s, 0:W], ones[0:Q, 0:Q], dgw[s].rearrange("p i q -> p (i q)"), start=True, stop=True)\
                    .then_inc(S("rows_made"), 1)

            with pe.Fori(0, NSC // 2) as v:
                broadcast(0, v * 2 + 1)
                broadcast(1, v * 2 + 2)

            pe.wait_ge(S("keyrow_free"), NSC + CREDIT)
            pe.wait_ge(S("wrow_out"), NSC + CREDIT)
            pe.wait_ge(S("ln_done"), 1 * NB)
            for h, (j0, nj) in enumerate(HALF):
                if h:
                    pe.wait_ge(S("L0sum"), 1)
                pe.sem_inc(S(f"L0used{h}"), CREDIT)

                def half(i, s, k, first, last_):
                    pe.wait_ge(S(f"L0rows{h}_{s}"), k)
                    for j in range(nj):
                        ins = mm(ps[0:Q, j // 2, (j % 2) * D:(j % 2 + 1) * D], Rp[s][0:Q, j * Q:(j + 1) * Q, 0],
                                 H[0:Q, bass.ds(i, 1), :].rearrange("p o f -> p (o f)"),
                                 start=first and j % 2 == 0, stop=last_, skip_group_check=True)
                    ins.then_inc(S(f"L0used{h}"), 1)

                half(0, 0, 16, True, False)
                with pe.Fori(0, PAIRS - 1) as v:
                    half(v * 2 + 1, 1, (v + 1) * 16, False, False)
                    half(v * 2 + 2, 0, (v + 2) * 16, False, False)
                half(NB - 2, 1, PAIRS * 16, False, False)
                half(NB - 1, 0, (PAIRS + 1) * 16, False, True)

            pe.wait_ge(S("L0sum"), 2)
            to_features("z", Bn)
            pe.wait_ge(S("ring_ev"), base["z"] + len(QG))
            feature_product("y1", w01, F)
            pe.wait_ge(S("bn1_done"), 2)
            feature_product("y2", w02, G)
            pe.wait_ge(S("bn2_done"), 2)
            to_nodes("l0", F)

            def agg(name, plane, rhs, ready):
                pe.sem_inc(S(name + "tr"), CREDIT_TR)
                pe.sem_inc(S(name + "mm"), CREDIT)

                def T(unit_s, grp, k, kg):
                    if grp == 0:
                        pe.wait_ge(S(ready(unit_s)), k)
                    s = kg[1]
                    pe.wait_ge(S(name + "ev"), kg[0])
                    for b in range(GB):
                        last = nc.tensor.transpose(tps[s][0:Q, b, 0:Q], row_slot(unit_s, plane)(grp * GB + b),
                                                   ident[0:Q, 0:Q])
                    last.then_inc(S(name + "tr"), 1)

                def M(unit_s, grp, ku, kg, s):
                    if grp == 0:
                        pe.wait_ge(S(name + "out"), ku)
                    pe.wait_ge(S(name + "ev"), kg)
                    for b in range(GB):
                        j = grp * GB + b
                        last = mm(acc[unit_s], PT[0:Q, s, b * Q:(b + 1) * Q], rhs[0:Q, j, :],
                                  start=j == 0, stop=j == NB - 1)
                    last.then_inc(S(name + "mm"), 1)
                return T, M

            def whole(name, plane, rhs):
                T, M = agg(name, plane, rhs, lambda s: f"{name}rows{s}")
                T(0, 0, 16, (1, 0))
                with pe.Fori(0, PAIRS) as v:
                    for g in range(2 * NG):
                        u, n = (g + 1) // NG, g + 1
                        T(u % 2, n % NG, (v + 1 + (u == 2)) * 16, (v * (2 * NG) + n + 1, n % 2))
                        M(g // NG, g % NG, v * 2 + g // NG + 1, v * (2 * NG) + g + 3, g % 2)
                b0 = 2 * NG * PAIRS
                for g in range(NG):
                    if g + 1 < NG:
                        T(0, g + 1, 0, (b0 + g + 2, (g + 1) % 2))
                    M(0, g, NB, b0 + g + 3, g % 2)

            to_features("h1", H, 1)
            pe.wait_ge(S("pick_made"), 1)

            def root(name, t):
                for k in range(KT):
                    for j in range(NB):
                        last = mm(ps[:, 6, k:k + 1], t[0:Q, j, k * 128:(k + 1) * 128], pick[0:Q, j:j + 1],
                                  start=j == 0, stop=j == NB - 1)
                last.then_inc(S(name), 1)

            root("root1", H)
            pe.wait_ge(S("ring_ev"), base["h1"] + len(QG))
            node_product("t1", w11, F)
            pe.wait_ge(S("ring_ev"), base["t1"] + len(JP))
            whole("L1a", 0, Bn)
            pe.wait_ge(S("rootb1"), 1)
            for k in range(KT):
                last = mm(ps[0:Q, 7, 0:D], rootb[:, k, :], w12[:, KT + k, :], start=k == 0, stop=k == KT - 1)
            last.then_inc(S("rootr1"), 1)
            pe.wait_ge(S("L1aout"), NB + CREDIT)
            root("root2", H)
            pe.wait_ge(S("f2_leaky"), 1)
            to_features("h2", H)
            pe.wait_ge(S("ring_ev"), base["h2"] + len(QG))
            node_product("t2", w12, F)
            pe.wait_ge(S("ring_ev"), base["t2"] + len(JP))
            whole("L1b", 0, Bn)
            pe.wait_ge(S("rootb2"), 1)
            for k in range(KT):
                last = mm(ps[0:Q, 7, 0:D], rootb[:, k, :], wl1[:, KT + k, :], start=k == 0, stop=k == KT - 1)
            last.then_inc(S("rootr2"), 1)
            pe.wait_ge(S("f3_leaky"), 1)
            to_features("h3", H)
            pe.wait_ge(S("ring_ev"), base["h3"] + len(QG))
            node_product("t3", wl1, F)
            pe.wait_ge(S("rootr_used"), 2)
            for ko in range(KT):
                for ki in range(KT):
                    last = nc.tensor.transpose(ps[:, 7, ki * D + ko * 128:ki * D + (ko + 1) * 128],
                                               w2[:, ko, ki * 128:(ki + 1) * 128], ident[:, :])
            last.then_inc(S("w2T_pe"), 1)

            pe.wait_ge(S("ring_ev"), base["t3"] + len(JP))
            to_features("h4", H, 2)
            pe.wait_ge(S("ring_ev"), base["h4"] + len(QG))
            pe.wait_ge(S("w2T_made"), 1)
            node_product("t4", w2T, F)
            pe.wait_ge(S("ring_ev"), base["t4"] + len(JP))
            whole("L2", 1, Bn)

            pe.wait_ge(S("L2out"), NB + CREDIT)
            to_features("h5", H, 3)
            pe.wait_ge(S("ring_ev"), base["h5"] + len(QG))
            pe.wait_ge(S("va_made"), 1)
            for n, (n0, nn) in enumerate(NCH):
                ring_wait(pe, "alsrow", n)
                for k in range(KT):
                    last = mm(ps[0:2 * HEADS, n % 4, 0:nn], va[:, k, :], F[:, k, n0:n0 + nn],
                              start=k == 0, stop=k == KT - 1)
                last.then_inc(S("ring_pe"), 1)
            for j in range(NB):
                for k in range(KT):
                    last = mm(ps[0:Q, 6, j * HEADS:(j + 1) * HEADS], F[:, k, j * Q:(j + 1) * Q],
                              va[:, k, HEADS:2 * HEADS], start=k == 0, stop=k == KT - 1)
            last.then_inc(S("ald_mm"), 1)
            pe.wait_ge(S("ring_ev"), base["alsrow"] + len(NCH))
            pe.wait_ge(S("ald_made"), 1)

            T, M = agg("L3a", None, H, lambda s: "L3aprob")

            def wide_T(s, k):
                pe.wait_ge(S("L3aout"), k)
                for t in range(KT):
                    last = nc.tensor.transpose(ps[:, 6, t * Q:(t + 1) * Q], ag[0:Q, s, t * 128:(t + 1) * 128],
                                               ident[0:Q, 0:Q])
                last.then_inc(S("agT_pe"), 1)

            def wide_M(hd, k):
                pe.wait_ge(S("agT_made"), k)
                for c in range(KT):
                    for t in range(KT):
                        last = mm(ps[:, 7, c * Q:(c + 1) * Q], w31[:, t, hd * D + c * 128:hd * D + (c + 1) * 128],
                                  agT[:, t, :], start=t == 0, stop=t == KT - 1)
                last.then_inc(S("y_pe"), 1)

            def run(units, v, last_run=False):
                for u in units:
                    for g in range(NG):
                        n = g + 1
                        u2 = u + n // NG
                        if not (last_run and u == units[-1] and n == NG):
                            T(u2 % 2, n % NG, v * 4 + u2 + 1, ((v * 4 + u) * NG + n + 1, ((u * NG) + n) % 2))
                        M(u % 2, g, v * 4 + u + 1, (v * 4 + u) * NG + g + 3, (u * NG + g) % 2)
                        if u > 0 and g == 0:
                            wide_T((u - 1) % 2, v * 4 + u + CREDIT)
                        if u > 0 and g == 2:
                            wide_M((u - 1) % 4, v * 4 + u)

            T(0, 0, 1, (1, 0))
            run([0], 0)
            with pe.Fori(0, NB - 1) as v:
                run([1, 2, 3, 4], v)
            run([1, 2, 3], NB - 1, True)
            wide_T(1, 4 * NB + CREDIT)
            wide_M(3, 4 * NB)

            pe.wait_ge(S("y_made"), NB)
            pe.wait_ge(S("L3aout"), 4 * NB + CREDIT)
            pe.wait_ge(S("v2_made"), 1)
            n = 0
            for c, (n0, nn) in enumerate(NCH):
                pe.wait_ge(S("wide_norm"), CT * (c + 1))
                slot = R[:, (c % 2) * 4096:(c % 2) * 4096 + CT * nn].rearrange("p (t n) -> p t n", t=CT)
                for b in range(nn // Q):
                    ring_wait(pe, "z3", n)
                    for t in range(CT):
                        last = mm(ps[0:Q, n % 4, 0:D + 2], slot[:, t, b * Q:(b + 1) * Q], w32[:, t, :],
                                  start=t == 0, stop=t == CT - 1)
                    last.then_inc(S("ring_pe"), 1)
                    n += 1
                if c >= 2:
                    pe.wait_ge(S("row2_ev"), c - 1)
                for t in range(CT):
                    last = mm(ps[0:2, 4 + c % 2, 0:nn], w32[:, t, D:D + 2], slot[:, t, :],
                              start=t == 0, stop=t == CT - 1)
                last.then_inc(S("wide_used"), 1)
            pe.wait_ge(S("ring_ev"), base["z3"] + NB)
            pe.wait_ge(S("row2_ev"), len(NCH))
            T, M = agg("L3b", None, Bn, lambda s: "L3bprob")
            T(0, 0, 1, (1, 0))
            with pe.Fori(0, PAIRS) as v:
                for g in range(2 * NG):
                    u, n = (g + 1) // NG, g + 1
                    T(u % 2, n % NG, v * 2 + u + 1, (v * (2 * NG) + n + 1, n % 2))
                    M(g // NG, g % NG, v * 2 + g // NG + 1, v * (2 * NG) + g + 3, g % 2)
            b0 = 2 * NG * PAIRS
            for g in range(NG):
                if g + 1 < NG:
                    T(0, g + 1, 0, (b0 + g + 2, (g + 1) % 2))
                M(0, g, NB, b0 + g + 3, g % 2)

        @block.scalar
        def _(act):
            a = nc.scalar.activation
            link = Chain(act, S("act_chain"))

            act.wait_ge(S("pool_consts"), 1)
            act.wait_ge(S("key_made"), 1)
            act.sem_inc(S("wrow_out"), CREDIT)

            def diag(t, s, k):
                act.wait_ge(S("rows_made"), k)
                for i in range(SC):
                    a(dgk[s][:, i, :], ident[0:Q, 0:Q], ACT.Copy, scale=key[:, bass.ds(t * SC + i, 1)])
                    last = a(dgw[s][:, i, :], ident[0:Q, 0:Q], ACT.Copy, scale=wgt[:, bass.ds(t * SC + i, 1)])
                last.then_inc(S("diag_made"), 1)

            def wrow_out(s, k):
                act.wait_ge(S("rows_made"), k + 2)
                act.wait_ge(S("keyrow_free"), k)
                a(wrow[s], ps[0:Q, 2 + s, 0:W], ACT.Copy).then_inc(S("wrow_out"), 1)

            act.sem_inc(S("rows_made"), 2)
            diag(0, 0, 1)
            with act.Fori(0, NSC // 2 - 1) as v:
                diag(v * 2 + 1, 1, v * 2 + 2)
                wrow_out(0, v * 2 + 1)
                diag(v * 2 + 2, 0, v * 2 + 3)
                wrow_out(1, v * 2 + 2)
            diag(NSC - 1, 1, NSC)
            wrow_out(0, NSC - 1)
            wrow_out(1, NSC)

            def normalise(l):
                act.wait_ge(S("ln_var"), l + 1)
                a(lns[0:Q, 4, :], lns[0:Q, 3, :], ACT.Sqrt).then_inc(S("ln_std"), 1)
                act.wait_ge(S("ln_aff"), l + 1)
                with act.Fori(0, NB) as j:
                    a(H[0:Q, bass.ds(j, 1), :].rearrange("p o f -> p (o f)"),
                      X[0:Q, bass.ds(j, 1), :].rearrange("p o f -> p (o f)"), ACT.Relu,
                      scale=lns[0:Q, 4, bass.ds(j, 1)], bias=lns[0:Q, 5, bass.ds(j, 1)]).then_inc(S("ln_done"), 1)

            normalise(0)

            def batch_norm(y, bn, buf, bias):
                n = 0
                for c in range(KT):
                    for n0, nn in NCH:
                        act.wait_ge(S("ring_pe"), base[y] + n + 1)
                        a(buf[:, c, n0:n0 + nn], ps[:, n % 4, 0:nn], ACT.Identity, bias=cols[:, bias, c:c + 1])\
                            .then_inc(S("ring_ev"), 1)
                        n += 1
                act.wait_ge(S(bn + "_var"), 1)
                a(aff[:, 1, 0:KT], aff[:, 0, 0:KT], ACT.Sqrt).then_inc(S(bn + "_std"), 1)
                act.wait_ge(S(bn + "_aff"), 1)
                for c in range(KT):
                    a(buf[:, c, :], buf[:, c, :], ACT.Relu, scale=aff[:, 2, c:c + 1], bias=aff[:, 3, c:c + 1])\
                        .then_inc(S(bn + "_done"), 1)

            batch_norm("y1", "bn1", G, 0)
            batch_norm("y2", "bn2", F, 3)
            normalise(1)

            def counts(i, s, k, kr):
                act.wait_ge(S(f"L1arows{s}"), kr)
                a(Rp[s][0:Q, :, 1], Rp[s][0:Q, :, 1], ACT.Copy, accum_out=norm[0:Q, bass.ds(i, 1)])\
                    .then_inc(S("deg_made"), 1)
                act.wait_ge(S("self_added"), k)
                a(Rp[s][:, :, 1], Rp[s][:, :, 1], ACT.Ln, bias=small[:, 1:2]).then_inc(S("ln_made"), 1)

            act.wait_ge(S("small_made"), 1)
            with act.Fori(0, PAIRS) as v:
                counts(v * 2, 0, v * 2 + 1, (v + 1) * 16)
                counts(v * 2 + 1, 1, v * 2 + 2, (v + 1) * 16)
            counts(NB - 1, 0, NB, (PAIRS + 1) * 16)
            act.wait_ge(S("deg_max"), 1)
            a(norm[0:Q, :], norm[0:Q, :], ACT.Sqrt).then_inc(S("deg_std"), 1)

            normalise(2)
            normalise(3)

            def scores(name, row, col, s, k):
                act.wait_ge(S(name + "tr"), k)
                a(scr[s][0:Q, :], row[0:Q, :], ACT.Identity, bias=col).then_inc(S(name + "score"), 1)

            def expo(name, s, k):
                act.wait_ge(S(name + "max"), k)
                a(scr[s][0:Q, :], scr[s][0:Q, :], ACT.Exp, bias=mx[0:Q, 2 + s:3 + s], accum_out=mx[0:Q, 4 + s:5 + s])\
                    .then_inc(S(name + "prob"), 1)

            act.wait_ge(S("als_in"), 16 * HEADS)
            act.wait_ge(S("ald_made"), 1)

            def sc3(i, u, v):
                scores("L3a", als[u % 4], ald[0:Q, bass.ds(i, 1), u % 4], u % 2, (v * 4 + u + 1) * NG)

            sc3(0, 0, 0)
            with act.Fori(0, NB - 1) as v:
                for u in range(4):
                    sc3(v + (u + 1) // 4, u + 1, v)
                    expo("L3a", u % 2, v * 4 + u + 1)
            for u in range(4):
                if u < 3:
                    sc3(NB - 1, u + 1, NB - 1)
                expo("L3a", u % 2, 4 * (NB - 1) + u + 1)

            act.wait_ge(S("gn_var"), 1)
            a(aff[:, 1, :], aff[:, 0, :], ACT.Sqrt).then_inc(S("gn_std"), 1)
            act.wait_ge(S("gn_aff"), 1)
            for c, (n0, nn) in enumerate(NCH):
                act.wait_ge(S(f"wide_in{c % 2}"), 16 * (c // 2 + 1))
                slot = R[:, (c % 2) * 4096:(c % 2) * 4096 + CT * nn].rearrange("p (t n) -> p t n", t=CT)
                for t in range(CT):
                    a(slot[:, t, :], slot[:, t, :], ACT.Relu, scale=aff[:, 2, t:t + 1], bias=aff[:, 3, t:t + 1])\
                        .then_inc(S("wide_norm"), 1)

            act.wait_ge(S("als2_in"), 16)
            act.wait_ge(S("ring_ev"), base["z3"] + NB)

            def sc4(i, s, k):
                scores("L3b", als[2], ald[0:Q, bass.ds(i, 1), 0], s, k)

            sc4(0, 0, NG)
            with act.Fori(0, PAIRS) as v:
                sc4(v * 2 + 1, 1, (v * 2 + 2) * NG)
                expo("L3b", 0, v * 2 + 1)
                sc4(v * 2 + 2, 0, (v * 2 + 3) * NG)
                expo("L3b", 1, v * 2 + 2)
            expo("L3b", 0, NB)

        @block.vector
        def _(dve):
            v_ = nc.vector
            tt, ts, stt, cp = v_.tensor_tensor, v_.tensor_scalar, v_.scalar_tensor_tensor, v_.tensor_copy
            link = Chain(dve, S("dve_chain"))

            v_.memset(R[:, 0:2 * N], 0.0).then_inc(S("zero_made"), 1)
            v_.memset(ones[:, :], 1.0).then_inc(S("ones_made"), 1)
            link.mark(v_.memset(val, 0.0))
            v_.memset(small[:, 1:2], TINY).then_inc(S("small_made"), 1)

            dve.wait_ge(S("edges_in"), 48)

            def block_of(out_, in_i, tmp):
                link(cp(out_, in_i))
                link(ts(tmp, out_, 1.0 / NB, 0.5 / NB - 0.5, ALU.mult, ALU.add))
                link(ts(tmp, tmp, ROUND, None, ALU.add))
                link(ts(tmp, tmp, ROUND, None, ALU.subtract))

            block_of(e1, dst_i, e2)
            link(ts(e1, e1, 128.0, None, ALU.mult))
            link(stt(e1, e2, -(128.0 * NB - 1.0), e1, ALU.mult, ALU.add))
            link(ts(key, e1, float(N), None, ALU.mult))
            block_of(e1, src_i, e2)
            link(stt(key, e1, float(Q), key, ALU.mult, ALU.add))
            stt(key, e2, -(float(Q) * NB - 1.0), key, ALU.mult, ALU.add).then_inc(S("key_made"), 1)
            dve.wait_ge(S("pool_consts"), 3 + SC)
            dve.wait_ge(S("key_made"), 1)
            link(cp(trash[:, :], trash_i[:, :]))
            link(cp(key_u.rearrange("p (t i) -> p t i", i=SC), trash[:, :].unsqueeze(1).to_broadcast([128, NSC, SC])))
            trashb = trash[0:Q, :].unsqueeze(1).to_broadcast([Q, 2, SC])

            dve.sem_inc(S("keyrow_free"), CREDIT)

            def merge(t, s, k):
                dve.wait_ge(S("wrow_out"), k)
                for i in range(SC):
                    c = t * SC + i
                    link.join(1)
                    link.mark(stt(junk[0], ps[0:Q, s, 0:W], key[:, bass.ds(c, 1)], wrow[s], ALU.is_equal, ALU.mult,
                                  accum_out=val[0:Q, bass.ds(c, 1), 0]))
                    link.join(1)
                    link.mark(stt(junk[1], ps[0:Q, s, 0:W], key[:, bass.ds(c, 1)], tri[:, i, :], ALU.is_equal,
                                  ALU.mult, accum_out=val[0:Q, bass.ds(c, 1), 1]))
                link.join()
                dve.sem_inc(S("keyrow_free"), 1)

            for v in link.loop(NSC // 2, 3 + 4 * SC):
                merge(v * 2, 0, v * 2 + 1 + CREDIT)
                merge(v * 2 + 1, 1, v * 2 + 2 + CREDIT)
                kk = key[:, bass.ds(v * (2 * SC), 2 * SC)].rearrange("p (a i) -> p a i", i=SC)
                f8 = small[0:Q, 8:8 + 2 * SC].rearrange("p (a i) -> p a i", i=SC)
                d8 = small[0:Q, 16:16 + 2 * SC].rearrange("p (a i) -> p a i", i=SC)
                link.mark(ts(f8, val[0:Q, bass.ds(v * (2 * SC), 2 * SC), 1].rearrange("p (a i) -> p a i", i=SC),
                             MARK, None, ALU.is_lt))
                link(tt(d8, kk, trashb, ALU.subtract))
                link(tt(d8, d8, f8, ALU.mult))
                tt(key_u[0:Q, bass.ds(v * (2 * SC), 2 * SC)].rearrange("p (a i) -> p a i", i=SC), d8, trashb,
                   ALU.add).then_inc(S("merged"), 1)

            dve.wait_ge(S("w_in"), 16 * 29)
            for k in range(KT):
                for w in range(2):
                    for h in range(HEADS):
                        link(stt(att_junk, w31[:, k, h * D:(h + 1) * D], 1.0, att1[w][:, h * D:(h + 1) * D],
                                 ALU.mult, ALU.mult, accum_out=va[:, k, w * HEADS + h:w * HEADS + h + 1]))
            dve.sem_inc(S("va_made"), 1)
            for k in range(CT):
                for w in range(2):
                    link(stt(att_junk, w32[:, k, 0:D], 1.0, att2[w], ALU.mult, ALU.mult,
                             accum_out=w32[:, k, D + w:D + w + 1]))
            dve.sem_inc(S("v2_made"), 1)
            link(cp(small[:, 4:5], idx_i[:, 0:1]))
            ts(pick[:, :], node[:, :], small[:, 4:5], None, ALU.is_equal).then_inc(S("pick_made"), 1)
            link(ts(small[:, 5:6], small[:, 0:1], 1.0, None, ALU.add))

            def ln_stats(l):
                L = [lns[0:Q, k, :] for k in range(6)]
                with dve.Fori(0, NB) as j:
                    v_.bn_stats(st[0:Q, bass.ds(j, 1), :].rearrange("p o s -> p (o s)"),
                                X[0:Q, bass.ds(j, 1), :].rearrange("p o f -> p (o f)")).then_inc(S("ln_st"), 1)
                dve.wait_ge(S("ln_st"), (l + 1) * NB)
                link.mark(tt(L[0], st[0:Q, :, 1], st[0:Q, :, 4], ALU.add))
                link.mark(tt(L[1], st[0:Q, :, 1], st[0:Q, :, 4], ALU.subtract))
                link(tt(L[2], st[0:Q, :, 2], st[0:Q, :, 5], ALU.add))
                link.mark(ts(L[0], L[0], 0.5, None, ALU.mult))
                link.mark(tt(L[1], L[1], L[1], ALU.mult))
                link(ts(L[2], L[2], 1.0 / D, LN_EPS, ALU.mult, ALU.add))
                stt(L[3], L[1], 0.25, L[2], ALU.mult, ALU.add).then_inc(S("ln_var"), 1)
                dve.wait_ge(S("ln_std"), l + 1)
                link(v_.reciprocal(L[4], L[4]))
                stt(L[5], L[0], -1.0, L[4], ALU.mult, ALU.mult).then_inc(S("ln_aff"), 1)

            dve.wait_ge(S("x_in"), 16)
            ln_stats(0)

            dve.wait_ge(S("ln_done"), 1 * NB)
            for h, (j0, nj) in enumerate(HALF):
                dve.wait_ge(S(f"L0used{h}"), NB + CREDIT)
                stt(Bn[0:Q, j0:j0 + nj, :].rearrange("p j f -> p (j f)"),
                    H[0:Q, j0:j0 + nj, :].rearrange("p j f -> p (j f)"), small[0:Q, 5:6], psflat[0:Q, 0:nj * D],
                    ALU.mult, ALU.add).then_inc(S("L0sum"), 1)

            def evac_features(name):
                for n, (k, j, nj) in enumerate(QG):
                    dve.wait_ge(S("ring_pe"), base[name] + n + 1)
                    cp(F[:, k, j * Q:(j + nj) * Q], ps[:, n % 4, 0:nj * Q]).then_inc(S("ring_ev"), 1)

            evac_features("z")

            def bn_stats(y, bn, buf, g_, be):
                n = 0
                for c in range(KT):
                    for m, (n0, nn) in enumerate(NCH):
                        dve.wait_ge(S("ring_ev"), base[y] + n + 1)
                        link.mark(v_.bn_stats(bst[:, c, m, :], buf[:, c, n0:n0 + nn]))
                        n += 1
                link.join()
                for c in range(KT):
                    link.mark(v_.bn_aggr(mv[:, c, :], bst[:, c, :, :].rearrange("p m s -> p (m s)")))
                link.join()
                ts(aff[:, 0, 0:KT], mv[:, 0:KT, 1], BN_EPS, None, ALU.add).then_inc(S(bn + "_var"), 1)
                dve.wait_ge(S(bn + "_std"), 1)
                link(v_.reciprocal(aff[:, 1, 0:KT], aff[:, 1, 0:KT]))
                link(tt(aff[:, 2, 0:KT], aff[:, 1, 0:KT], cols[:, g_, :], ALU.mult))
                link(tt(aff[:, 4, 0:KT], aff[:, 2, 0:KT], mv[:, 0:KT, 0], ALU.mult))
                tt(aff[:, 3, 0:KT], cols[:, be, :], aff[:, 4, 0:KT], ALU.subtract).then_inc(S(bn + "_aff"), 1)

            bn_stats("y1", "bn1", G, 1, 2)
            dve.wait_ge(S("bn1_done"), 2)
            bn_stats("y2", "bn2", F, 4, 5)
            for n, (j, nj) in enumerate(JP):
                dve.wait_ge(S("ring_pe"), base["l0"] + n + 1)
                xx = X[0:Q, j:j + nj, :].rearrange("p j f -> p (j f)")
                tt(xx, xx, ps[0:Q, n % 4, 0:nj * D], ALU.add).then_inc(S("ring_ev"), 1)
            dve.wait_ge(S("ring_ev"), base["l0"] + len(JP))

            ln_stats(1)
            evac_features("h1")
            dve.sem_inc(S("r_free_L1a"), 1)

            def root_column(name, bname, leaky):
                dve.wait_ge(S(name), 1)
                if leaky:
                    link(ts(small[:, 26:28], ps[:, 6, 0:KT], 0.01, None, ALU.mult))
                    link(tt(rootc[:, :], small[:, 26:28], ps[:, 6, 0:KT], ALU.max))
                else:
                    link(cp(rootc[:, :], ps[:, 6, 0:KT]))
                for k in range(KT):
                    link.mark(ts(rootb[:, k, :], ones[:, 0:Q], rootc[:, k:k + 1], None, ALU.mult))
                link.join()
                dve.sem_inc(S(bname), 1)

            root_column("root1", "rootb1", True)
            for n, (j, nj) in enumerate(JP):
                dve.wait_ge(S("ring_pe"), base["t1"] + n + 1)
                cp(Bn[0:Q, j:j + nj, :].rearrange("p j f -> p (j f)"), ps[0:Q, n % 4, 0:nj * D]).then_inc(S("ring_ev"), 1)

            def evac_group(name, s, ktr, kmm):
                dve.wait_ge(S(name + "tr"), ktr)
                dve.wait_ge(S(name + "mm"), kmm)
                cp(PT[0:Q, s, :].rearrange("p (b q) -> p b q", q=Q), tps[s][0:Q, :, 0:Q]).then_inc(S(name + "ev"), 1)

            def sums(name, out_unit, each_unit=None):
                dve.sem_inc(S(name + "ev"), CREDIT)
                dve.sem_inc(S(name + "out"), CREDIT)

                def unit(u, par, first=False):
                    for g in range(NG):
                        evac_group(name, (par * NG + g) % 2, u * NG + g + 1 + CREDIT_TR, u * NG + g + 1)
                        if g == 0 and not first:
                            dve.wait_ge(S(name + "mm"), u * NG + CREDIT)
                            out_unit(u - 1, 1 - par)
                        if g == 1 and each_unit:
                            each_unit(u, par)

                unit(0, 0, True)
                return unit

            def out_bias(bias, name):
                def f(i, s):
                    tt(H[0:Q, bass.ds(i, 1), :].rearrange("p o f -> p (o f)"), acc[s], bcs[0:Q, bias, :], ALU.add)\
                        .then_inc(S(name + "out"), 1)
                return f

            dve.sem_inc(S("lnc_read"), CREDIT)

            def lnc_unit(i, s, rows, k):
                dve.wait_ge(S("deg_made"), k)
                dg = Rp[s][0:Q, bass.ds(i * Q, Q), 1]
                tt(dg, dg, ident[0:Q, 0:Q], ALU.add).then_inc(S("diag_in"), 1)
                dve.wait_ge(S("diag_in"), k)
                if rows is not None:
                    dve.wait_ge(S(f"lnc_out{s}"), rows)
                ts(lncW[s], Rp[s][:, :, 1], 0.5, NEG, ALU.is_lt, ALU.mult).then_inc(S("self_added"), 1)

            def lnc_unit2(s, k):
                dve.wait_ge(S("ln_made"), k)
                tt(lncW[s], lncW[s], Rp[s][:, :, 1], ALU.add).then_inc(S("lnc_read"), 1)

            def pass_1a():
                name = "L1a"
                out_unit = out_bias(0, name)
                dve.sem_inc(S(name + "ev"), CREDIT)
                dve.sem_inc(S(name + "out"), CREDIT)
                dve.wait_ge(S("ring_ev"), base["t1"] + len(JP))

                def unit(u, par, klnc, first=False):
                    for g in range(NG):
                        evac_group(name, (par * NG + g) % 2, u * NG + g + 1 + CREDIT_TR, u * NG + g + 1)
                        if g == 0 and not first:
                            dve.wait_ge(S(name + "mm"), u * NG + CREDIT)
                            out_unit(u - 1, 1 - par)
                        if g == 1:
                            lnc_unit(u, par, klnc, u + 1)
                        if g == 3:
                            lnc_unit2(par, u + 1)

                unit(0, 0, None, True)
                unit(1, 1, None)
                with dve.Fori(0, PAIRS - 1) as v:
                    unit(v * 2 + 2, 0, (v + 1) * 16)
                    unit(v * 2 + 3, 1, (v + 1) * 16)
                unit(NB - 1, 0, PAIRS * 16)
                dve.wait_ge(S(name + "mm"), NB * NG + CREDIT)
                out_unit(NB - 1, 0)

            pass_1a()

            def plain_pass(name, out_unit):
                unit = sums(name, out_unit)
                with dve.Fori(0, PAIRS) as v:
                    unit(v * 2 + 1, 1)
                    unit(v * 2 + 2, 0)
                dve.wait_ge(S(name + "mm"), NB * NG + CREDIT)
                out_unit(NB - 1, 0)

            dve.wait_ge(S("deg_made"), NB)
            ts(norm[0:Q, :], norm[0:Q, :], 1.0, None, ALU.max).then_inc(S("deg_max"), 1)
            dve.wait_ge(S("lnc_read"), NB + CREDIT)
            dve.sem_inc(S("L1a_done"), 1)
            dve.wait_ge(S("rootr1"), 1)
            cp(rootr[0:Q, :], ps[0:Q, 7, 0:D]).then_inc(S("rootr_used"), 1)
            dve.wait_ge(S("L1aout"), NB + CREDIT)
            root_column("root2", "rootb2", False)
            hh = H[0:Q, :, :].rearrange("p j f -> p (j f)")
            stt(hh, hh, 0.01, hh, ALU.mult, ALU.max).then_inc(S("f2_leaky"), 1)
            dve.wait_ge(S("lnc_out0"), 16 * (PAIRS + 1))
            dve.wait_ge(S("lnc_out1"), 16 * PAIRS)
            evac_features("h2")
            rb2 = rootr[0:Q, :].unsqueeze(1)
            dve.wait_ge(S("rootr_used"), 1)
            for n, (j, nj) in enumerate(JP):
                dve.wait_ge(S("ring_pe"), base["t2"] + n + 1)
                tt(Bn[0:Q, j:j + nj, :], ps[0:Q, n % 4, 0:nj * D].rearrange("p (j f) -> p j f", f=D),
                   rb2.to_broadcast([Q, nj, D]), ALU.add).then_inc(S("ring_ev"), 1)
            plain_pass("L1b", out_bias(1, "L1b"))
            dve.wait_ge(S("ring_ev"), base["t2"] + len(JP))
            dve.sem_inc(S("L1b_done"), 1)
            dve.wait_ge(S("rootr2"), 1)
            tt(rootr[0:Q, :], ps[0:Q, 7, 0:D], bcs[0:Q, 2, :], ALU.add).then_inc(S("rootr_used"), 1)
            dve.wait_ge(S("L1bout"), NB + CREDIT)
            stt(hh, hh, 0.01, hh, ALU.mult, ALU.max).then_inc(S("f3_leaky"), 1)
            evac_features("h3")
            dve.wait_ge(S("rootr_used"), 2)
            for n, (j, nj) in enumerate(JP):
                dve.wait_ge(S("ring_pe"), base["t3"] + n + 1)
                bb = Bn[0:Q, j:j + nj, :]
                tt(bb, ps[0:Q, n % 4, 0:nj * D].rearrange("p (j f) -> p j f", f=D),
                   rb2.to_broadcast([Q, nj, D]), ALU.add).then_inc(S("ring_ev"), 1)
            dve.wait_ge(S("ring_ev"), base["t3"] + len(JP))
            bb = B[0:Q, 0:NB * D]
            xx = X[0:Q, :, :].rearrange("p j f -> p (j f)")
            link(stt(bb, bb, 0.01, bb, ALU.mult, ALU.max))
            link(tt(xx, xx, bb, ALU.add))
            dve.wait_ge(S("w2T_pe"), 1)
            cp(w2T[:, :, :].rearrange("p k n -> p (k n)"), ps[:, 7, :]).then_inc(S("w2T_made"), 1)

            ln_stats(2)
            evac_features("h4")
            dve.wait_ge(S("deg_std"), 1)
            link(v_.reciprocal(norm[0:Q, :], norm[0:Q, :]))
            for n, (j, nj) in enumerate(JP):
                dve.wait_ge(S("ring_pe"), base["t4"] + n + 1)
                bb = Bn[0:Q, j:j + nj, :]
                link(tt(bb, ps[0:Q, n % 4, 0:nj * D].rearrange("p (j f) -> p j f", f=D),
                        bcs[0:Q, 3, :].unsqueeze(1).to_broadcast([Q, nj, D]), ALU.add))
                tt(bb, bb, norm[0:Q, j:j + nj].unsqueeze(2).to_broadcast([Q, nj, D]), ALU.mult)\
                    .then_inc(S("ring_ev"), 1)

            def out_residual(name, col):
                def f(i, s):
                    xi = X[0:Q, bass.ds(i, 1), :].rearrange("p o f -> p (o f)")
                    stt(xi, acc[s], col(i, s), xi, ALU.mult, ALU.add).then_inc(S(name + "out"), 1)
                return f

            plain_pass("L2", out_residual("L2", lambda i, s: norm[0:Q, bass.ds(i, 1)]))
            dve.wait_ge(S("L2out"), NB + CREDIT)

            ln_stats(3)
            evac_features("h5")
            for n, (n0, nn) in enumerate(NCH):
                dve.wait_ge(S("ring_pe"), base["alsrow"] + n + 1)
                cp(R[0:2 * HEADS, n0:n0 + nn], ps[0:2 * HEADS, n % 4, 0:nn]).then_inc(S("ring_ev"), 1)
            dve.wait_ge(S("ring_ev"), base["alsrow"] + len(NCH))
            dve.sem_inc(S("alsrow_made"), 1)
            dve.wait_ge(S("ald_mm"), 1)
            cp(ald[0:Q, :, :].rearrange("p j h -> p (j h)"), ps[0:Q, 6, 0:NB * HEADS]).then_inc(S("ald_made"), 1)
            link(tt(X[0:Q, :, :], X[0:Q, :, :], bcs[0:Q, 4, :].unsqueeze(1).to_broadcast([Q, NB, D]), ALU.add))
            dve.wait_ge(S("alsrow_out"), 16)
            dve.sem_inc(S("L3alnc_used"), CREDIT)

            def mask(name, rs, s, kl, k, klnc, last_use):
                if klnc is not None:
                    dve.wait_ge(S(f"{name}lnc{rs}"), klnc)
                dve.wait_ge(S(name + "score"), k)
                link(stt(scr[s][0:Q, :], scr[s][0:Q, :], 0.2, scr[s][0:Q, :], ALU.mult, ALU.max))
                dve.sem_inc(S("masks_begun"), 1)
                ins = v_.tensor_tensor_reduce(scr[s][0:Q, :], scr[s][0:Q, :], lncR[rs][0:Q, :], 1.0, 2.0 * NEG,
                                              ALU.add, ALU.max, accum_out=mx[0:Q, s:s + 1])
                link(ins)
                ts(mx[0:Q, 2 + s:3 + s], mx[0:Q, s:s + 1], -1.0, None, ALU.mult).then_inc(S(name + "max"), 1)
                if last_use:
                    dve.sem_inc(S(name + "lnc_used"), 1)

            def denom(s):
                return link(v_.reciprocal(mx[0:Q, 6 + s:7 + s], mx[0:Q, 4 + s:5 + s]))

            def attention_out(u, s, k):
                dve.wait_ge(S("L3amm"), k)
                ts(ag[0:Q, s, :], acc[s], mx[0:Q, 6 + s:7 + s], None, ALU.mult).then_inc(S("L3aout"), 1)

            def wide_in(k):
                dve.wait_ge(S("agT_pe"), k)
                cp(agT[:, :, :].rearrange("p t q -> p (t q)"), ps[:, 6, 0:KT * Q]).then_inc(S("agT_made"), 1)

            def wide_out(hd, ys, k):
                dve.wait_ge(S("y_pe"), k)
                for c in range(KT):
                    t = hd * KT + c
                    link.mark(ts(yT[:, ys, t, :], ps[:, 7, c * Q:(c + 1) * Q], colw[:, 0, t:t + 1], None, ALU.add))
                link.join()

            def wide_stats(i, ys):
                for t in range(CT):
                    last = v_.bn_stats(gst[:, t, bass.ds(i * 6, 6)], yT[:, ys, t, :])
                last.then_inc(S("y_made"), 1)

            def steps(i, h, par, v, klnc, first=False, last=False):
                u = i * 4 + h
                s = h % 2
                for g in range(NG):
                    evac_group("L3a", (h * NG + g) % 2, u * NG + g + 1 + CREDIT_TR, u * NG + g + 1)
                    if g == 0:
                        if not first:
                            attention_out(u - 1, 1 - s, u * NG + CREDIT)
                        denom(s)
                        if not last:
                            nh = (h + 1) % 4
                            npar = par if h < 3 else 1 - par
                            mask("L3a", npar, 1 - s, None, u + 2, klnc if nh == 0 else None, nh == 3)
                    if not first and g == 1:
                        wide_in(u)
                    if not first and g == 3:
                        hd = (h - 1) % 4
                        ypar = par if h > 0 else 1 - par
                        if hd == 0:
                            dve.wait_ge(S("y_free"), i + 1)
                        wide_out(hd, ypar, u)
                        if hd == 3:
                            wide_stats(i - 1, ypar)

            dve.sem_inc(S("L3aev"), CREDIT)
            dve.sem_inc(S("L3aout"), CREDIT)
            mask("L3a", 0, 0, None, 1, 16, False)
            steps(0, 0, 0, 0, None, first=True)
            for v in link.loop(PAIRS, 8 * 5):
                i0 = v * 2
                for h in range(1, 4):
                    steps(i0, h, 0, v, (v + 1) * 16)
                for h in range(0, 4):
                    steps(i0 + 1, h, 1, v, (v + 2) * 16)
                steps(i0 + 2, 0, 0, v, None)
            for h in range(1, 4):
                steps(NB - 1, h, 0, PAIRS, None, last=h == 3)
            U = 4 * NB
            attention_out(U - 1, 1, U * NG + CREDIT)
            wide_in(U)
            wide_out(3, 0, U)
            wide_stats(NB - 1, 0)
            dve.wait_ge(S("y_made"), NB)

            for t in range(CT):
                link.mark(v_.bn_aggr(mv[:, t, :], gst[:, t, :]))
            link.join()
            link(ts(aff[:, 4, :], colw[:, 3, :], -1.0, 1.0, ALU.mult, ALU.add))
            link(tt(aff[:, 4, :], aff[:, 4, :], mv[:, :, 0], ALU.mult))
            link(tt(aff[:, 4, :], aff[:, 4, :], aff[:, 4, :], ALU.mult))
            stt(aff[:, 0, :], mv[:, :, 1], BN_EPS, aff[:, 4, :], ALU.add, ALU.add).then_inc(S("gn_var"), 1)
            dve.wait_ge(S("gn_std"), 1)
            link(v_.reciprocal(aff[:, 1, :], aff[:, 1, :]))
            link(tt(aff[:, 2, :], aff[:, 1, :], colw[:, 1, :], ALU.mult))
            link(tt(aff[:, 4, :], colw[:, 3, :], mv[:, :, 0], ALU.mult))
            link(tt(aff[:, 4, :], aff[:, 4, :], aff[:, 2, :], ALU.mult))
            tt(aff[:, 3, :], colw[:, 2, :], aff[:, 4, :], ALU.subtract).then_inc(S("gn_aff"), 1)

            n = 0
            for c, (n0, nn) in enumerate(NCH):
                for b in range(nn // Q):
                    dve.wait_ge(S("ring_pe"), base["z3"] + n + 1)
                    cp(Bn[0:Q, n, :], ps[0:Q, n % 4, 0:D])
                    cp(ald[0:Q, n, 0:1], ps[0:Q, n % 4, D + 1:D + 2]).then_inc(S("ring_ev"), 1)
                    n += 1
                dve.wait_ge(S("wide_used"), c + 1)
                cp(R[0:2, 8192 + n0:8192 + n0 + nn], ps[0:2, 4 + c % 2, 0:nn]).then_inc(S("row2_ev"), 1)
            dve.wait_ge(S("row2_ev"), len(NCH))
            dve.sem_inc(S("row2_made"), 1)
            dve.wait_ge(S("row2_out"), 16)

            dve.sem_inc(S("L3blnc_used"), CREDIT)
            dve.sem_inc(S("L3bev"), CREDIT)
            dve.sem_inc(S("L3bout"), CREDIT)

            def last_out(i, s):
                xi = X[0:Q, bass.ds(i, 1), :].rearrange("p o f -> p (o f)")
                stt(xi, acc[s], mx[0:Q, 6 + s:7 + s], xi, ALU.mult, ALU.add).then_inc(S("L3bout"), 1)

            def unit(u, par, klnc, first=False, last=False):
                for g in range(NG):
                    evac_group("L3b", (par * NG + g) % 2, u * NG + g + 1 + CREDIT_TR, u * NG + g + 1)
                    if g == 0:
                        if not first:
                            dve.wait_ge(S("L3bmm"), u * NG + CREDIT)
                            last_out(u - 1, 1 - par)
                        denom(par)
                        if not last:
                            mask("L3b", 1 - par, 1 - par, None, u + 2, klnc, True)

            mask("L3b", 0, 0, None, 1, 16, True)
            unit(0, 0, 16, first=True)
            for v in link.loop(PAIRS - 1, 6):
                unit(v * 2 + 1, 1, (v + 2) * 16)
                unit(v * 2 + 2, 0, (v + 2) * 16)
            unit(NB - 2, 1, (PAIRS + 1) * 16)
            unit(NB - 1, 0, None, last=True)
            dve.wait_ge(S("L3bmm"), NB * NG + CREDIT)
            last_out(NB - 1, 0)


_INS = ["x", "src", "dst", "edge_weight", "L0_gnn_eps", "L0_gnn_W1", "L0_gnn_b1", "L0_gnn_g1", "L0_gnn_be1",
        "L0_gnn_W2", "L0_gnn_b2", "L0_gnn_g2", "L0_gnn_be2", "L1_gnn_W1", "L1_gnn_b1", "L1_gnn_W2", "L1_gnn_b2",
        "L1_gnn_Wl", "L1_gnn_bl", "L1_gnn_root_idx", "L2_gnn_W", "L2_gnn_b", "L3_gnn_W1", "L3_gnn_att_src1",
        "L3_gnn_att_dst1", "L3_gnn_b1", "L3_gnn_gn_w", "L3_gnn_gn_b", "L3_gnn_gn_ms", "L3_gnn_W2",
        "L3_gnn_att_src2", "L3_gnn_att_dst2", "L3_gnn_b2"]


def kernel(**inputs):
    import numpy as _np
    import concourse.bacc as _bacc
    from concourse import mybir as _mybir
    from concourse.bass_utils import run_bass_kernel_spmd as _run

    nc = _bacc.Bacc("TRN2", target_bir_lowering=False, num_devices=1)
    arrays, args = {}, []
    for name in _INS:
        a = _np.ascontiguousarray(inputs[name])
        arrays["in_" + name] = a
        args.append(nc.dram_tensor("in_" + name, a.shape, _mybir.dt.from_np(a.dtype), kind="ExternalInput").ap())
    args.append(nc.dram_tensor("out_0", (N, D), F32, kind="ExternalOutput").ap())
    gnn_stack(nc, *args)
    r = _run(nc, [arrays], core_ids=[0])
    return r.results[0]["out_0"]
```

```python
from contextlib import ExitStack

import concourse.bass as bass
from concourse import mybir

ALU = mybir.AluOpType
ACT = mybir.ActivationFunctionType
F32 = mybir.dt.float32
I32 = mybir.dt.int32
U32 = mybir.dt.uint32
AX_X = mybir.AxisListType.X

N = 3125
Q = 125
NB = N // Q
D = 256
KT = D // 128
E = 50000
EC = E // Q
HEADS = 4
WIDE = HEADS * D
CT = WIDE // 128
ROWS = NB * 128
SC = 4
NSC = EC // SC
TRASH = ROWS * N
GROUPS = [(0, 4), (4, 4), (8, 4), (12, 4), (16, 3), (19, 3), (22, 3)]
NG = len(GROUPS)
RING = 4
AHEAD = RING - 1
NA = (NG + 1) // 2
ND = NG // 2
HALF = [(0, 13), (13, 12)]
LN_EPS = 1e-5
BN_EPS = 1e-5
NEG = -1.0e30
TINY = 1.0e-18
MARK = 1024.0
ROUND = 12582912.0
CREDIT_TR = 2 * NG
CREDIT = 2


class Chain:

    def __init__(self, eng, sem):
        self.eng, self.sem, self.n, self.iv, self.per = eng, sem, 0, None, 0

    def value(self):
        return self.n if self.iv is None else self.iv * self.per + self.n

    def mark(self, ins):
        self.n += 1
        ins.then_inc(self.sem, 1)

    def join(self, but=0):
        self.eng.wait_ge(self.sem, self.value() - but)

    def __call__(self, ins):
        self.mark(ins)
        self.join()

    def loop(self, trips, per):
        with self.eng.Fori(0, trips) as iv:
            n0 = self.n
            self.iv, self.per = iv, per
            yield iv
            assert self.n - n0 == per, (self.n - n0, per)
        self.iv = None
        self.n = n0 + per * trips


def gnn_stack(nc, x, src, dst, edge_weight, eps0, W01, b01, g01, be01, W02, b02, g02, be02,
              W11, b11, W12, b12, Wl1, bl1, root_idx, W2, b2, W31, as31, ad31, b31, gnw, gnb, gnms,
              W32, as32, ad32, b32, out):
    with ExitStack() as ctx:
        sems = {}

        def S(name):
            if name not in sems:
                sems[name] = ctx.enter_context(nc.semaphore(name))
            return sems[name]

        def sb(name, shape, dt=F32):
            return ctx.enter_context(nc.sbuf_tensor(name, shape, dt))

        pairs = nc.dram_tensor("pairs", (TRASH + SC * 128, 2), F32, kind="Internal").ap()
        lnc_d = nc.dram_tensor("lnc_d", (NB, 128, N), F32, kind="Internal").ap()
        rows_d = nc.dram_tensor("rows_d", (2 * HEADS, N), F32, kind="Internal").ap()
        wide_d = nc.dram_tensor("wide_d", (128, CT, N), F32, kind="Internal").ap()
        x_d = nc.dram_tensor("x_d", (Q, NB * D), F32, kind="Internal").ap()
        row2_d = nc.dram_tensor("row2_d", (2, N), F32, kind="Internal").ap()
        pair_rows = pairs[0:TRASH, :].rearrange("(i p c) t -> i p c t", p=128, c=N)

        X = sb("X", [128, NB, D])
        H = sb("H", [128, NB, D])
        B = sb("B", [128, NB * D])
        Fb = sb("Fb", [128, KT * N])
        R = sb("R", [128, 4 * N])
        PT = sb("PT", [128, RING, 4 * Q])
        Bn = B[:, :].rearrange("p (j f) -> p j f", f=D)
        F = Fb[:, :].rearrange("p (k n) -> p k n", k=KT)
        G = R[:, 0:2 * N].rearrange("p (k n) -> p k n", k=KT)
        Rp = [R[:, s * 2 * N:(s + 1) * 2 * N].rearrange("p (n t) -> p n t", t=2) for s in range(2)]
        lncR = [R[:, s * N:(s + 1) * N] for s in range(2)]
        XH = [t[:, :, :].rearrange("p j f -> p (j f)") for t in (X, H)]
        scr = [[R[:, 2 * N:3 * N], R[:, 3 * N:4 * N], t[:, 0:N], t[:, N:2 * N]] for t in XH]
        lncW = [Fb[:, s * N:(s + 1) * N] for s in range(2)]
        als = [B[:, 0:N], B[:, N:2 * N], Fb[:, 0:N], Fb[:, N:2 * N]]

        wA = sb("wA", [128, 5 * KT * D])
        w01, w02, w11 = [wA[:, k * KT * D:(k + 1) * KT * D].rearrange("p (k n) -> p k n", k=KT) for k in range(3)]
        w12 = wA[:, 3 * KT * D:5 * KT * D].rearrange("p (k n) -> p k n", k=2 * KT)
        wB = sb("wB", [128, 4 * KT * D])
        wl1 = wB[:, 0:2 * KT * D].rearrange("p (k n) -> p k n", k=2 * KT)
        w2, w2T = [wB[:, k * KT * D:(k + 1) * KT * D].rearrange("p (k n) -> p k n", k=KT) for k in (2, 3)]
        gst = wB[:, 0:CT * NB * 6].rearrange("p (t s) -> p t s", t=CT)
        w31 = sb("w31", [128, KT, WIDE])
        w32 = sb("w32", [128, CT, D + 2])
        va = sb("va", [128, KT, 2 * HEADS])
        cols = sb("cols", [128, 6, KT])
        colw = sb("colw", [128, 4, CT])
        bcs = sb("bcs", [128, 5, D])
        ident = sb("ident", [128, 128])
        ones = sb("ones", [128, 128])
        small = sb("small", [128, 40])
        st = sb("st", [128, NB, 6])
        lns = sb("lns", [128, 6, NB])
        node = sb("node", [128, NB])
        pick = sb("pick", [128, NB])
        norm = sb("norm", [128, NB])
        rootc = sb("rootc", [128, KT])
        rootr = sb("rootr", [128, D])
        ald = sb("ald", [128, NB, HEADS])
        bst = sb("bst", [128, KT, 7, 6])
        mv = sb("mv", [128, CT, 2])
        aff = sb("aff", [128, 6, CT])
        mx = sb("mx", [128, 4, 4])
        ag = sb("ag", [128, 2, D])
        agT = sb("agT", [128, KT, Q])
        rootb = agT
        yT = wA[:, 0:2 * CT * Q].rearrange("p (s t q) -> p s t q", s=2, t=CT)
        idx_i = sb("idx_i", [128, 4], I32)
        stage_k = sb("stage_k", [128, 2, SC], U32)
        stage_v = sb("stage_v", [128, 2, SC, 2])
        trash = sb("trash", [128, SC])
        trash_i = sb("trash_i", [128, SC], I32)

        src_i = Fb[0:Q, 0:EC].bitcast(I32)
        dst_i = Fb[0:Q, EC:2 * EC].bitcast(I32)
        wgt = Fb[0:Q, 2 * EC:3 * EC]
        key = Fb[0:Q, 3 * EC:4 * EC]
        e1 = Fb[0:Q, 4 * EC:5 * EC]
        e2 = Fb[0:Q, 5 * EC:6 * EC]
        key_u = Fb[:, 6 * EC:7 * EC].bitcast(U32)
        val = Fb[:, 7 * EC:9 * EC].rearrange("p (c t) -> p c t", t=2)
        M0 = 2 * N
        W = SC * Q
        tri = R[0:Q, M0:M0 + SC * W].rearrange("p (i w) -> p i w", i=SC)
        dgk = [R[0:Q, M0 + (4 + s) * W:M0 + (5 + s) * W].rearrange("p (i q) -> p i q", q=Q) for s in range(2)]
        dgw = [R[0:Q, M0 + (6 + s) * W:M0 + (7 + s) * W].rearrange("p (i q) -> p i q", q=Q) for s in range(2)]
        wrow = [R[0:Q, M0 + (8 + s) * W:M0 + (9 + s) * W] for s in range(2)]
        junk = [R[0:Q, M0 + (10 + s) * W:M0 + (11 + s) * W] for s in range(2)]
        att1 = [B[:, 0:WIDE], B[:, WIDE:2 * WIDE]]
        att2 = [B[:, 2 * WIDE:2 * WIDE + D], B[:, 2 * WIDE + D:2 * WIDE + 2 * D]]
        att_junk = B[:, 2 * WIDE + 2 * D:2 * WIDE + 3 * D]

        ps = ctx.enter_context(nc.psum_tensor("ps", [128, 8, 512], F32))
        psflat = ps[:, :, :].rearrange("p b c -> p (b c)")
        acc = [ps[0:Q, 4 + s, 0:D] for s in range(2)]

        block = ctx.enter_context(nc.Block())

        NCH = [(n0, min(4 * Q, N - n0)) for n0 in range(0, N, 4 * Q)]
        JP = [(j, min(2, NB - j)) for j in range(0, NB, 2)]
        QG = [(k, j, min(4, NB - j)) for k in range(KT) for j in range(0, NB, 4)]
        PAIRS = (NB - 1) // 2

        base, total = {}, 0
        for stage_name, groups in (("z", len(QG)), ("y1", KT * len(NCH)), ("y2", KT * len(NCH)), ("l0", len(JP)),
                                   ("h1", len(QG)), ("t1", len(JP)), ("h2", len(QG)), ("t2", len(JP)),
                                   ("h3", len(QG)), ("t3", len(JP)), ("h4", len(QG)), ("t4", len(JP)),
                                   ("h5", len(QG)), ("alsrow", len(NCH)), ("z3", NB)):
            base[stage_name] = total
            total += groups

        def ring_wait(eng, name, n):
            if n >= 4 or (n == 0 and base[name]):
                eng.wait_ge(S("ring_ev"), base[name] + max(n - 3, 0))

        @block.sync
        def _(sp):
            sp.dma_start(src_i, src.rearrange("(p c) -> p c", c=EC)).then_inc(S("edges_in"), 16)
            sp.dma_start(dst_i, dst.rearrange("(p c) -> p c", c=EC)).then_inc(S("edges_in"), 16)
            sp.dma_start(wgt, edge_weight.rearrange("(p c) -> p c", c=EC)).then_inc(S("edges_in"), 16)
            sp.wait_ge(S("zero_made"), 1)
            flat = pairs[0:TRASH, :].rearrange("(i p c) t -> i p (c t)", p=128, c=N)
            with sp.Fori(0, NB) as i:
                sp.dma_start(flat[bass.ds(i, 1)].rearrange("o p c -> (o p) c"), R[:, 0:2 * N]).then_inc(S("zeroed"), 16)
            sp.dma_start(pairs[TRASH:TRASH + SC * 128, :].rearrange("(p c) t -> p (c t)", p=128),
                         R[:, 0:2 * SC]).then_inc(S("zeroed"), 16)
            sp.dma_start(X[0:Q, :, :], x.rearrange("(p j) f -> p j f", j=NB)).then_inc(S("x_in"), 16)
            w_in = S("w_in")
            nw = 0
            for t, w in ((w01, W01), (w02, W02), (w11, W11), (w12, W12), (wl1, Wl1), (w2, W2), (w31, W31)):
                sp.dma_start(t[:, :, :], w.rearrange("(k p) n -> p k n", p=128)).then_inc(w_in, 16)
                nw += 1
            sp.dma_start(w32[:, :, 0:D], W32.rearrange("(k p) n -> p k n", p=128)).then_inc(w_in, 16)
            for k, a in enumerate((as31, ad31)):
                sp.dma_start(att1[k], a.rearrange("h c -> (h c)").partition_broadcast(128)).then_inc(w_in, 16)
            for k, a in enumerate((as32, ad32)):
                sp.dma_start(att2[k], a.rearrange("h c -> (h c)").partition_broadcast(128)).then_inc(w_in, 16)
            for k, v in enumerate((b11, b12, bl1, b2, b32)):
                sp.dma_start(bcs[:, k, :], v.partition_broadcast(128)).then_inc(w_in, 16)
            sp.dma_start(idx_i[:, 0:1], root_idx[0:1].partition_broadcast(128)).then_inc(w_in, 16)
            sp.dma_start(small[:, 0:1], eps0.partition_broadcast(128)).then_inc(w_in, 16)
            with nc.allow_non_contiguous_dma(reason="a few hundred per-feature values"):
                for k, v in enumerate((b01, g01, be01, b02, g02, be02)):
                    sp.dma_start(cols[:, k, :], v.rearrange("(k p) -> p k", p=128)).then_inc(w_in, 16)
                for k, v in enumerate((b31, gnw, gnb, gnms)):
                    sp.dma_start(colw[:, k, :], v.rearrange("(k p) -> p k", p=128)).then_inc(w_in, 16)

            sp.wait_ge(S("scattered"), 16 * EC)
            for h, (j0, nj) in enumerate(HALF):
                def half_rows(i, s, k):
                    sp.wait_ge(S(f"L0used{h}"), k)
                    r = pair_rows[bass.ds(i, 1)].rearrange("o p c t -> (o p) c t")[:, j0 * Q:(j0 + nj) * Q, :]
                    sp.dma_start(Rp[s][:, 0:nj * Q, :], r).then_inc(S(f"L0rows{h}_{s}"), 16)
                if h:
                    sp.wait_ge(S("L0used0"), NB + CREDIT)
                with sp.Fori(0, PAIRS) as v:
                    half_rows(v * 2, 0, v * 2 + 1)
                    half_rows(v * 2 + 1, 1, v * 2 + 2)
                half_rows(NB - 1, 0, NB)

            def pair_pass(name, extra=None):
                def load(i, s, k):
                    sp.wait_ge(S(name + "tr"), k * NG)
                    if extra:
                        sp.wait_ge(S(extra), k)
                    sp.dma_start(Rp[s], pair_rows[bass.ds(i, 1)].rearrange("o p c t -> (o p) c t"))\
                        .then_inc(S(f"{name}rows{s}"), 16)

                with sp.Fori(0, PAIRS) as v:
                    load(v * 2, 0, v * 2 + 1)
                    load(v * 2 + 1, 1, v * 2 + 2)
                load(NB - 1, 0, NB)

            sp.wait_ge(S("r_free_L1a"), 1)
            pair_pass("L1a", "lnc_read")
            sp.wait_ge(S("L1a_done"), 1)
            pair_pass("L1b")
            sp.wait_ge(S("L1b_done"), 1)
            pair_pass("L2")

            sp.wait_ge(S("alsrow_made"), 1)
            sp.dma_start(rows_d[:, :], R[0:2 * HEADS, 0:N]).then_inc(S("alsrow_out"), 16)
            sp.wait_ge(S("alsrow_out"), 16)
            sp.wait_ge(S("ald_mm"), 1)
            for h in range(HEADS):
                sp.dma_start(als[h], rows_d[h, :].partition_broadcast(128)).then_inc(S("als_in"), 16)

            def lnc_load(name, i, s, k):
                sp.wait_ge(S(name + "lnc_used"), k)
                sp.dma_start(lncR[s], lnc_d[bass.ds(i, 1)].rearrange("o p c -> (o p) c"))\
                    .then_inc(S(f"{name}lnc{s}"), 16)

            def wide_store(i, s, k, ks):
                sp.wait_ge(S("y_made"), k)
                with nc.allow_non_contiguous_dma(reason="rows of a block"):
                    sp.dma_start(wide_d[:, :, bass.ds(i * Q, Q)], yT[:, s, :, :]).then_inc(S(f"y_out{s}"), 16)
                sp.wait_ge(S(f"y_out{s}"), ks)
                sp.sem_inc(S("y_free"), 1)

            sp.sem_inc(S("y_free"), CREDIT)
            sp.wait_ge(S("bias_in_x"), 1)
            sp.dma_start(x_d[:, :], XH[0][0:Q, :]).then_inc(S("x_out"), 16)
            lnc_load("L3a", 0, 0, 1)
            lnc_load("L3a", 1, 1, 2)
            with sp.Fori(0, PAIRS - 1) as v:
                lnc_load("L3a", v * 2 + 2, 0, v * 2 + 3)
                wide_store(v * 2, 0, v * 2 + 1, (v + 1) * 16)
                lnc_load("L3a", v * 2 + 3, 1, v * 2 + 4)
                wide_store(v * 2 + 1, 1, v * 2 + 2, (v + 1) * 16)
            lnc_load("L3a", NB - 1, 0, NB)
            wide_store(NB - 3, 0, NB - 2, PAIRS * 16)
            wide_store(NB - 2, 1, NB - 1, PAIRS * 16)
            wide_store(NB - 1, 0, NB, (PAIRS + 1) * 16)
            sp.dma_start(XH[0][0:Q, :], x_d[:, :]).then_inc(S("x_back"), 16)
            for c, (n0, nn) in enumerate(NCH):
                if c >= 2:
                    sp.wait_ge(S("wide_used"), c - 1)
                slot = R[:, (c % 2) * 4096:(c % 2) * 4096 + CT * nn].rearrange("p (t n) -> p t n", t=CT)
                sp.dma_start(slot, wide_d[:, :, n0:n0 + nn]).then_inc(S(f"wide_in{c % 2}"), 16)
            sp.wait_ge(S("row2_made"), 1)
            sp.dma_start(row2_d[:, :], R[0:2, 8192:8192 + N]).then_inc(S("row2_out"), 16)
            sp.wait_ge(S("row2_out"), 16)
            sp.dma_start(als[2], row2_d[0, :].partition_broadcast(128)).then_inc(S("als2_in"), 16)
            sp.wait_ge(S("als2_in"), 16)
            out_v = out.rearrange("(p j) f -> p j f", j=NB)

            def out_store(i):
                sp.wait_ge(S("L3bout"), i + 1 + CREDIT)
                sp.dma_start(out_v[:, bass.ds(i, 1), :], X[0:Q, bass.ds(i, 1), :]).then_inc(S("stored"), 16)

            lnc_load("L3b", 0, 0, 1)
            lnc_load("L3b", 1, 1, 2)
            lnc_load("L3b", 2, 0, 3)
            with sp.Fori(0, PAIRS - 1) as v:
                lnc_load("L3b", v * 2 + 3, 1, v * 2 + 4)
                out_store(v * 2)
                lnc_load("L3b", v * 2 + 4, 0, v * 2 + 5)
                out_store(v * 2 + 1)
            for i in range(2 * (PAIRS - 1), NB):
                out_store(i)
            sp.wait_ge(S("stored"), 16 * NB)
        @block.gpsimd
        def _(pool):
            g = nc.gpsimd
            link = Chain(pool, S("pool_chain"))
            link(g.memset(ident[:, :], 0.0))
            g.affine_select(out=ident[:, :], in_=ident[:, :], compare_op=ALU.not_equal, fill=1.0, base=0,
                            pattern=[[-1, 128]], channel_multiplier=1).then_inc(S("pool_consts"), 1)
            link(g.memset(tri, 1.0))
            for i in range(SC):
                g.affine_select(out=tri[:, i, :], in_=tri[:, i, :], compare_op=ALU.is_ge, fill=1.0 + MARK,
                                base=-i * Q, pattern=[[1, W]], channel_multiplier=-1).then_inc(S("pool_consts"), 1)
            g.iota(trash_i[:, :], pattern=[[128, SC]], base=TRASH, channel_multiplier=1).then_inc(S("pool_consts"), 1)
            g.iota(node[:, :], pattern=[[1, NB]], base=0, channel_multiplier=NB,
                   allow_small_or_imprecise_dtypes=True).then_inc(S("pool_consts"), 1)

            def stage(t, s, k):
                pool.wait_ge(S("merged"), k)
                link.mark(g.tensor_copy(stage_k[:, s, :], key_u[:, bass.ds(t * SC, SC)]))
                link(g.tensor_copy(stage_v[:, s, :, :], val[:, bass.ds(t * SC, SC), :]))

            def scatter(s):
                pool.sem_inc(S("rounds_begun"), 1)
                for i in range(SC):
                    pool.indirect_dma_start(pairs, bass.IndirectOffsetOnAxis(ap=stage_k[:, s, i:i + 1], axis=0),
                                            stage_v[:, s, i, :], None, compute_op=ALU.add).then_inc(S("scattered"), 16)

            stage(0, 0, 1)
            pool.wait_ge(S("zeroed"), 16 * (NB + 1))
            for v in link.loop(NSC // 2 - 1, 4):
                scatter(0)
                stage(v * 2 + 1, 1, v + 1)
                pool.wait_ge(S("scattered"), (v * 2 + 1) * (16 * SC))
                scatter(1)
                stage(v * 2 + 2, 0, v + 2)
                pool.wait_ge(S("scattered"), (v * 2 + 2) * (16 * SC))
            scatter(0)
            stage(NSC - 1, 1, NSC // 2)
            pool.wait_ge(S("scattered"), (NSC - 1) * (16 * SC))
            scatter(1)

            pool.sem_inc(S("lnc_free"), CREDIT)

            def lnc_store(i, s, k):
                pool.wait_ge(S("lnc_read"), k + CREDIT)
                pool.dma_start(lnc_d[bass.ds(i, 1)].rearrange("o p c -> (o p) c"), lncW[s]).then_inc(S("lnc_out"), 16)
                pool.wait_ge(S("lnc_out"), k * 16)
                pool.sem_inc(S("lnc_free"), 1)

            with pool.Fori(0, PAIRS) as v:
                lnc_store(v * 2, 0, v * 2 + 1)
                lnc_store(v * 2 + 1, 1, v * 2 + 2)
            lnc_store(NB - 1, 0, NB)

        @block.tensor
        def _(pe):
            mm = nc.tensor.matmul

            def to_features(name, node_major, gate=None):
                for n, (k, j, nj) in enumerate(QG):
                    if gate is not None:
                        pe.wait_ge(S("ln_done"), gate * NB + min(NB, j + nj))
                    ring_wait(pe, name, n)
                    for m in range(nj):
                        last = nc.tensor.transpose(ps[:, n % 4, m * Q:(m + 1) * Q],
                                                   node_major[0:Q, j + m, k * 128:(k + 1) * 128], ident[0:Q, 0:Q])
                    last.then_inc(S("ring_pe"), 1)

            def feature_product(name, w, inp):
                n = 0
                for c in range(KT):
                    for n0, nn in NCH:
                        ring_wait(pe, name, n)
                        for k in range(KT):
                            last = mm(ps[:, n % 4, 0:nn], w[:, k, c * 128:(c + 1) * 128], inp[:, k, n0:n0 + nn],
                                      start=k == 0, stop=k == KT - 1)
                        last.then_inc(S("ring_pe"), 1)
                        n += 1

            def node_product(name, w, inp):
                for n, (j, nj) in enumerate(JP):
                    ring_wait(pe, name, n)
                    for m in range(nj):
                        for k in range(KT):
                            last = mm(ps[0:Q, n % 4, m * D:(m + 1) * D], inp[:, k, (j + m) * Q:(j + m + 1) * Q],
                                      w[:, k, :], start=k == 0, stop=k == KT - 1)
                    last.then_inc(S("ring_pe"), 1)

            def to_nodes(name, feat):
                for n, (j, nj) in enumerate(JP):
                    ring_wait(pe, name, n)
                    for m in range(nj):
                        for k in range(KT):
                            last = nc.tensor.transpose(ps[0:Q, n % 4, m * D + k * 128:m * D + (k + 1) * 128],
                                                       feat[:, k, (j + m) * Q:(j + m + 1) * Q], ident[:, :])
                    last.then_inc(S("ring_pe"), 1)

            pe.wait_ge(S("ones_made"), 1)

            def broadcast(s, k):
                pe.wait_ge(S("diag_made"), k)
                pe.wait_ge(S("keyrow_free"), k)
                pe.wait_ge(S("wrow_out"), k)
                mm(ps[0:Q, s, 0:W], ones[0:Q, 0:Q], dgk[s].rearrange("p i q -> p (i q)"), start=True, stop=True)
                mm(ps[0:Q, 2 + s, 0:W], ones[0:Q, 0:Q], dgw[s].rearrange("p i q -> p (i q)"), start=True, stop=True)\
                    .then_inc(S("rows_made"), 1)

            with pe.Fori(0, NSC // 2) as v:
                broadcast(0, v * 2 + 1)
                broadcast(1, v * 2 + 2)

            pe.wait_ge(S("keyrow_free"), NSC + CREDIT)
            pe.wait_ge(S("wrow_out"), NSC + CREDIT)
            pe.wait_ge(S("ln_done"), 1 * NB)
            for h, (j0, nj) in enumerate(HALF):
                if h:
                    pe.wait_ge(S("L0sum"), 1)
                pe.sem_inc(S(f"L0used{h}"), CREDIT)

                def half(i, s, k, first, last_):
                    pe.wait_ge(S(f"L0rows{h}_{s}"), k)
                    for j in range(nj):
                        ins = mm(ps[0:Q, j // 2, (j % 2) * D:(j % 2 + 1) * D], Rp[s][0:Q, j * Q:(j + 1) * Q, 0],
                                 H[0:Q, bass.ds(i, 1), :].rearrange("p o f -> p (o f)"),
                                 start=first and j % 2 == 0, stop=last_, skip_group_check=True)
                    ins.then_inc(S(f"L0used{h}"), 1)

                half(0, 0, 16, True, False)
                with pe.Fori(0, PAIRS - 1) as v:
                    half(v * 2 + 1, 1, (v + 1) * 16, False, False)
                    half(v * 2 + 2, 0, (v + 2) * 16, False, False)
                half(NB - 2, 1, PAIRS * 16, False, False)
                half(NB - 1, 0, (PAIRS + 1) * 16, False, True)

            pe.wait_ge(S("L0sum"), 2)
            to_features("z", Bn)
            pe.wait_ge(S("ring_ev"), base["z"] + len(QG))
            feature_product("y1", w01, F)
            pe.wait_ge(S("bn1_done"), 2)
            feature_product("y2", w02, G)
            pe.wait_ge(S("bn2_done"), 2)
            to_nodes("l0", F)

            def agg(name, rows, rhs, ready):
                pe.sem_inc(S(name + "tr"), CREDIT * NG)
                pe.sem_inc(S(name + "mm"), RING)

                def T(u, du, g, k):
                    if g == 0:
                        pe.wait_ge(S(ready(du)), k)
                    j, nj = GROUPS[g]
                    ring = (du * NG + g) % RING
                    for b in range(nj):
                        last = nc.tensor.transpose(ps[0:Q, ring, b * Q:(b + 1) * Q], rows(du, j + b), ident[0:Q, 0:Q])
                    last.then_inc(S(name + "tr"), 1)

                def M(u, du, g):
                    if g == 0:
                        pe.wait_ge(S(name + "out"), u + 1)
                    if g % 2 == 0:
                        pe.wait_ge(S(name + "evA"), u * NA + g // 2 + 1)
                    else:
                        pe.wait_ge(S(name + "evD"), u * ND + g // 2 + 1)
                    j, nj = GROUPS[g]
                    ring = (du * NG + g) % RING
                    for b in range(nj):
                        last = mm(acc[du % 2], PT[0:Q, ring, b * Q:(b + 1) * Q], rhs[0:Q, j + b, :],
                                  start=j + b == 0, stop=j + b == NB - 1)
                    last.then_inc(S(name + "mm"), 1)

                def unit(u, du, key, last=False, between=None):
                    for g in range(NG):
                        n = g + AHEAD
                        if n < NG:
                            T(u, du, n, None)
                        elif not last:
                            T(u + 1, (du + 1) % 4, n - NG, key(u + 1, du + 1))
                        M(u, du, g)
                        if between:
                            between(g)

                for g in range(AHEAD):
                    T(0, 0, g, key_first[name])
                return unit

            key_first = {"L1a": 16, "L1b": 16, "L2": 16, "L3a": 1, "L3b": 1}

            def whole(name, plane, rhs):
                unit = agg(name, lambda du, j: Rp[du % 2][0:Q, j * Q:(j + 1) * Q, plane], rhs,
                           lambda du: f"{name}rows{du % 2}")
                with pe.Fori(0, NB // 4) as v:
                    for du in range(4):
                        unit(v * 4 + du, du, lambda u, d: (v * 2 + d // 2 + 1) * 16)
                unit(NB - 1, 0, None, True)

            to_features("h1", H, 1)
            pe.wait_ge(S("pick_made"), 1)

            def root(name, t):
                for k in range(KT):
                    for j in range(NB):
                        last = mm(ps[:, 6, k:k + 1], t[0:Q, j, k * 128:(k + 1) * 128], pick[0:Q, j:j + 1],
                                  start=j == 0, stop=j == NB - 1)
                last.then_inc(S(name), 1)

            root("root1", H)
            pe.wait_ge(S("ring_ev"), base["h1"] + len(QG))
            node_product("t1", w11, F)
            pe.wait_ge(S("ring_ev"), base["t1"] + len(JP))
            whole("L1a", 0, Bn)
            pe.wait_ge(S("rootb1"), 1)
            for k in range(KT):
                last = mm(ps[0:Q, 7, 0:D], rootb[:, k, :], w12[:, KT + k, :], start=k == 0, stop=k == KT - 1)
            last.then_inc(S("rootr1"), 1)
            pe.wait_ge(S("L1aout"), NB + CREDIT)
            root("root2", H)
            pe.wait_ge(S("f2_leaky"), 1)
            to_features("h2", H)
            pe.wait_ge(S("ring_ev"), base["h2"] + len(QG))
            node_product("t2", w12, F)
            pe.wait_ge(S("ring_ev"), base["t2"] + len(JP))
            whole("L1b", 0, Bn)
            pe.wait_ge(S("rootb2"), 1)
            for k in range(KT):
                last = mm(ps[0:Q, 7, 0:D], rootb[:, k, :], wl1[:, KT + k, :], start=k == 0, stop=k == KT - 1)
            last.then_inc(S("rootr2"), 1)
            pe.wait_ge(S("f3_leaky"), 1)
            to_features("h3", H)
            pe.wait_ge(S("ring_ev"), base["h3"] + len(QG))
            node_product("t3", wl1, F)
            pe.wait_ge(S("rootr_used"), 2)
            for ko in range(KT):
                for ki in range(KT):
                    last = nc.tensor.transpose(ps[:, 7, ki * D + ko * 128:ki * D + (ko + 1) * 128],
                                               w2[:, ko, ki * 128:(ki + 1) * 128], ident[:, :])
            last.then_inc(S("w2T_pe"), 1)

            pe.wait_ge(S("ring_ev"), base["t3"] + len(JP))
            to_features("h4", H, 2)
            pe.wait_ge(S("ring_ev"), base["h4"] + len(QG))
            pe.wait_ge(S("w2T_made"), 1)
            node_product("t4", w2T, F)
            pe.wait_ge(S("ring_ev"), base["t4"] + len(JP))
            whole("L2", 1, Bn)

            pe.wait_ge(S("L2out"), NB + CREDIT)
            to_features("h5", H, 3)
            pe.wait_ge(S("ring_ev"), base["h5"] + len(QG))
            pe.wait_ge(S("va_made"), 1)
            for n, (n0, nn) in enumerate(NCH):
                ring_wait(pe, "alsrow", n)
                for k in range(KT):
                    last = mm(ps[0:2 * HEADS, n % 4, 0:nn], va[:, k, :], F[:, k, n0:n0 + nn],
                              start=k == 0, stop=k == KT - 1)
                last.then_inc(S("ring_pe"), 1)
            for j in range(NB):
                for k in range(KT):
                    last = mm(ps[0:Q, 6, j * HEADS:(j + 1) * HEADS], F[:, k, j * Q:(j + 1) * Q],
                              va[:, k, HEADS:2 * HEADS], start=k == 0, stop=k == KT - 1)
            last.then_inc(S("ald_mm"), 1)
            pe.wait_ge(S("ring_ev"), base["alsrow"] + len(NCH))
            pe.wait_ge(S("ald_made"), 1)

            def wide_T(s, k):
                pe.wait_ge(S("L3aout"), k)
                for t in range(KT):
                    last = nc.tensor.transpose(ps[:, 6, t * Q:(t + 1) * Q], ag[0:Q, s, t * 128:(t + 1) * 128],
                                               ident[0:Q, 0:Q])
                last.then_inc(S("agT_pe"), 1)

            def wide_M(hd, k):
                pe.wait_ge(S("agT_made"), k)
                for c in range(KT):
                    for t in range(KT):
                        last = mm(ps[:, 7, c * Q:(c + 1) * Q], w31[:, t, hd * D + c * 128:hd * D + (c + 1) * 128],
                                  agT[:, t, :], start=t == 0, stop=t == KT - 1)
                last.then_inc(S("y_pe"), 1)

            unit = agg("L3a", lambda du, j: scr[0][du][0:Q, j * Q:(j + 1) * Q], H, lambda du: "L3aprob")

            def wide_unit(u, du, last=False):
                def between(g):
                    if g == 3:
                        wide_T((du - 1) % 2, u + CREDIT)
                    if g == 6:
                        wide_M((du - 1) % 4, u)
                unit(u, du, lambda w, d: w + 1, last, between)

            unit(0, 0, lambda w, d: w + 1)
            with pe.Fori(0, NB - 1) as v:
                for k in range(1, 5):
                    wide_unit(v * 4 + k, k % 4)
            for u in range(4 * (NB - 1) + 1, 4 * NB):
                wide_unit(u, u % 4, u == 4 * NB - 1)
            wide_T(1, 4 * NB + CREDIT)
            wide_M(3, 4 * NB)

            pe.wait_ge(S("y_made"), NB)
            pe.wait_ge(S("L3aout"), 4 * NB + CREDIT)
            pe.wait_ge(S("v2_made"), 1)
            n = 0
            for c, (n0, nn) in enumerate(NCH):
                pe.wait_ge(S("wide_norm"), CT * (c + 1))
                slot = R[:, (c % 2) * 4096:(c % 2) * 4096 + CT * nn].rearrange("p (t n) -> p t n", t=CT)
                for b in range(nn // Q):
                    ring_wait(pe, "z3", n)
                    for t in range(CT):
                        last = mm(ps[0:Q, n % 4, 0:D + 2], slot[:, t, b * Q:(b + 1) * Q], w32[:, t, :],
                                  start=t == 0, stop=t == CT - 1)
                    last.then_inc(S("ring_pe"), 1)
                    n += 1
                if c >= 2:
                    pe.wait_ge(S("row2_ev"), c - 1)
                for t in range(CT):
                    last = mm(ps[0:2, 4 + c % 2, 0:nn], w32[:, t, D:D + 2], slot[:, t, :],
                              start=t == 0, stop=t == CT - 1)
                last.then_inc(S("wide_used"), 1)
            pe.wait_ge(S("ring_ev"), base["z3"] + NB)
            pe.wait_ge(S("row2_ev"), len(NCH))
            unit = agg("L3b", lambda du, j: scr[1][du][0:Q, j * Q:(j + 1) * Q], Bn, lambda du: "L3bprob")
            with pe.Fori(0, NB // 4) as v:
                for du in range(4):
                    unit(v * 4 + du, du, lambda w, d: w + 1)
            unit(NB - 1, 0, None, True)

        @block.scalar
        def _(act):
            a = nc.scalar.activation
            link = Chain(act, S("act_chain"))

            act.wait_ge(S("pool_consts"), 1)
            act.wait_ge(S("key_made"), 1)
            act.sem_inc(S("wrow_out"), CREDIT)

            def diag(t, s, k):
                act.wait_ge(S("rows_made"), k)
                for i in range(SC):
                    a(dgk[s][:, i, :], ident[0:Q, 0:Q], ACT.Copy, scale=key[:, bass.ds(t * SC + i, 1)])
                    last = a(dgw[s][:, i, :], ident[0:Q, 0:Q], ACT.Copy, scale=wgt[:, bass.ds(t * SC + i, 1)])
                last.then_inc(S("diag_made"), 1)

            def wrow_out(s, k):
                act.wait_ge(S("rows_made"), k + 2)
                act.wait_ge(S("keyrow_free"), k)
                a(wrow[s], ps[0:Q, 2 + s, 0:W], ACT.Copy).then_inc(S("wrow_out"), 1)

            act.sem_inc(S("rows_made"), 2)
            diag(0, 0, 1)
            with act.Fori(0, NSC // 2 - 1) as v:
                diag(v * 2 + 1, 1, v * 2 + 2)
                wrow_out(0, v * 2 + 1)
                diag(v * 2 + 2, 0, v * 2 + 3)
                wrow_out(1, v * 2 + 2)
            diag(NSC - 1, 1, NSC)
            wrow_out(0, NSC - 1)
            wrow_out(1, NSC)

            def evac(name, u, du, g):
                ring = (du * NG + g) % RING
                w = GROUPS[g][1] * Q
                act.wait_ge(S(name + "tr"), u * NG + (g + 1 + CREDIT * NG))
                act.wait_ge(S(name + "mm"), u * NG + (g + 1))
                a(PT[0:Q, ring, 0:w], ps[0:Q, ring, 0:w], ACT.Copy).then_inc(S(name + "evA"), 1)

            def evac_pass(name, beside=None):
                def unit(u, du, v=0):
                    for g in range(0, NG, 2):
                        evac(name, u, du, g)
                        if beside:
                            beside(g, u, du, v)
                with act.Fori(0, NB // 4) as v:
                    for du in range(4):
                        unit(v * 4 + du, du, v)
                unit(NB - 1, 0, NB // 4)

            def normalise(l):
                act.wait_ge(S("ln_var"), l + 1)
                a(lns[0:Q, 4, :], lns[0:Q, 3, :], ACT.Sqrt).then_inc(S("ln_std"), 1)
                act.wait_ge(S("ln_aff"), l + 1)
                with act.Fori(0, NB) as j:
                    a(H[0:Q, bass.ds(j, 1), :].rearrange("p o f -> p (o f)"),
                      X[0:Q, bass.ds(j, 1), :].rearrange("p o f -> p (o f)"), ACT.Relu,
                      scale=lns[0:Q, 4, bass.ds(j, 1)], bias=lns[0:Q, 5, bass.ds(j, 1)]).then_inc(S("ln_done"), 1)

            normalise(0)

            def batch_norm(y, bn, buf, bias):
                n = 0
                for c in range(KT):
                    for n0, nn in NCH:
                        act.wait_ge(S("ring_pe"), base[y] + n + 1)
                        a(buf[:, c, n0:n0 + nn], ps[:, n % 4, 0:nn], ACT.Identity, bias=cols[:, bias, c:c + 1])\
                            .then_inc(S("ring_ev"), 1)
                        n += 1
                act.wait_ge(S(bn + "_var"), 1)
                a(aff[:, 1, 0:KT], aff[:, 0, 0:KT], ACT.Sqrt).then_inc(S(bn + "_std"), 1)
                act.wait_ge(S(bn + "_aff"), 1)
                for c in range(KT):
                    a(buf[:, c, :], buf[:, c, :], ACT.Relu, scale=aff[:, 2, c:c + 1], bias=aff[:, 3, c:c + 1])\
                        .then_inc(S(bn + "_done"), 1)

            batch_norm("y1", "bn1", G, 0)
            batch_norm("y2", "bn2", F, 3)
            normalise(1)

            def counts(g, u, du, v):
                s = du % 2
                if g == 0:
                    act.wait_ge(S(f"L1arows{s}"), (v * 2 + du // 2 + 1) * 16)
                    a(Rp[s][0:Q, :, 1], Rp[s][0:Q, :, 1], ACT.Copy, accum_out=norm[0:Q, bass.ds(u, 1)])\
                        .then_inc(S("deg_made"), 1)
                if g == 4:
                    act.wait_ge(S("self_added"), u + 1)
                    a(Rp[s][:, :, 1], Rp[s][:, :, 1], ACT.Ln, bias=small[:, 1:2]).then_inc(S("ln_made"), 1)

            act.wait_ge(S("small_made"), 1)
            evac_pass("L1a", counts)
            evac_pass("L1b")
            act.wait_ge(S("deg_max"), 1)
            a(norm[0:Q, :], norm[0:Q, :], ACT.Sqrt).then_inc(S("deg_std"), 1)

            normalise(2)
            evac_pass("L2")
            normalise(3)

            def expo(name, slots, u, du):
                act.wait_ge(S(name + "max"), u + 1)
                a(slots[du][0:Q, :], slots[du][0:Q, :], ACT.Exp, bias=mx[0:Q, 1, du:du + 1],
                  accum_out=mx[0:Q, 2, du:du + 1]).then_inc(S(name + "prob"), 1)

            def attend(name, slots, row, col, units, rounds):
                def sc(u, du):
                    if isinstance(u, int) and u < 4:
                        a(slots[du][0:Q, :], row(u, du)[0:Q, :], ACT.Identity, bias=col(u, du))\
                            .then_inc(S(name + "score"), 1)
                    else:
                        act.wait_ge(S(name + "tr"), u * NG + (CREDIT - 3) * NG)
                        a(slots[du][0:Q, :], row(u, du)[0:Q, :], ACT.Identity, bias=col(u, du))\
                            .then_inc(S(name + "score"), 1)

                def step(t, dt):
                    for g in range(0, NG, 2):
                        evac(name, t, dt, g)
                        if g == 0 and not (isinstance(t, int) and t + 1 >= units):
                            expo(name, slots, t + 1, (dt + 1) % 4)
                        if g == 2 and not (isinstance(t, int) and t + 3 >= units):
                            sc(t + 3, (dt + 3) % 4)

                for u in range(3):
                    sc(u, u)
                expo(name, slots, 0, 0)
                step(0, 0)
                with act.Fori(0, rounds) as v:
                    for k in range(1, 5):
                        step(v * 4 + k, k % 4)
                for t in range(4 * rounds + 1, units):
                    step(t, t % 4)

            def ald3(u, h):
                flat = ald[0:Q, :, :].rearrange("p j h -> p (j h)")
                return flat[:, bass.ds(u, 1)]

            act.wait_ge(S("als_in"), 16 * HEADS)
            act.wait_ge(S("ald_made"), 1)
            act.wait_ge(S("x_out"), 16)
            attend("L3a", scr[0], lambda u, du: als[du], lambda u, du: ald3(u, du), 4 * NB, NB - 1)

            act.wait_ge(S("gn_var"), 1)
            a(aff[:, 1, :], aff[:, 0, :], ACT.Sqrt).then_inc(S("gn_std"), 1)
            act.wait_ge(S("gn_aff"), 1)
            for c, (n0, nn) in enumerate(NCH):
                act.wait_ge(S(f"wide_in{c % 2}"), 16 * (c // 2 + 1))
                slot = R[:, (c % 2) * 4096:(c % 2) * 4096 + CT * nn].rearrange("p (t n) -> p t n", t=CT)
                for t in range(CT):
                    a(slot[:, t, :], slot[:, t, :], ACT.Relu, scale=aff[:, 2, t:t + 1], bias=aff[:, 3, t:t + 1])\
                        .then_inc(S("wide_norm"), 1)

            act.wait_ge(S("als2_in"), 16)
            act.wait_ge(S("ring_ev"), base["z3"] + NB)

            attend("L3b", scr[1], lambda u, du: als[2], lambda u, du: ald[0:Q, bass.ds(u, 1), 0], NB, NB // 4 - 1)

        @block.vector
        def _(dve):
            v_ = nc.vector
            tt, ts, stt, cp = v_.tensor_tensor, v_.tensor_scalar, v_.scalar_tensor_tensor, v_.tensor_copy
            link = Chain(dve, S("dve_chain"))

            v_.memset(R[:, 0:2 * N], 0.0).then_inc(S("zero_made"), 1)
            v_.memset(ones[:, :], 1.0).then_inc(S("ones_made"), 1)
            link.mark(v_.memset(val, 0.0))
            v_.memset(small[:, 1:2], TINY).then_inc(S("small_made"), 1)

            dve.wait_ge(S("edges_in"), 48)

            def block_of(out_, in_i, tmp):
                link(cp(out_, in_i))
                link(ts(tmp, out_, 1.0 / NB, 0.5 / NB - 0.5, ALU.mult, ALU.add))
                link(ts(tmp, tmp, ROUND, None, ALU.add))
                link(ts(tmp, tmp, ROUND, None, ALU.subtract))

            block_of(e1, dst_i, e2)
            link(ts(e1, e1, 128.0, None, ALU.mult))
            link(stt(e1, e2, -(128.0 * NB - 1.0), e1, ALU.mult, ALU.add))
            link(ts(key, e1, float(N), None, ALU.mult))
            block_of(e1, src_i, e2)
            link(stt(key, e1, float(Q), key, ALU.mult, ALU.add))
            stt(key, e2, -(float(Q) * NB - 1.0), key, ALU.mult, ALU.add).then_inc(S("key_made"), 1)
            dve.wait_ge(S("pool_consts"), 3 + SC)
            dve.wait_ge(S("key_made"), 1)
            link(cp(trash[:, :], trash_i[:, :]))
            link(cp(key_u.rearrange("p (t i) -> p t i", i=SC), trash[:, :].unsqueeze(1).to_broadcast([128, NSC, SC])))
            trashb = trash[0:Q, :].unsqueeze(1).to_broadcast([Q, 2, SC])

            dve.sem_inc(S("keyrow_free"), CREDIT)

            def merge(t, s, k):
                dve.wait_ge(S("wrow_out"), k)
                for i in range(SC):
                    c = t * SC + i
                    link.join(1)
                    link.mark(stt(junk[0], ps[0:Q, s, 0:W], key[:, bass.ds(c, 1)], wrow[s], ALU.is_equal, ALU.mult,
                                  accum_out=val[0:Q, bass.ds(c, 1), 0]))
                    link.join(1)
                    link.mark(stt(junk[1], ps[0:Q, s, 0:W], key[:, bass.ds(c, 1)], tri[:, i, :], ALU.is_equal,
                                  ALU.mult, accum_out=val[0:Q, bass.ds(c, 1), 1]))
                link.join()
                dve.sem_inc(S("keyrow_free"), 1)

            for v in link.loop(NSC // 2, 3 + 4 * SC):
                merge(v * 2, 0, v * 2 + 1 + CREDIT)
                merge(v * 2 + 1, 1, v * 2 + 2 + CREDIT)
                kk = key[:, bass.ds(v * (2 * SC), 2 * SC)].rearrange("p (a i) -> p a i", i=SC)
                f8 = small[0:Q, 8:8 + 2 * SC].rearrange("p (a i) -> p a i", i=SC)
                d8 = small[0:Q, 16:16 + 2 * SC].rearrange("p (a i) -> p a i", i=SC)
                link.mark(ts(f8, val[0:Q, bass.ds(v * (2 * SC), 2 * SC), 1].rearrange("p (a i) -> p a i", i=SC),
                             MARK, None, ALU.is_lt))
                link(tt(d8, kk, trashb, ALU.subtract))
                link(tt(d8, d8, f8, ALU.mult))
                tt(key_u[0:Q, bass.ds(v * (2 * SC), 2 * SC)].rearrange("p (a i) -> p a i", i=SC), d8, trashb,
                   ALU.add).then_inc(S("merged"), 1)

            dve.wait_ge(S("w_in"), 16 * 29)
            for k in range(KT):
                for w in range(2):
                    for h in range(HEADS):
                        link(stt(att_junk, w31[:, k, h * D:(h + 1) * D], 1.0, att1[w][:, h * D:(h + 1) * D],
                                 ALU.mult, ALU.mult, accum_out=va[:, k, w * HEADS + h:w * HEADS + h + 1]))
            dve.sem_inc(S("va_made"), 1)
            for k in range(CT):
                for w in range(2):
                    link(stt(att_junk, w32[:, k, 0:D], 1.0, att2[w], ALU.mult, ALU.mult,
                             accum_out=w32[:, k, D + w:D + w + 1]))
            dve.sem_inc(S("v2_made"), 1)
            link(cp(small[:, 4:5], idx_i[:, 0:1]))
            ts(pick[:, :], node[:, :], small[:, 4:5], None, ALU.is_equal).then_inc(S("pick_made"), 1)
            link(ts(small[:, 5:6], small[:, 0:1], 1.0, None, ALU.add))

            def ln_stats(l):
                L = [lns[0:Q, k, :] for k in range(6)]
                with dve.Fori(0, NB) as j:
                    v_.bn_stats(st[0:Q, bass.ds(j, 1), :].rearrange("p o s -> p (o s)"),
                                X[0:Q, bass.ds(j, 1), :].rearrange("p o f -> p (o f)")).then_inc(S("ln_st"), 1)
                dve.wait_ge(S("ln_st"), (l + 1) * NB)
                link.mark(tt(L[0], st[0:Q, :, 1], st[0:Q, :, 4], ALU.add))
                link.mark(tt(L[1], st[0:Q, :, 1], st[0:Q, :, 4], ALU.subtract))
                link(tt(L[2], st[0:Q, :, 2], st[0:Q, :, 5], ALU.add))
                link.mark(ts(L[0], L[0], 0.5, None, ALU.mult))
                link.mark(tt(L[1], L[1], L[1], ALU.mult))
                link(ts(L[2], L[2], 1.0 / D, LN_EPS, ALU.mult, ALU.add))
                stt(L[3], L[1], 0.25, L[2], ALU.mult, ALU.add).then_inc(S("ln_var"), 1)
                dve.wait_ge(S("ln_std"), l + 1)
                link(v_.reciprocal(L[4], L[4]))
                stt(L[5], L[0], -1.0, L[4], ALU.mult, ALU.mult).then_inc(S("ln_aff"), 1)

            dve.wait_ge(S("x_in"), 16)
            ln_stats(0)

            dve.wait_ge(S("ln_done"), 1 * NB)
            for h, (j0, nj) in enumerate(HALF):
                dve.wait_ge(S(f"L0used{h}"), NB + CREDIT)
                stt(Bn[0:Q, j0:j0 + nj, :].rearrange("p j f -> p (j f)"),
                    H[0:Q, j0:j0 + nj, :].rearrange("p j f -> p (j f)"), small[0:Q, 5:6], psflat[0:Q, 0:nj * D],
                    ALU.mult, ALU.add).then_inc(S("L0sum"), 1)

            def evac_features(name):
                for n, (k, j, nj) in enumerate(QG):
                    dve.wait_ge(S("ring_pe"), base[name] + n + 1)
                    cp(F[:, k, j * Q:(j + nj) * Q], ps[:, n % 4, 0:nj * Q]).then_inc(S("ring_ev"), 1)

            evac_features("z")

            def bn_stats(y, bn, buf, g_, be):
                n = 0
                for c in range(KT):
                    for m, (n0, nn) in enumerate(NCH):
                        dve.wait_ge(S("ring_ev"), base[y] + n + 1)
                        link.mark(v_.bn_stats(bst[:, c, m, :], buf[:, c, n0:n0 + nn]))
                        n += 1
                link.join()
                for c in range(KT):
                    link.mark(v_.bn_aggr(mv[:, c, :], bst[:, c, :, :].rearrange("p m s -> p (m s)")))
                link.join()
                ts(aff[:, 0, 0:KT], mv[:, 0:KT, 1], BN_EPS, None, ALU.add).then_inc(S(bn + "_var"), 1)
                dve.wait_ge(S(bn + "_std"), 1)
                link(v_.reciprocal(aff[:, 1, 0:KT], aff[:, 1, 0:KT]))
                link(tt(aff[:, 2, 0:KT], aff[:, 1, 0:KT], cols[:, g_, :], ALU.mult))
                link(tt(aff[:, 4, 0:KT], aff[:, 2, 0:KT], mv[:, 0:KT, 0], ALU.mult))
                tt(aff[:, 3, 0:KT], cols[:, be, :], aff[:, 4, 0:KT], ALU.subtract).then_inc(S(bn + "_aff"), 1)

            bn_stats("y1", "bn1", G, 1, 2)
            dve.wait_ge(S("bn1_done"), 2)
            bn_stats("y2", "bn2", F, 4, 5)
            for n, (j, nj) in enumerate(JP):
                dve.wait_ge(S("ring_pe"), base["l0"] + n + 1)
                xx = X[0:Q, j:j + nj, :].rearrange("p j f -> p (j f)")
                tt(xx, xx, ps[0:Q, n % 4, 0:nj * D], ALU.add).then_inc(S("ring_ev"), 1)
            dve.wait_ge(S("ring_ev"), base["l0"] + len(JP))

            ln_stats(1)
            evac_features("h1")
            dve.sem_inc(S("r_free_L1a"), 1)

            def root_column(name, bname, leaky):
                dve.wait_ge(S(name), 1)
                if leaky:
                    link(ts(small[:, 26:28], ps[:, 6, 0:KT], 0.01, None, ALU.mult))
                    link(tt(rootc[:, :], small[:, 26:28], ps[:, 6, 0:KT], ALU.max))
                else:
                    link(cp(rootc[:, :], ps[:, 6, 0:KT]))
                for k in range(KT):
                    link.mark(ts(rootb[:, k, :], ones[:, 0:Q], rootc[:, k:k + 1], None, ALU.mult))
                link.join()
                dve.sem_inc(S(bname), 1)

            root_column("root1", "rootb1", True)
            for n, (j, nj) in enumerate(JP):
                dve.wait_ge(S("ring_pe"), base["t1"] + n + 1)
                cp(Bn[0:Q, j:j + nj, :].rearrange("p j f -> p (j f)"), ps[0:Q, n % 4, 0:nj * D]).then_inc(S("ring_ev"), 1)

            def evac(name, u, du, g):
                ring = (du * NG + g) % RING
                w = GROUPS[g][1] * Q
                dve.wait_ge(S(name + "tr"), u * NG + (g + 1 + CREDIT * NG))
                dve.wait_ge(S(name + "mm"), u * NG + (g + 1))
                cp(PT[0:Q, ring, 0:w], ps[0:Q, ring, 0:w]).then_inc(S(name + "evD"), 1)

            def plain_pass(name, out_unit, beside=None):
                dve.sem_inc(S(name + "out"), CREDIT)

                def unit(u, du, v, first=False):
                    for g in range(1, NG, 2):
                        evac(name, u, du, g)
                        if g == 1 and not first:
                            dve.wait_ge(S(name + "mm"), u * NG + RING)
                            out_unit(u - 1, 1 - du % 2)
                        if beside:
                            beside(g, u, du, v)

                unit(0, 0, 0, True)
                with dve.Fori(0, NB // 4) as v:
                    for k in range(1, 5):
                        unit(v * 4 + k, k % 4, v)
                dve.wait_ge(S(name + "mm"), NB * NG + RING)
                out_unit(NB - 1, 0)

            def out_bias(bias, name):
                def f(i, s):
                    tt(H[0:Q, bass.ds(i, 1), :].rearrange("p o f -> p (o f)"), acc[s], bcs[0:Q, bias, :], ALU.add)\
                        .then_inc(S(name + "out"), 1)
                return f

            dve.sem_inc(S("lnc_read"), CREDIT)

            def counts(g, u, du, v):
                s = du % 2
                if g == 1:
                    dve.wait_ge(S("deg_made"), u + 1)
                    dg = Rp[s][0:Q, bass.ds(u * Q, Q), 1]
                    tt(dg, dg, ident[0:Q, 0:Q], ALU.add).then_inc(S("diag_in"), 1)
                    dve.wait_ge(S("lnc_free"), u + 1)
                    dve.wait_ge(S("diag_in"), u + 1)
                    ts(lncW[s], Rp[s][:, :, 1], 0.5, NEG, ALU.is_lt, ALU.mult).then_inc(S("self_added"), 1)
                if g == 5:
                    dve.wait_ge(S("ln_made"), u + 1)
                    tt(lncW[s], lncW[s], Rp[s][:, :, 1], ALU.add).then_inc(S("lnc_read"), 1)

            dve.wait_ge(S("ring_ev"), base["t1"] + len(JP))
            plain_pass("L1a", out_bias(0, "L1a"), counts)

            dve.wait_ge(S("deg_made"), NB)
            ts(norm[0:Q, :], norm[0:Q, :], 1.0, None, ALU.max).then_inc(S("deg_max"), 1)
            dve.wait_ge(S("lnc_read"), NB + CREDIT)
            dve.sem_inc(S("L1a_done"), 1)
            dve.wait_ge(S("rootr1"), 1)
            cp(rootr[0:Q, :], ps[0:Q, 7, 0:D]).then_inc(S("rootr_used"), 1)
            dve.wait_ge(S("L1aout"), NB + CREDIT)
            root_column("root2", "rootb2", False)
            hh = H[0:Q, :, :].rearrange("p j f -> p (j f)")
            stt(hh, hh, 0.01, hh, ALU.mult, ALU.max).then_inc(S("f2_leaky"), 1)
            dve.wait_ge(S("lnc_free"), NB + CREDIT)
            evac_features("h2")
            rb2 = rootr[0:Q, :].unsqueeze(1)
            dve.wait_ge(S("rootr_used"), 1)
            for n, (j, nj) in enumerate(JP):
                dve.wait_ge(S("ring_pe"), base["t2"] + n + 1)
                tt(Bn[0:Q, j:j + nj, :], ps[0:Q, n % 4, 0:nj * D].rearrange("p (j f) -> p j f", f=D),
                   rb2.to_broadcast([Q, nj, D]), ALU.add).then_inc(S("ring_ev"), 1)
            plain_pass("L1b", out_bias(1, "L1b"))
            dve.wait_ge(S("ring_ev"), base["t2"] + len(JP))
            dve.sem_inc(S("L1b_done"), 1)
            dve.wait_ge(S("rootr2"), 1)
            tt(rootr[0:Q, :], ps[0:Q, 7, 0:D], bcs[0:Q, 2, :], ALU.add).then_inc(S("rootr_used"), 1)
            dve.wait_ge(S("L1bout"), NB + CREDIT)
            stt(hh, hh, 0.01, hh, ALU.mult, ALU.max).then_inc(S("f3_leaky"), 1)
            evac_features("h3")
            dve.wait_ge(S("rootr_used"), 2)
            for n, (j, nj) in enumerate(JP):
                dve.wait_ge(S("ring_pe"), base["t3"] + n + 1)
                bb = Bn[0:Q, j:j + nj, :]
                tt(bb, ps[0:Q, n % 4, 0:nj * D].rearrange("p (j f) -> p j f", f=D),
                   rb2.to_broadcast([Q, nj, D]), ALU.add).then_inc(S("ring_ev"), 1)
            dve.wait_ge(S("ring_ev"), base["t3"] + len(JP))
            bb = B[0:Q, 0:NB * D]
            xx = X[0:Q, :, :].rearrange("p j f -> p (j f)")
            link(stt(bb, bb, 0.01, bb, ALU.mult, ALU.max))
            link(tt(xx, xx, bb, ALU.add))
            dve.wait_ge(S("w2T_pe"), 1)
            cp(w2T[:, :, :].rearrange("p k n -> p (k n)"), ps[:, 7, :]).then_inc(S("w2T_made"), 1)

            ln_stats(2)
            evac_features("h4")
            dve.wait_ge(S("deg_std"), 1)
            link(v_.reciprocal(norm[0:Q, :], norm[0:Q, :]))
            for n, (j, nj) in enumerate(JP):
                dve.wait_ge(S("ring_pe"), base["t4"] + n + 1)
                bb = Bn[0:Q, j:j + nj, :]
                link(tt(bb, ps[0:Q, n % 4, 0:nj * D].rearrange("p (j f) -> p j f", f=D),
                        bcs[0:Q, 3, :].unsqueeze(1).to_broadcast([Q, nj, D]), ALU.add))
                tt(bb, bb, norm[0:Q, j:j + nj].unsqueeze(2).to_broadcast([Q, nj, D]), ALU.mult)\
                    .then_inc(S("ring_ev"), 1)

            def out_residual(name, col):
                def f(i, s):
                    xi = X[0:Q, bass.ds(i, 1), :].rearrange("p o f -> p (o f)")
                    stt(xi, acc[s], col(i, s), xi, ALU.mult, ALU.add).then_inc(S(name + "out"), 1)
                return f

            plain_pass("L2", out_residual("L2", lambda i, s: norm[0:Q, bass.ds(i, 1)]))
            dve.wait_ge(S("L2out"), NB + CREDIT)

            ln_stats(3)
            evac_features("h5")
            for n, (n0, nn) in enumerate(NCH):
                dve.wait_ge(S("ring_pe"), base["alsrow"] + n + 1)
                cp(R[0:2 * HEADS, n0:n0 + nn], ps[0:2 * HEADS, n % 4, 0:nn]).then_inc(S("ring_ev"), 1)
            dve.wait_ge(S("ring_ev"), base["alsrow"] + len(NCH))
            dve.sem_inc(S("alsrow_made"), 1)
            dve.wait_ge(S("ald_mm"), 1)
            cp(ald[0:Q, :, :].rearrange("p j h -> p (j h)"), ps[0:Q, 6, 0:NB * HEADS]).then_inc(S("ald_made"), 1)
            tt(X[0:Q, :, :], X[0:Q, :, :], bcs[0:Q, 4, :].unsqueeze(1).to_broadcast([Q, NB, D]), ALU.add)\
                .then_inc(S("bias_in_x"), 1)
            dve.sem_inc(S("L3alnc_used"), CREDIT)

            def leaky(name, t, u, du):
                dve.wait_ge(S(name + "score"), u + 1)
                link(stt(t[0:Q, :], t[0:Q, :], 0.2, t[0:Q, :], ALU.mult, ALU.max))

            def mask(name, t, du, rs, klnc, last_use):
                if klnc is not None:
                    dve.wait_ge(S(f"{name}lnc{rs}"), klnc)
                dve.sem_inc(S("masks_begun"), 1)
                link(v_.tensor_tensor_reduce(t[0:Q, :], t[0:Q, :], lncR[rs][0:Q, :], 1.0, 2.0 * NEG,
                                             ALU.add, ALU.max, accum_out=mx[0:Q, 0, du:du + 1]))
                ts(mx[0:Q, 1, du:du + 1], mx[0:Q, 0, du:du + 1], -1.0, None, ALU.mult).then_inc(S(name + "max"), 1)
                if last_use:
                    dve.sem_inc(S(name + "lnc_used"), 1)

            def inverse(u, du):
                link(v_.reciprocal(mx[0:Q, 3, du:du + 1], mx[0:Q, 2, du:du + 1]))

            def attention_out(u, du):
                inverse(u, du)
                dve.wait_ge(S("L3amm"), u * NG + (NG + RING))
                ts(ag[0:Q, du % 2, :], acc[du % 2], mx[0:Q, 3, du:du + 1], None, ALU.mult).then_inc(S("L3aout"), 1)

            def wide_in(u):
                dve.wait_ge(S("agT_pe"), u + 1)
                cp(agT[:, :, :].rearrange("p t q -> p (t q)"), ps[:, 6, 0:KT * Q]).then_inc(S("agT_made"), 1)

            def wide_out(u, hd, ys, i):
                if hd == 0:
                    dve.wait_ge(S("y_free"), i + 1)
                dve.wait_ge(S("y_pe"), u + 1)
                for c in range(KT):
                    t = hd * KT + c
                    link.mark(ts(yT[:, ys, t, :], ps[:, 7, c * Q:(c + 1) * Q], colw[:, 0, t:t + 1], None, ALU.add))
                link.join()
                if hd == HEADS - 1:
                    for t in range(CT):
                        last = v_.bn_stats(gst[:, t, bass.ds(i * 6, 6)], yT[:, ys, t, :])
                    last.then_inc(S("y_made"), 1)

            U = 4 * NB

            def step(t, dt8, i8, v):
                def unit(d):
                    return t + d, (dt8 + d) % 4
                done = dt8 == 0 and isinstance(t, int) and t == 0
                ahead = not (isinstance(t, int) and t + 2 >= U)
                u2, d2 = unit(2)
                blk = (dt8 + 2) // 4
                evac("L3a", t, dt8 % 4, 1)
                if ahead:
                    leaky("L3a", scr[0][d2], u2, d2)
                if not done:
                    attention_out(*unit(-1))
                evac("L3a", t, dt8 % 4, 3)
                if ahead:
                    mask("L3a", scr[0][d2], d2, blk % 2, (v + blk // 2 + 1) * 16 if d2 == 0 else None, d2 == 3)
                if not done:
                    wide_in(t - 1)
                evac("L3a", t, dt8 % 4, 5)
                if not done:
                    b1 = (dt8 - 1) // 4
                    wide_out(t - 1, (dt8 - 1) % 4, b1 % 2, i8 + b1)

            dve.sem_inc(S("L3aout"), CREDIT)
            for u in range(2):
                leaky("L3a", scr[0][u], u, u)
                mask("L3a", scr[0][u], u, 0, 16, False)
            step(0, 0, 0, 0)
            for v in link.loop(U // 8, 8 * 5):
                for k in range(1, 9):
                    step(v * 8 + k, k, v * 2, v)
            v = U // 8
            for k in range(1, 4):
                step(8 * v + k, k, 2 * v, v)
            attention_out(U - 1, 3)
            wide_in(U - 1)
            wide_out(U - 1, 3, 0, NB - 1)
            dve.wait_ge(S("y_made"), NB)

            for t in range(CT):
                link.mark(v_.bn_aggr(mv[:, t, :], gst[:, t, :]))
            link.join()
            link(ts(aff[:, 4, :], colw[:, 3, :], -1.0, 1.0, ALU.mult, ALU.add))
            link(tt(aff[:, 4, :], aff[:, 4, :], mv[:, :, 0], ALU.mult))
            link(tt(aff[:, 4, :], aff[:, 4, :], aff[:, 4, :], ALU.mult))
            stt(aff[:, 0, :], mv[:, :, 1], BN_EPS, aff[:, 4, :], ALU.add, ALU.add).then_inc(S("gn_var"), 1)
            dve.wait_ge(S("gn_std"), 1)
            link(v_.reciprocal(aff[:, 1, :], aff[:, 1, :]))
            link(tt(aff[:, 2, :], aff[:, 1, :], colw[:, 1, :], ALU.mult))
            link(tt(aff[:, 4, :], colw[:, 3, :], mv[:, :, 0], ALU.mult))
            link(tt(aff[:, 4, :], aff[:, 4, :], aff[:, 2, :], ALU.mult))
            tt(aff[:, 3, :], colw[:, 2, :], aff[:, 4, :], ALU.subtract).then_inc(S("gn_aff"), 1)

            n = 0
            for c, (n0, nn) in enumerate(NCH):
                for b in range(nn // Q):
                    dve.wait_ge(S("ring_pe"), base["z3"] + n + 1)
                    cp(Bn[0:Q, n, :], ps[0:Q, n % 4, 0:D])
                    cp(ald[0:Q, n, 0:1], ps[0:Q, n % 4, D + 1:D + 2]).then_inc(S("ring_ev"), 1)
                    n += 1
                dve.wait_ge(S("wide_used"), c + 1)
                cp(R[0:2, 8192 + n0:8192 + n0 + nn], ps[0:2, 4 + c % 2, 0:nn]).then_inc(S("row2_ev"), 1)
            dve.wait_ge(S("row2_ev"), len(NCH))
            dve.sem_inc(S("row2_made"), 1)
            dve.wait_ge(S("row2_out"), 16)

            dve.sem_inc(S("L3blnc_used"), CREDIT)
            dve.sem_inc(S("L3bout"), CREDIT)
            dve.wait_ge(S("x_back"), 16)

            def last_out(u, du):
                inverse(u, du)
                dve.wait_ge(S("L3bmm"), u * NG + (NG + RING))
                xi = X[0:Q, bass.ds(u, 1), :].rearrange("p o f -> p (o f)")
                stt(xi, acc[du % 2], mx[0:Q, 3, du:du + 1], xi, ALU.mult, ALU.add).then_inc(S("L3bout"), 1)

            def last_step(t, dt, v):
                ahead = not (isinstance(t, int) and t + 2 >= NB)
                d2 = (dt + 2) % 4
                evac("L3b", t, dt % 4, 1)
                if ahead:
                    leaky("L3b", scr[1][d2], t + 2, d2)
                if not (isinstance(t, int) and t == 0):
                    last_out(t - 1, (dt - 1) % 4)
                evac("L3b", t, dt % 4, 3)
                if ahead:
                    mask("L3b", scr[1][d2], d2, dt % 2, (v * 2 + (dt + 2) // 2 + 1) * 16, True)
                evac("L3b", t, dt % 4, 5)

            for u in range(2):
                leaky("L3b", scr[1][u], u, u)
                mask("L3b", scr[1][u], u, u, 16, True)
            last_step(0, 0, 0)
            for v in link.loop(NB // 4 - 1, 4 * 3):
                for k in range(1, 5):
                    last_step(v * 4 + k, k, v)
            v = NB // 4 - 1
            for k in range(1, 5):
                last_step(v * 4 + k, k, v)
            last_out(NB - 1, 0)


_INS = ["x", "src", "dst", "edge_weight", "L0_gnn_eps", "L0_gnn_W1", "L0_gnn_b1", "L0_gnn_g1", "L0_gnn_be1",
        "L0_gnn_W2", "L0_gnn_b2", "L0_gnn_g2", "L0_gnn_be2", "L1_gnn_W1", "L1_gnn_b1", "L1_gnn_W2", "L1_gnn_b2",
        "L1_gnn_Wl", "L1_gnn_bl", "L1_gnn_root_idx", "L2_gnn_W", "L2_gnn_b", "L3_gnn_W1", "L3_gnn_att_src1",
        "L3_gnn_att_dst1", "L3_gnn_b1", "L3_gnn_gn_w", "L3_gnn_gn_b", "L3_gnn_gn_ms", "L3_gnn_W2",
        "L3_gnn_att_src2", "L3_gnn_att_dst2", "L3_gnn_b2"]


def kernel(**inputs):
    import numpy as _np
    import concourse.bacc as _bacc
    from concourse import mybir as _mybir
    from concourse.bass_utils import run_bass_kernel_spmd as _run

    nc = _bacc.Bacc("TRN2", target_bir_lowering=False, num_devices=1)
    arrays, args = {}, []
    for name in _INS:
        a = _np.ascontiguousarray(inputs[name])
        arrays["in_" + name] = a
        args.append(nc.dram_tensor("in_" + name, a.shape, _mybir.dt.from_np(a.dtype), kind="ExternalInput").ap())
    args.append(nc.dram_tensor("out_0", (N, D), F32, kind="ExternalOutput").ap())
    gnn_stack(nc, *args)
    r = _run(nc, [arrays], core_ids=[0])
    return r.results[0]["out_0"]
```

```python
from contextlib import ExitStack

import concourse.bass as bass
from concourse import mybir

ALU = mybir.AluOpType
ACT = mybir.ActivationFunctionType
F32 = mybir.dt.float32
I32 = mybir.dt.int32
U32 = mybir.dt.uint32
AX_X = mybir.AxisListType.X

N = 3125
Q = 125
NB = N // Q
D = 256
KT = D // 128
E = 50000
EC = E // Q
HEADS = 4
WIDE = HEADS * D
CT = WIDE // 128
ROWS = NB * 128
SC = 4
NSC = EC // SC
TRASH = ROWS * N
GROUPS = [(0, 4), (4, 4), (8, 4), (12, 4), (16, 3), (19, 3), (22, 3)]
NG = len(GROUPS)
RING = 4
AHEAD = RING - 1
NA = (NG + 1) // 2
ND = NG // 2
HALF = [(0, 13), (13, 12)]
LN_EPS = 1e-5
BN_EPS = 1e-5
NEG = -1.0e30
TINY = 1.0e-18
MARK = 1024.0
ROUND = 12582912.0
CREDIT_TR = 2 * NG
CREDIT = 2


class Chain:

    def __init__(self, eng, sem):
        self.eng, self.sem, self.n, self.iv, self.per = eng, sem, 0, None, 0

    def value(self):
        return self.n if self.iv is None else self.iv * self.per + self.n

    def mark(self, ins):
        self.n += 1
        ins.then_inc(self.sem, 1)

    def join(self, but=0):
        self.eng.wait_ge(self.sem, self.value() - but)

    def __call__(self, ins):
        self.mark(ins)
        self.join()

    def loop(self, trips, per):
        with self.eng.Fori(0, trips) as iv:
            n0 = self.n
            self.iv, self.per = iv, per
            yield iv
            assert self.n - n0 == per, (self.n - n0, per)
        self.iv = None
        self.n = n0 + per * trips


def gnn_stack(nc, x, src, dst, edge_weight, eps0, W01, b01, g01, be01, W02, b02, g02, be02,
              W11, b11, W12, b12, Wl1, bl1, root_idx, W2, b2, W31, as31, ad31, b31, gnw, gnb, gnms,
              W32, as32, ad32, b32, out):
    with ExitStack() as ctx:
        sems = {}

        def S(name):
            if name not in sems:
                sems[name] = ctx.enter_context(nc.semaphore(name))
            return sems[name]

        def sb(name, shape, dt=F32):
            return ctx.enter_context(nc.sbuf_tensor(name, shape, dt))

        pairs = nc.dram_tensor("pairs", (TRASH + SC * 128, 2), F32, kind="Internal").ap()
        lnc_d = nc.dram_tensor("lnc_d", (NB, 128, N), F32, kind="Internal").ap()
        rows_d = nc.dram_tensor("rows_d", (HEADS, N), F32, kind="Internal").ap()
        wide_d = nc.dram_tensor("wide_d", (128, CT, N), F32, kind="Internal").ap()
        x_d = nc.dram_tensor("x_d", (Q, NB * D), F32, kind="Internal").ap()
        row2_d = nc.dram_tensor("row2_d", (N,), F32, kind="Internal").ap()
        pair_rows = pairs[0:TRASH, :].rearrange("(i p c) t -> i p c t", p=128, c=N)

        X = sb("X", [128, NB, D])
        H = sb("H", [128, NB, D])
        B = sb("B", [128, NB * D])
        Fb = sb("Fb", [128, KT * N])
        R = sb("R", [128, 4 * N])
        PT = sb("PT", [128, RING, 4 * Q])
        Bn = B[:, :].rearrange("p (j f) -> p j f", f=D)
        F = Fb[:, :].rearrange("p (k n) -> p k n", k=KT)
        G = R[:, 0:2 * N].rearrange("p (k n) -> p k n", k=KT)
        Rp = [R[:, s * 2 * N:(s + 1) * 2 * N].rearrange("p (n t) -> p n t", t=2) for s in range(2)]
        lncR = [R[:, s * N:(s + 1) * N] for s in range(2)]
        XH = [t[:, :, :].rearrange("p j f -> p (j f)") for t in (X, H)]
        scr = [[R[:, 2 * N:3 * N], R[:, 3 * N:4 * N], t[:, 0:N], t[:, N:2 * N]] for t in XH]
        lncW = [Fb[:, s * N:(s + 1) * N] for s in range(2)]
        als = [B[:, 0:N], B[:, N:2 * N], Fb[:, 0:N], Fb[:, N:2 * N]]

        wA = sb("wA", [128, 5 * KT * D])
        w01, w02, w11 = [wA[:, k * KT * D:(k + 1) * KT * D].rearrange("p (k n) -> p k n", k=KT) for k in range(3)]
        w12 = wA[:, 3 * KT * D:5 * KT * D].rearrange("p (k n) -> p k n", k=2 * KT)
        wB = sb("wB", [128, 4 * KT * D])
        wl1 = wB[:, 0:2 * KT * D].rearrange("p (k n) -> p k n", k=2 * KT)
        w2, w2T = [wB[:, k * KT * D:(k + 1) * KT * D].rearrange("p (k n) -> p k n", k=KT) for k in (2, 3)]
        gst = wB[:, 0:CT * NB * 6].rearrange("p (t s) -> p t s", t=CT)
        w31 = sb("w31", [128, KT, WIDE])
        w32 = sb("w32", [128, CT, D + 2])
        va = sb("va", [128, KT, 2 * HEADS])
        cols = sb("cols", [128, 6, KT])
        colw = sb("colw", [128, 4, CT])
        bcs = sb("bcs", [128, 5, D])
        ident = sb("ident", [128, 128])
        ones = sb("ones", [128, 128])
        small = sb("small", [128, 40])
        st = sb("st", [128, NB, 6])
        lns = sb("lns", [128, 6, NB])
        node = sb("node", [128, NB])
        pick = sb("pick", [128, NB])
        norm = sb("norm", [128, NB])
        rootc = sb("rootc", [128, KT])
        rootr = sb("rootr", [128, D])
        ald = sb("ald", [128, NB, HEADS])
        bst = sb("bst", [128, KT, 7, 6])
        mv = sb("mv", [128, CT, 2])
        aff = sb("aff", [128, 6, CT])
        mx = sb("mx", [128, 4, 4])
        ag = sb("ag", [128, 2, D])
        agT = sb("agT", [128, KT, Q])
        rootb = agT
        racc = ag[:, 0, :]
        alsc, alsr = ag[:, 0, :], ag[:, 1, :]
        yT = wA[:, 0:2 * CT * Q].rearrange("p (s t q) -> p s t q", s=2, t=CT)
        idx_i = sb("idx_i", [128, 4], I32)
        stage_k = sb("stage_k", [128, 2, SC], U32)
        stage_v = sb("stage_v", [128, 2, SC, 2])
        trash = sb("trash", [128, SC])
        trash_i = sb("trash_i", [128, SC], I32)

        src_i = Fb[0:Q, 0:EC].bitcast(I32)
        dst_i = Fb[0:Q, EC:2 * EC].bitcast(I32)
        wgt = Fb[0:Q, 2 * EC:3 * EC]
        key = Fb[0:Q, 3 * EC:4 * EC]
        e1 = Fb[0:Q, 4 * EC:5 * EC]
        e2 = Fb[0:Q, 5 * EC:6 * EC]
        key_u = Fb[:, 6 * EC:7 * EC].bitcast(U32)
        val = Fb[:, 7 * EC:9 * EC].rearrange("p (c t) -> p c t", t=2)
        M0 = 2 * N
        W = SC * Q
        tri = R[0:Q, M0:M0 + SC * W].rearrange("p (i w) -> p i w", i=SC)
        dgk = [R[0:Q, M0 + (4 + s) * W:M0 + (5 + s) * W].rearrange("p (i q) -> p i q", q=Q) for s in range(2)]
        dgw = [R[0:Q, M0 + (6 + s) * W:M0 + (7 + s) * W].rearrange("p (i q) -> p i q", q=Q) for s in range(2)]
        wrow = [R[0:Q, M0 + (8 + s) * W:M0 + (9 + s) * W] for s in range(2)]
        junk = [R[0:Q, M0 + (10 + s) * W:M0 + (11 + s) * W] for s in range(2)]
        att1 = [B[:, 0:WIDE], B[:, WIDE:2 * WIDE]]
        att2 = [B[:, 2 * WIDE:2 * WIDE + D], B[:, 2 * WIDE + D:2 * WIDE + 2 * D]]
        att_junk = B[:, 2 * WIDE + 2 * D:2 * WIDE + 3 * D]

        ps = ctx.enter_context(nc.psum_tensor("ps", [128, 8, 512], F32))
        psflat = ps[:, :, :].rearrange("p b c -> p (b c)")
        acc = [ps[0:Q, 4 + s, 0:D] for s in range(2)]

        block = ctx.enter_context(nc.Block())

        NCH = [(n0, min(4 * Q, N - n0)) for n0 in range(0, N, 4 * Q)]
        JP = [(j, min(2, NB - j)) for j in range(0, NB, 2)]
        CB = [(j, min(4, NB - j)) for j in range(0, NB, 4)]
        QG = [(k, j, nj) for j, nj in CB for k in range(KT)]
        PAIRS = (NB - 1) // 2
        MIX, gone = [], 0
        for c in range(len(CB) + 1):
            ready = gone
            if c < len(CB):
                MIX += [("F", k) + CB[c] for k in range(KT)]
                gone = len(MIX)
            if c:
                j, nj = CB[c - 1]
                MIX += [("P", ready, jj, min(2, j + nj - jj)) for jj in range(j, j + nj, 2)]
        WSLOT = [(c % 2) * 4096 if c < len(NCH) - 1 else 8192 for c in range(len(NCH))]
        WSEM = [f"wide_in{c % 2}" if c < len(NCH) - 1 else "wide_in_last" for c in range(len(NCH))]

        base, total = {}, 0
        for stage_name, groups in (("z", len(QG)), ("y1", KT * len(NCH)), ("y2", KT * len(NCH)), ("l0", len(JP)),
                                   ("m1", len(MIX)), ("m2", len(MIX)), ("m3", len(MIX)), ("m4", len(MIX)),
                                   ("h5", len(QG)), ("z3", NB)):
            base[stage_name] = total
            total += groups

        def ring_wait(eng, name, n):
            if n >= 4 or (n == 0 and base[name]):
                eng.wait_ge(S("ring_ev"), base[name] + max(n - 3, 0))

        @block.sync
        def _(sp):
            sp.dma_start(src_i, src.rearrange("(p c) -> p c", c=EC)).then_inc(S("edges_in"), 16)
            sp.dma_start(dst_i, dst.rearrange("(p c) -> p c", c=EC)).then_inc(S("edges_in"), 16)
            sp.dma_start(wgt, edge_weight.rearrange("(p c) -> p c", c=EC)).then_inc(S("edges_in"), 16)
            sp.wait_ge(S("zero_made"), 1)
            flat = pairs[0:TRASH, :].rearrange("(i p c) t -> i p (c t)", p=128, c=N)
            with sp.Fori(0, NB) as i:
                sp.dma_start(flat[bass.ds(i, 1)].rearrange("o p c -> (o p) c"), R[:, 0:2 * N]).then_inc(S("zeroed"), 16)
            sp.dma_start(pairs[TRASH:TRASH + SC * 128, :].rearrange("(p c) t -> p (c t)", p=128),
                         R[:, 0:2 * SC]).then_inc(S("zeroed"), 16)
            sp.dma_start(X[0:Q, :, :], x.rearrange("(p j) f -> p j f", j=NB)).then_inc(S("x_in"), 16)
            w_in = S("w_in")
            nw = 0
            for t, w in ((w01, W01), (w02, W02), (w11, W11), (w12, W12), (wl1, Wl1), (w2, W2), (w31, W31)):
                sp.dma_start(t[:, :, :], w.rearrange("(k p) n -> p k n", p=128)).then_inc(w_in, 16)
                nw += 1
            sp.dma_start(w32[:, :, 0:D], W32.rearrange("(k p) n -> p k n", p=128)).then_inc(w_in, 16)
            for k, a in enumerate((as31, ad31)):
                sp.dma_start(att1[k], a.rearrange("h c -> (h c)").partition_broadcast(128)).then_inc(w_in, 16)
            for k, a in enumerate((as32, ad32)):
                sp.dma_start(att2[k], a.rearrange("h c -> (h c)").partition_broadcast(128)).then_inc(w_in, 16)
            for k, v in enumerate((b11, b12, bl1, b2, b32)):
                sp.dma_start(bcs[:, k, :], v.partition_broadcast(128)).then_inc(w_in, 16)
            sp.dma_start(idx_i[:, 0:1], root_idx[0:1].partition_broadcast(128)).then_inc(w_in, 16)
            sp.dma_start(small[:, 0:1], eps0.partition_broadcast(128)).then_inc(w_in, 16)
            with nc.allow_non_contiguous_dma(reason="a few hundred per-feature values"):
                for k, v in enumerate((b01, g01, be01, b02, g02, be02)):
                    sp.dma_start(cols[:, k, :], v.rearrange("(k p) -> p k", p=128)).then_inc(w_in, 16)
                for k, v in enumerate((b31, gnw, gnb, gnms)):
                    sp.dma_start(colw[:, k, :], v.rearrange("(k p) -> p k", p=128)).then_inc(w_in, 16)

            sp.wait_ge(S("scattered"), 16 * EC)
            for h, (j0, nj) in enumerate(HALF):
                def half_rows(i, s, k):
                    sp.wait_ge(S(f"L0used{h}"), k)
                    r = pair_rows[bass.ds(i, 1)].rearrange("o p c t -> (o p) c t")[:, j0 * Q:(j0 + nj) * Q, :]
                    sp.dma_start(Rp[s][:, 0:nj * Q, :], r).then_inc(S(f"L0rows{h}_{s}"), 16)
                if h:
                    sp.wait_ge(S("L0used0"), NB + CREDIT)
                with sp.Fori(0, PAIRS) as v:
                    half_rows(v * 2, 0, v * 2 + 1)
                    half_rows(v * 2 + 1, 1, v * 2 + 2)
                half_rows(NB - 1, 0, NB)

            def pair_pass(name, extra=None):
                def load(i, s, k):
                    sp.wait_ge(S(name + "tr"), k * NG)
                    if extra:
                        sp.wait_ge(S(extra), k)
                    sp.dma_start(Rp[s], pair_rows[bass.ds(i, 1)].rearrange("o p c t -> (o p) c t"))\
                        .then_inc(S(f"{name}rows{s}"), 16)

                with sp.Fori(0, PAIRS) as v:
                    load(v * 2, 0, v * 2 + 1)
                    load(v * 2 + 1, 1, v * 2 + 2)
                load(NB - 1, 0, NB)

            sp.wait_ge(S("r_free_L1a"), 1)
            pair_pass("L1a", "lnc_read")
            sp.wait_ge(S("L1a_done"), 1)
            pair_pass("L1b")
            sp.wait_ge(S("L1b_done"), 1)
            pair_pass("L2")

            def lnc_load(name, i, s, k):
                sp.wait_ge(S(name + "lnc_used"), k)
                sp.dma_start(lncR[s], lnc_d[bass.ds(i, 1)].rearrange("o p c -> (o p) c"))\
                    .then_inc(S(f"{name}lnc{s}"), 16)

            def wide_store(i, s, k, ks):
                sp.wait_ge(S("y_made"), k)
                with nc.allow_non_contiguous_dma(reason="rows of a block"):
                    sp.dma_start(wide_d[:, :, bass.ds(i * Q, Q)], yT[:, s, :, :]).then_inc(S(f"y_out{s}"), 16)
                sp.wait_ge(S(f"y_out{s}"), ks)
                sp.sem_inc(S("y_free"), 1)

            sp.sem_inc(S("y_free"), CREDIT)
            lnc_load("L3a", 0, 0, 1)
            lnc_load("L3a", 1, 1, 2)
            sp.wait_ge(S("alsrow_made"), 1)
            sp.dma_start(rows_d.rearrange("h (j q) -> (h j) q", q=Q), alsr[0:HEADS * NB, 0:Q])\
                .then_inc(S("alsrow_out"), 16)
            sp.wait_ge(S("alsrow_out"), 16)
            for h in range(HEADS):
                if h == 2:
                    sp.wait_ge(S("bias_in_x"), 1)
                    sp.dma_start(x_d[:, :], XH[0][0:Q, :]).then_inc(S("x_out"), 16)
                sp.dma_start(als[h], rows_d[h, :].partition_broadcast(128)).then_inc(S("als_in"), 16)
                sp.wait_ge(S("als_in"), 16 * (h + 1))
            with sp.Fori(0, PAIRS - 1) as v:
                lnc_load("L3a", v * 2 + 2, 0, v * 2 + 3)
                wide_store(v * 2, 0, v * 2 + 1, (v + 1) * 16)
                lnc_load("L3a", v * 2 + 3, 1, v * 2 + 4)
                wide_store(v * 2 + 1, 1, v * 2 + 2, (v + 1) * 16)
            lnc_load("L3a", NB - 1, 0, NB)
            wide_store(NB - 3, 0, NB - 2, PAIRS * 16)
            wide_store(NB - 2, 1, NB - 1, PAIRS * 16)
            wide_store(NB - 1, 0, NB, (PAIRS + 1) * 16)
            for c in [0, 1, len(NCH) - 1] + list(range(2, len(NCH) - 1)):
                n0, nn = NCH[c]
                if 2 <= c < len(NCH) - 1:
                    sp.wait_ge(S("ring_pe"), base["z3"] + 4 * (c - 1))
                slot = R[:, WSLOT[c]:WSLOT[c] + CT * nn].rearrange("p (t n) -> p t n", t=CT)
                sp.dma_start(slot, wide_d[:, :, n0:n0 + nn]).then_inc(S(WSEM[c]), 16)
            sp.dma_start(XH[0][0:Q, :], x_d[:, :]).then_inc(S("x_back"), 16)
            sp.wait_ge(S("ring_pe"), base["z3"] + 4 * (len(NCH) - 2))
            lnc_load("L3b", 0, 0, 1)
            sp.wait_ge(S("ring_pe"), base["z3"] + 4 * (len(NCH) - 1))
            lnc_load("L3b", 1, 1, 2)
            sp.wait_ge(S("row2_made"), 1)
            sp.dma_start(row2_d.rearrange("(j q) -> j q", q=Q), alsr[0:NB, 0:Q]).then_inc(S("row2_out"), 16)
            sp.wait_ge(S("row2_out"), 16)
            sp.dma_start(als[2], row2_d.partition_broadcast(128)).then_inc(S("als2_in"), 16)
            sp.wait_ge(S("als2_in"), 16)
            out_v = out.rearrange("(p j) f -> p j f", j=NB)

            def out_store(i):
                sp.wait_ge(S("L3bout"), i + 1 + CREDIT)
                sp.dma_start(out_v[:, bass.ds(i, 1), :], X[0:Q, bass.ds(i, 1), :]).then_inc(S("stored"), 16)

            lnc_load("L3b", 2, 0, 3)
            with sp.Fori(0, PAIRS - 1) as v:
                lnc_load("L3b", v * 2 + 3, 1, v * 2 + 4)
                out_store(v * 2)
                lnc_load("L3b", v * 2 + 4, 0, v * 2 + 5)
                out_store(v * 2 + 1)
            for i in range(2 * (PAIRS - 1), NB):
                out_store(i)
            sp.wait_ge(S("stored"), 16 * NB)
        @block.gpsimd
        def _(pool):
            g = nc.gpsimd
            link = Chain(pool, S("pool_chain"))
            link(g.memset(ident[:, :], 0.0))
            g.affine_select(out=ident[:, :], in_=ident[:, :], compare_op=ALU.not_equal, fill=1.0, base=0,
                            pattern=[[-1, 128]], channel_multiplier=1).then_inc(S("pool_consts"), 1)
            link(g.memset(tri, 1.0))
            for i in range(SC):
                g.affine_select(out=tri[:, i, :], in_=tri[:, i, :], compare_op=ALU.is_ge, fill=1.0 + MARK,
                                base=-i * Q, pattern=[[1, W]], channel_multiplier=-1).then_inc(S("pool_consts"), 1)
            g.iota(trash_i[:, :], pattern=[[128, SC]], base=TRASH, channel_multiplier=1).then_inc(S("pool_consts"), 1)
            g.iota(node[:, :], pattern=[[1, NB]], base=0, channel_multiplier=NB,
                   allow_small_or_imprecise_dtypes=True).then_inc(S("pool_consts"), 1)

            def stage(t, s, k):
                pool.wait_ge(S("merged"), k)
                link.mark(g.tensor_copy(stage_k[:, s, :], key_u[:, bass.ds(t * SC, SC)]))
                link(g.tensor_copy(stage_v[:, s, :, :], val[:, bass.ds(t * SC, SC), :]))

            def scatter(s):
                pool.sem_inc(S("rounds_begun"), 1)
                for i in range(SC):
                    pool.indirect_dma_start(pairs, bass.IndirectOffsetOnAxis(ap=stage_k[:, s, i:i + 1], axis=0),
                                            stage_v[:, s, i, :], None, compute_op=ALU.add).then_inc(S("scattered"), 16)

            stage(0, 0, 1)
            pool.wait_ge(S("zeroed"), 16 * (NB + 1))
            for v in link.loop(NSC // 2 - 1, 4):
                scatter(0)
                stage(v * 2 + 1, 1, v + 1)
                pool.wait_ge(S("scattered"), (v * 2 + 1) * (16 * SC))
                scatter(1)
                stage(v * 2 + 2, 0, v + 2)
                pool.wait_ge(S("scattered"), (v * 2 + 2) * (16 * SC))
            scatter(0)
            stage(NSC - 1, 1, NSC // 2)
            pool.wait_ge(S("scattered"), (NSC - 1) * (16 * SC))
            scatter(1)

            pool.sem_inc(S("lnc_free"), CREDIT)

            def lnc_store(i, s, k):
                pool.wait_ge(S("lnc_read"), k + CREDIT)
                pool.dma_start(lnc_d[bass.ds(i, 1)].rearrange("o p c -> (o p) c"), lncW[s]).then_inc(S("lnc_out"), 16)
                pool.wait_ge(S("lnc_out"), k * 16)
                pool.sem_inc(S("lnc_free"), 1)

            with pool.Fori(0, PAIRS) as v:
                lnc_store(v * 2, 0, v * 2 + 1)
                lnc_store(v * 2 + 1, 1, v * 2 + 2)
            lnc_store(NB - 1, 0, NB)

        @block.tensor
        def _(pe):
            mm = nc.tensor.matmul

            def features_group(n, node_major, k, j, nj):
                for m in range(nj):
                    last = nc.tensor.transpose(ps[:, n % 4, m * Q:(m + 1) * Q],
                                               node_major[0:Q, j + m, k * 128:(k + 1) * 128], ident[0:Q, 0:Q])
                last.then_inc(S("ring_pe"), 1)

            def mixed(name, node_major, w, gate=None, beside=None):
                for n, (kind, a, j, nj) in enumerate(MIX):
                    if kind == "F":
                        if gate is not None and a == 0:
                            pe.wait_ge(S("ln_done"), gate * NB + j + nj)
                            if beside:
                                beside(j, nj)
                        ring_wait(pe, name, n)
                        features_group(n, node_major, a, j, nj)
                    else:
                        pe.wait_ge(S("ring_ev"), base[name] + max(a, n - 3))
                        for m in range(nj):
                            for k in range(KT):
                                last = mm(ps[0:Q, n % 4, m * D:(m + 1) * D], F[:, k, (j + m) * Q:(j + m + 1) * Q],
                                          w[:, k, :], start=k == 0, stop=k == KT - 1)
                        last.then_inc(S("ring_pe"), 1)

            def feature_product(name, w, inp, ready=None):
                n = 0
                for m, (n0, nn) in enumerate(NCH):
                    if ready:
                        pe.wait_ge(S(ready), KT * (m + 1))
                    for c in range(KT):
                        ring_wait(pe, name, n)
                        for k in range(KT):
                            last = mm(ps[:, n % 4, 0:nn], w[:, k, c * 128:(c + 1) * 128], inp[:, k, n0:n0 + nn],
                                      start=k == 0, stop=k == KT - 1)
                        last.then_inc(S("ring_pe"), 1)
                        n += 1

            def to_nodes(name, feat, ready):
                for n, (j, nj) in enumerate(JP):
                    pe.wait_ge(S(ready), KT * ((j + nj - 1) // 4 + 1))
                    ring_wait(pe, name, n)
                    for m in range(nj):
                        for k in range(KT):
                            last = nc.tensor.transpose(ps[0:Q, n % 4, m * D + k * 128:m * D + (k + 1) * 128],
                                                       feat[:, k, (j + m) * Q:(j + m + 1) * Q], ident[:, :])
                    last.then_inc(S("ring_pe"), 1)

            pe.wait_ge(S("ones_made"), 1)

            def broadcast(s, k):
                pe.wait_ge(S("diag_made"), k)
                pe.wait_ge(S("keyrow_free"), k)
                pe.wait_ge(S("wrow_out"), k)
                mm(ps[0:Q, s, 0:W], ones[0:Q, 0:Q], dgk[s].rearrange("p i q -> p (i q)"), start=True, stop=True)
                mm(ps[0:Q, 2 + s, 0:W], ones[0:Q, 0:Q], dgw[s].rearrange("p i q -> p (i q)"), start=True, stop=True)\
                    .then_inc(S("rows_made"), 1)

            with pe.Fori(0, NSC // 2) as v:
                broadcast(0, v * 2 + 1)
                broadcast(1, v * 2 + 2)

            pe.wait_ge(S("keyrow_free"), NSC + CREDIT)
            pe.wait_ge(S("wrow_out"), NSC + CREDIT)
            pe.wait_ge(S("ln_done"), 1 * NB)
            for h, (j0, nj) in enumerate(HALF):
                if h:
                    pe.wait_ge(S("L0sum"), 1)
                pe.sem_inc(S(f"L0used{h}"), CREDIT)

                def half(i, s, k, first, last_):
                    pe.wait_ge(S(f"L0rows{h}_{s}"), k)
                    for j in range(nj):
                        ins = mm(ps[0:Q, j // 2, (j % 2) * D:(j % 2 + 1) * D], Rp[s][0:Q, j * Q:(j + 1) * Q, 0],
                                 H[0:Q, bass.ds(i, 1), :].rearrange("p o f -> p (o f)"),
                                 start=first and j % 2 == 0, stop=last_, skip_group_check=True)
                    ins.then_inc(S(f"L0used{h}"), 1)

                half(0, 0, 16, True, False)
                with pe.Fori(0, PAIRS - 1) as v:
                    half(v * 2 + 1, 1, (v + 1) * 16, False, False)
                    half(v * 2 + 2, 0, (v + 2) * 16, False, False)
                half(NB - 2, 1, PAIRS * 16, False, False)
                half(NB - 1, 0, (PAIRS + 1) * 16, False, True)

            for name in ("L1a", "L1b", "L2"):
                pe.sem_inc(S(name + "tr"), CREDIT * NG)
            pe.wait_ge(S("L0sum"), 2)
            for n, (k, j, nj) in enumerate(QG):
                ring_wait(pe, "z", n)
                features_group(n, Bn, k, j, nj)
            pe.wait_ge(S("ring_ev"), base["z"] + len(QG))
            feature_product("y1", w01, F)
            feature_product("y2", w02, G, "bn1_done")
            to_nodes("l0", F, "bn2_done")

            def agg(name, rows, rhs, ready):
                if name in ("L3a", "L3b"):
                    pe.sem_inc(S(name + "tr"), CREDIT * NG)
                pe.sem_inc(S(name + "mm"), RING)

                def T(u, du, g, k):
                    if g == 0:
                        pe.wait_ge(S(ready(du)), k)
                    j, nj = GROUPS[g]
                    ring = (du * NG + g) % RING
                    for b in range(nj):
                        last = nc.tensor.transpose(ps[0:Q, ring, b * Q:(b + 1) * Q], rows(du, j + b), ident[0:Q, 0:Q])
                    last.then_inc(S(name + "tr"), 1)

                def M(u, du, g):
                    if g == 0:
                        pe.wait_ge(S(name + "out"), u + 1)
                    if g % 2 == 0:
                        pe.wait_ge(S(name + "evA"), u * NA + g // 2 + 1)
                    else:
                        pe.wait_ge(S(name + "evD"), u * ND + g // 2 + 1)
                    j, nj = GROUPS[g]
                    ring = (du * NG + g) % RING
                    for b in range(nj):
                        last = mm(acc[du % 2], PT[0:Q, ring, b * Q:(b + 1) * Q], rhs[0:Q, j + b, :],
                                  start=j + b == 0, stop=j + b == NB - 1)
                    last.then_inc(S(name + "mm"), 1)

                def unit(u, du, key, last=False, between=None):
                    for g in range(NG):
                        n = g + AHEAD
                        if n < NG:
                            T(u, du, n, None)
                        elif not last:
                            T(u + 1, (du + 1) % 4, n - NG, key(u + 1, du + 1))
                        M(u, du, g)
                        if between:
                            between(g)

                for g in range(AHEAD):
                    T(0, 0, g, key_first[name])
                return unit

            key_first = {"L1a": 16, "L1b": 16, "L2": 16, "L3a": 1, "L3b": 1}

            def whole(name, plane, rhs):
                unit = agg(name, lambda du, j: Rp[du % 2][0:Q, j * Q:(j + 1) * Q, plane], rhs,
                           lambda du: f"{name}rows{du % 2}")
                with pe.Fori(0, NB // 4) as v:
                    for du in range(4):
                        unit(v * 4 + du, du, lambda u, d: (v * 2 + d // 2 + 1) * 16)
                unit(NB - 1, 0, None, True)

            pe.wait_ge(S("pick_made"), 1)

            def root1(j0, nj):
                for j in range(j0, j0 + nj):
                    for k in range(KT):
                        last = mm(ps[:, 6, k:k + 1], H[0:Q, j, k * 128:(k + 1) * 128], pick[0:Q, j:j + 1],
                                  start=j == 0 and k == 0, stop=j == NB - 1, skip_group_check=True)
                if j0 + nj == NB:
                    last.then_inc(S("root1"), 1)

            mixed("m1", H, w11, 1, root1)
            pe.wait_ge(S("ring_ev"), base["m1"] + len(MIX))
            whole("L1a", 0, Bn)
            pe.wait_ge(S("rootb1"), 1)
            for k in range(KT):
                last = mm(ps[0:Q, 7, 0:D], rootb[:, k, :], w12[:, KT + k, :], start=k == 0, stop=k == KT - 1)
            last.then_inc(S("rootr1"), 1)
            pe.wait_ge(S("root_acc"), NB + 1)
            for k in range(KT):
                last = mm(ps[:, 6, k:k + 1], racc[0:Q, k * 128:(k + 1) * 128], ones[0:Q, 0:1], start=True, stop=True)
            last.then_inc(S("root2"), 1)
            pe.wait_ge(S("f2_leaky"), NB)
            mixed("m2", H, w12)
            pe.wait_ge(S("ring_ev"), base["m2"] + len(MIX))
            whole("L1b", 0, Bn)
            pe.wait_ge(S("rootb2"), 1)
            for k in range(KT):
                last = mm(ps[0:Q, 7, 0:D], rootb[:, k, :], wl1[:, KT + k, :], start=k == 0, stop=k == KT - 1)
            last.then_inc(S("rootr2"), 1)
            pe.wait_ge(S("f3_leaky"), NB)
            mixed("m3", H, wl1)
            pe.wait_ge(S("rootr_used"), 2)
            for ko in range(KT):
                for ki in range(KT):
                    last = nc.tensor.transpose(ps[:, 7, ki * D + ko * 128:ki * D + (ko + 1) * 128],
                                               w2[:, ko, ki * 128:(ki + 1) * 128], ident[:, :])
            last.then_inc(S("w2T_pe"), 1)

            pe.wait_ge(S("w2T_made"), 1)
            mixed("m4", H, w2T, 2)
            pe.wait_ge(S("ring_ev"), base["m4"] + len(MIX))
            whole("L2", 1, Bn)

            pe.wait_ge(S("va_made"), 1)

            def score_columns(j0, nj):
                for j in range(j0, j0 + nj):
                    for k in range(KT):
                        last = mm(ps[0:Q, 6, j * 2 * HEADS:(j + 1) * 2 * HEADS], F[:, k, j * Q:(j + 1) * Q],
                                  va[:, k, :], start=k == 0, stop=k == KT - 1)
                return last

            for n, (k, j, nj) in enumerate(QG):
                if k == 0:
                    pe.wait_ge(S("ln_done"), 3 * NB + j + nj)
                ring_wait(pe, "h5", n)
                features_group(n, H, k, j, nj)
                if k == KT - 1 and n >= 2 * KT:
                    pe.wait_ge(S("ring_ev"), base["h5"] + n + 1 - 2 * KT)
                    score_columns(*CB[n // KT - 2])
            pe.wait_ge(S("ring_ev"), base["h5"] + len(QG))
            score_columns(*CB[-2])
            score_columns(*CB[-1]).then_inc(S("ald_mm"), 1)
            pe.wait_ge(S("alsc_made"), 1)
            nc.tensor.transpose(ps[0:HEADS * NB, 7, 0:Q], alsc[0:Q, 0:HEADS * NB], ident[0:Q, 0:Q])\
                .then_inc(S("alsT_pe"), 1)
            pe.wait_ge(S("ald_made"), 1)

            def wide_T(s, k):
                pe.wait_ge(S("L3aout"), k)
                for t in range(KT):
                    last = nc.tensor.transpose(ps[:, 6, t * Q:(t + 1) * Q], ag[0:Q, s, t * 128:(t + 1) * 128],
                                               ident[0:Q, 0:Q])
                last.then_inc(S("agT_pe"), 1)

            def wide_M(hd, k):
                pe.wait_ge(S("agT_made"), k)
                for c in range(KT):
                    for t in range(KT):
                        last = mm(ps[:, 7, c * Q:(c + 1) * Q], w31[:, t, hd * D + c * 128:hd * D + (c + 1) * 128],
                                  agT[:, t, :], start=t == 0, stop=t == KT - 1)
                last.then_inc(S("y_pe"), 1)

            unit = agg("L3a", lambda du, j: scr[0][du][0:Q, j * Q:(j + 1) * Q], H, lambda du: "L3aprob")

            def wide_unit(u, du, last=False):
                def between(g):
                    if g == 3:
                        wide_T((du - 1) % 2, u + CREDIT)
                    if g == 6:
                        wide_M((du - 1) % 4, u)
                unit(u, du, lambda w, d: w + 1, last, between)

            unit(0, 0, lambda w, d: w + 1)
            with pe.Fori(0, NB - 1) as v:
                for k in range(1, 5):
                    wide_unit(v * 4 + k, k % 4)
            for u in range(4 * (NB - 1) + 1, 4 * NB):
                wide_unit(u, u % 4, u == 4 * NB - 1)
            wide_T(1, 4 * NB + CREDIT)
            wide_M(3, 4 * NB)

            pe.wait_ge(S("y_made"), NB)
            pe.wait_ge(S("L3aout"), 4 * NB + CREDIT)
            pe.wait_ge(S("v2_made"), 1)
            n = 0
            for c, (n0, nn) in enumerate(NCH):
                pe.wait_ge(S("wide_norm"), CT * (c + 1))
                slot = R[:, WSLOT[c]:WSLOT[c] + CT * nn].rearrange("p (t n) -> p t n", t=CT)
                for b in range(nn // Q):
                    ring_wait(pe, "z3", n)
                    for t in range(CT):
                        last = mm(ps[0:Q, n % 4, 0:D + 2], slot[:, t, b * Q:(b + 1) * Q], w32[:, t, :],
                                  start=t == 0, stop=t == CT - 1)
                    last.then_inc(S("ring_pe"), 1)
                    n += 1
            pe.wait_ge(S("ring_ev"), base["z3"] + NB)
            nc.tensor.transpose(ps[0:NB, 6, 0:Q], ald[0:Q, :, 0], ident[0:Q, 0:Q]).then_inc(S("als2_pe"), 1)
            unit = agg("L3b", lambda du, j: scr[1][du][0:Q, j * Q:(j + 1) * Q], Bn, lambda du: "L3bprob")
            with pe.Fori(0, NB // 4) as v:
                for du in range(4):
                    unit(v * 4 + du, du, lambda w, d: w + 1)
            unit(NB - 1, 0, None, True)

        @block.scalar
        def _(act):
            a = nc.scalar.activation
            link = Chain(act, S("act_chain"))

            act.wait_ge(S("pool_consts"), 1)
            act.wait_ge(S("key_made"), 1)
            act.sem_inc(S("wrow_out"), CREDIT)

            def diag(t, s, k):
                act.wait_ge(S("rows_made"), k)
                for i in range(SC):
                    a(dgk[s][:, i, :], ident[0:Q, 0:Q], ACT.Copy, scale=key[:, bass.ds(t * SC + i, 1)])
                    last = a(dgw[s][:, i, :], ident[0:Q, 0:Q], ACT.Copy, scale=wgt[:, bass.ds(t * SC + i, 1)])
                last.then_inc(S("diag_made"), 1)

            def wrow_out(s, k):
                act.wait_ge(S("rows_made"), k + 2)
                act.wait_ge(S("keyrow_free"), k)
                a(wrow[s], ps[0:Q, 2 + s, 0:W], ACT.Copy).then_inc(S("wrow_out"), 1)

            act.sem_inc(S("rows_made"), 2)
            diag(0, 0, 1)
            with act.Fori(0, NSC // 2 - 1) as v:
                diag(v * 2 + 1, 1, v * 2 + 2)
                wrow_out(0, v * 2 + 1)
                diag(v * 2 + 2, 0, v * 2 + 3)
                wrow_out(1, v * 2 + 2)
            diag(NSC - 1, 1, NSC)
            wrow_out(0, NSC - 1)
            wrow_out(1, NSC)

            def evac(name, u, du, g):
                ring = (du * NG + g) % RING
                w = GROUPS[g][1] * Q
                act.wait_ge(S(name + "tr"), u * NG + (g + 1 + CREDIT * NG))
                act.wait_ge(S(name + "mm"), u * NG + (g + 1))
                a(PT[0:Q, ring, 0:w], ps[0:Q, ring, 0:w], ACT.Copy).then_inc(S(name + "evA"), 1)

            def evac_pass(name, beside=None):
                def unit(u, du, v=0):
                    for g in range(0, NG, 2):
                        evac(name, u, du, g)
                        if beside:
                            beside(g, u, du, v)
                with act.Fori(0, NB // 4) as v:
                    for du in range(4):
                        unit(v * 4 + du, du, v)
                unit(NB - 1, 0, NB // 4)

            def normalise(l):
                act.wait_ge(S("ln_var"), l + 1)
                a(lns[0:Q, 4, :], lns[0:Q, 3, :], ACT.Sqrt).then_inc(S("ln_std"), 1)
                act.wait_ge(S("ln_aff"), l + 1)
                with act.Fori(0, NB // 5) as v:
                    for k in range(5):
                        j = v * 5 + k
                        a(H[0:Q, bass.ds(j, 1), :].rearrange("p o f -> p (o f)"),
                          X[0:Q, bass.ds(j, 1), :].rearrange("p o f -> p (o f)"), ACT.Relu,
                          scale=lns[0:Q, 4, bass.ds(j, 1)], bias=lns[0:Q, 5, bass.ds(j, 1)]).then_inc(S("ln_done"), 1)

            normalise(0)

            def batch_norm(y, bn, buf, bias):
                n = 0
                for n0, nn in NCH:
                    for c in range(KT):
                        act.wait_ge(S("ring_pe"), base[y] + n + 1)
                        a(buf[:, c, n0:n0 + nn], ps[:, n % 4, 0:nn], ACT.Identity, bias=cols[:, bias, c:c + 1])\
                            .then_inc(S("ring_ev"), 1)
                        n += 1
                act.wait_ge(S(bn + "_var"), 1)
                a(aff[:, 1, 0:KT], aff[:, 0, 0:KT], ACT.Sqrt).then_inc(S(bn + "_std"), 1)
                act.wait_ge(S(bn + "_aff"), 1)
                for n0, nn in NCH:
                    for c in range(KT):
                        y_ = buf[:, c, n0:n0 + nn]
                        a(y_, y_, ACT.Relu, scale=aff[:, 2, c:c + 1], bias=aff[:, 3, c:c + 1])\
                            .then_inc(S(bn + "_done"), 1)

            batch_norm("y1", "bn1", G, 0)
            batch_norm("y2", "bn2", F, 3)
            normalise(1)

            def counts(g, u, du, v):
                s = du % 2
                if g == 0:
                    act.wait_ge(S(f"L1arows{s}"), (v * 2 + du // 2 + 1) * 16)
                    a(Rp[s][0:Q, :, 1], Rp[s][0:Q, :, 1], ACT.Copy, accum_out=norm[0:Q, bass.ds(u, 1)])\
                        .then_inc(S("deg_made"), 1)
                if g == 4:
                    act.wait_ge(S("self_added"), u + 1)
                    a(Rp[s][:, :, 1], Rp[s][:, :, 1], ACT.Ln, bias=small[:, 1:2]).then_inc(S("ln_made"), 1)

            act.wait_ge(S("small_made"), 1)
            evac_pass("L1a", counts)
            evac_pass("L1b")
            act.wait_ge(S("deg_max"), 1)
            a(norm[0:Q, :], norm[0:Q, :], ACT.Sqrt).then_inc(S("deg_std"), 1)

            normalise(2)
            evac_pass("L2")
            normalise(3)

            def expo(name, slots, u, du):
                act.wait_ge(S(name + "max"), u + 1)
                a(slots[du][0:Q, :], slots[du][0:Q, :], ACT.Exp, bias=mx[0:Q, 1, du:du + 1],
                  accum_out=mx[0:Q, 2, du:du + 1]).then_inc(S(name + "prob"), 1)

            def attend(name, slots, row, col, units, rounds, ready=None):
                def sc(u, du):
                    if isinstance(u, int) and u < 4:
                        if ready:
                            ready(u)
                        a(slots[du][0:Q, :], row(u, du)[0:Q, :], ACT.Identity, bias=col(u, du))\
                            .then_inc(S(name + "score"), 1)
                    else:
                        act.wait_ge(S(name + "tr"), u * NG + (CREDIT - 3) * NG)
                        a(slots[du][0:Q, :], row(u, du)[0:Q, :], ACT.Identity, bias=col(u, du))\
                            .then_inc(S(name + "score"), 1)

                def step(t, dt):
                    for g in range(0, NG, 2):
                        evac(name, t, dt, g)
                        if g == 0 and not (isinstance(t, int) and t + 1 >= units):
                            expo(name, slots, t + 1, (dt + 1) % 4)
                        if g == 2 and not (isinstance(t, int) and t + 3 >= units):
                            sc(t + 3, (dt + 3) % 4)

                for u in range(2):
                    sc(u, u)
                expo(name, slots, 0, 0)
                sc(2, 2)
                step(0, 0)
                with act.Fori(0, rounds) as v:
                    for k in range(1, 5):
                        step(v * 4 + k, k % 4)
                for t in range(4 * rounds + 1, units):
                    step(t, t % 4)

            def ald3(u, h):
                flat = ald[0:Q, :, :].rearrange("p j h -> p (j h)")
                return flat[:, bass.ds(u, 1)]

            def rows_ready(u):
                act.wait_ge(S("als_in"), 16 * (u + 1))
                if u == 2:
                    act.wait_ge(S("x_out"), 16)

            act.wait_ge(S("ald_made"), 1)
            attend("L3a", scr[0], lambda u, du: als[du], lambda u, du: ald3(u, du), 4 * NB, NB - 1, rows_ready)

            act.wait_ge(S("gn_var"), 1)
            a(aff[:, 1, :], aff[:, 0, :], ACT.Sqrt).then_inc(S("gn_std"), 1)
            act.wait_ge(S("gn_aff"), 1)
            for c, (n0, nn) in enumerate(NCH):
                act.wait_ge(S(WSEM[c]), 16 * (c // 2 + 1) if c < len(NCH) - 1 else 16)
                slot = R[:, WSLOT[c]:WSLOT[c] + CT * nn].rearrange("p (t n) -> p t n", t=CT)
                for t in range(CT):
                    a(slot[:, t, :], slot[:, t, :], ACT.Relu, scale=aff[:, 2, t:t + 1], bias=aff[:, 3, t:t + 1])\
                        .then_inc(S("wide_norm"), 1)

            act.wait_ge(S("als2_in"), 16)
            act.wait_ge(S("ring_ev"), base["z3"] + NB)

            attend("L3b", scr[1], lambda u, du: als[2], lambda u, du: ald[0:Q, bass.ds(u, 1), 1], NB, NB // 4 - 1)

        @block.vector
        def _(dve):
            v_ = nc.vector
            tt, ts, stt, cp = v_.tensor_tensor, v_.tensor_scalar, v_.scalar_tensor_tensor, v_.tensor_copy
            link = Chain(dve, S("dve_chain"))

            v_.memset(R[:, 0:2 * N], 0.0).then_inc(S("zero_made"), 1)
            v_.memset(ones[:, :], 1.0).then_inc(S("ones_made"), 1)
            link.mark(v_.memset(val, 0.0))
            v_.memset(small[:, 1:2], TINY).then_inc(S("small_made"), 1)

            dve.wait_ge(S("edges_in"), 48)

            def block_of(out_, in_i, tmp):
                link(cp(out_, in_i))
                link(ts(tmp, out_, 1.0 / NB, 0.5 / NB - 0.5, ALU.mult, ALU.add))
                link(ts(tmp, tmp, ROUND, None, ALU.add))
                link(ts(tmp, tmp, ROUND, None, ALU.subtract))

            block_of(e1, dst_i, e2)
            link(ts(e1, e1, 128.0, None, ALU.mult))
            link(stt(e1, e2, -(128.0 * NB - 1.0), e1, ALU.mult, ALU.add))
            link(ts(key, e1, float(N), None, ALU.mult))
            block_of(e1, src_i, e2)
            link(stt(key, e1, float(Q), key, ALU.mult, ALU.add))
            stt(key, e2, -(float(Q) * NB - 1.0), key, ALU.mult, ALU.add).then_inc(S("key_made"), 1)
            dve.wait_ge(S("pool_consts"), 3 + SC)
            dve.wait_ge(S("key_made"), 1)
            link(cp(trash[:, :], trash_i[:, :]))
            link(cp(key_u.rearrange("p (t i) -> p t i", i=SC), trash[:, :].unsqueeze(1).to_broadcast([128, NSC, SC])))
            trashb = trash[0:Q, :].unsqueeze(1).to_broadcast([Q, 2, SC])

            dve.sem_inc(S("keyrow_free"), CREDIT)

            def merge(t, s, k):
                dve.wait_ge(S("wrow_out"), k)
                for i in range(SC):
                    c = t * SC + i
                    link.join(1)
                    link.mark(stt(junk[0], ps[0:Q, s, 0:W], key[:, bass.ds(c, 1)], wrow[s], ALU.is_equal, ALU.mult,
                                  accum_out=val[0:Q, bass.ds(c, 1), 0]))
                    link.join(1)
                    link.mark(stt(junk[1], ps[0:Q, s, 0:W], key[:, bass.ds(c, 1)], tri[:, i, :], ALU.is_equal,
                                  ALU.mult, accum_out=val[0:Q, bass.ds(c, 1), 1]))
                link.join()
                dve.sem_inc(S("keyrow_free"), 1)

            for v in link.loop(NSC // 2, 3 + 4 * SC):
                merge(v * 2, 0, v * 2 + 1 + CREDIT)
                merge(v * 2 + 1, 1, v * 2 + 2 + CREDIT)
                kk = key[:, bass.ds(v * (2 * SC), 2 * SC)].rearrange("p (a i) -> p a i", i=SC)
                f8 = small[0:Q, 8:8 + 2 * SC].rearrange("p (a i) -> p a i", i=SC)
                d8 = small[0:Q, 16:16 + 2 * SC].rearrange("p (a i) -> p a i", i=SC)
                link.mark(ts(f8, val[0:Q, bass.ds(v * (2 * SC), 2 * SC), 1].rearrange("p (a i) -> p a i", i=SC),
                             MARK, None, ALU.is_lt))
                link(tt(d8, kk, trashb, ALU.subtract))
                link(tt(d8, d8, f8, ALU.mult))
                tt(key_u[0:Q, bass.ds(v * (2 * SC), 2 * SC)].rearrange("p (a i) -> p a i", i=SC), d8, trashb,
                   ALU.add).then_inc(S("merged"), 1)

            dve.wait_ge(S("w_in"), 16 * 29)
            for k in range(KT):
                for w in range(2):
                    for h in range(HEADS):
                        link(stt(att_junk, w31[:, k, h * D:(h + 1) * D], 1.0, att1[w][:, h * D:(h + 1) * D],
                                 ALU.mult, ALU.mult, accum_out=va[:, k, w * HEADS + h:w * HEADS + h + 1]))
            dve.sem_inc(S("va_made"), 1)
            for k in range(CT):
                for w in range(2):
                    link(stt(att_junk, w32[:, k, 0:D], 1.0, att2[w], ALU.mult, ALU.mult,
                             accum_out=w32[:, k, D + w:D + w + 1]))
            dve.sem_inc(S("v2_made"), 1)
            link(cp(small[:, 4:5], idx_i[:, 0:1]))
            ts(pick[:, :], node[:, :], small[:, 4:5], None, ALU.is_equal).then_inc(S("pick_made"), 1)
            link(ts(small[:, 5:6], small[:, 0:1], 1.0, None, ALU.add))

            def stats_of(j):
                v_.bn_stats(st[0:Q, bass.ds(j, 1), :].rearrange("p o s -> p (o s)"),
                            X[0:Q, bass.ds(j, 1), :].rearrange("p o f -> p (o f)")).then_inc(S("ln_st"), 1)

            def ln_scale(l):
                L = [lns[0:Q, k, :] for k in range(6)]
                dve.wait_ge(S("ln_st"), (l + 1) * NB)
                link.mark(tt(L[0], st[0:Q, :, 1], st[0:Q, :, 4], ALU.add))
                link.mark(tt(L[1], st[0:Q, :, 1], st[0:Q, :, 4], ALU.subtract))
                link(tt(L[2], st[0:Q, :, 2], st[0:Q, :, 5], ALU.add))
                link.mark(ts(L[0], L[0], 0.5, None, ALU.mult))
                link.mark(tt(L[1], L[1], L[1], ALU.mult))
                link(ts(L[2], L[2], 1.0 / D, LN_EPS, ALU.mult, ALU.add))
                stt(L[3], L[1], 0.25, L[2], ALU.mult, ALU.add).then_inc(S("ln_var"), 1)
                dve.wait_ge(S("ln_std"), l + 1)
                link(v_.reciprocal(L[4], L[4]))
                stt(L[5], L[0], -1.0, L[4], ALU.mult, ALU.mult).then_inc(S("ln_aff"), 1)

            dve.wait_ge(S("x_in"), 16)
            with dve.Fori(0, NB) as j:
                stats_of(j)
            ln_scale(0)

            dve.wait_ge(S("ln_done"), 1 * NB)
            for h, (j0, nj) in enumerate(HALF):
                dve.wait_ge(S(f"L0used{h}"), NB + CREDIT)
                stt(Bn[0:Q, j0:j0 + nj, :].rearrange("p j f -> p (j f)"),
                    H[0:Q, j0:j0 + nj, :].rearrange("p j f -> p (j f)"), small[0:Q, 5:6], psflat[0:Q, 0:nj * D],
                    ALU.mult, ALU.add).then_inc(S("L0sum"), 1)

            def features_out(name):
                for n, (k, j, nj) in enumerate(QG):
                    dve.wait_ge(S("ring_pe"), base[name] + n + 1)
                    cp(F[:, k, j * Q:(j + nj) * Q], ps[:, n % 4, 0:nj * Q]).then_inc(S("ring_ev"), 1)

            def mixed_out(name, product):
                for n, (kind, a, j, nj) in enumerate(MIX):
                    dve.wait_ge(S("ring_pe"), base[name] + n + 1)
                    if kind == "P":
                        product(j, nj, n, ps[0:Q, n % 4, 0:nj * D].rearrange("p (j f) -> p j f", f=D))
                        continue
                    f_, p_ = F[:, a, j * Q:(j + nj) * Q], ps[:, n % 4, 0:nj * Q]
                    cp(f_, p_).then_inc(S("ring_ev"), 1)

            features_out("z")

            def bn_stats(y, bn, buf, g_, be):
                n = 0
                for m, (n0, nn) in enumerate(NCH):
                    for c in range(KT):
                        dve.wait_ge(S("ring_ev"), base[y] + n + 1)
                        link.mark(v_.bn_stats(bst[:, c, m, :], buf[:, c, n0:n0 + nn]))
                        n += 1
                link.join()
                for c in range(KT):
                    link.mark(v_.bn_aggr(mv[:, c, :], bst[:, c, :, :].rearrange("p m s -> p (m s)")))
                link.join()
                ts(aff[:, 0, 0:KT], mv[:, 0:KT, 1], BN_EPS, None, ALU.add).then_inc(S(bn + "_var"), 1)
                dve.wait_ge(S(bn + "_std"), 1)
                link(v_.reciprocal(aff[:, 1, 0:KT], aff[:, 1, 0:KT]))
                link(tt(aff[:, 2, 0:KT], aff[:, 1, 0:KT], cols[:, g_, :], ALU.mult))
                link(tt(aff[:, 4, 0:KT], aff[:, 2, 0:KT], mv[:, 0:KT, 0], ALU.mult))
                tt(aff[:, 3, 0:KT], cols[:, be, :], aff[:, 4, 0:KT], ALU.subtract).then_inc(S(bn + "_aff"), 1)

            bn_stats("y1", "bn1", G, 1, 2)
            dve.wait_ge(S("bn1_done"), KT * len(NCH))
            bn_stats("y2", "bn2", F, 4, 5)
            dve.sem_inc(S("lnc_read"), CREDIT)
            dve.sem_inc(S("r_free_L1a"), 1)
            for n, (j, nj) in enumerate(JP):
                dve.wait_ge(S("ring_pe"), base["l0"] + n + 1)
                xx = X[0:Q, j:j + nj, :].rearrange("p j f -> p (j f)")
                tt(xx, xx, ps[0:Q, n % 4, 0:nj * D], ALU.add).then_inc(S("ring_ev"), 1)
                dve.wait_ge(S("ring_ev"), base["l0"] + n + 1)
                for m in range(nj):
                    stats_of(j + m)

            ln_scale(1)

            def root_column(name, bname, leaky):
                dve.wait_ge(S(name), 1)
                if leaky:
                    link(ts(small[:, 26:28], ps[:, 6, 0:KT], 0.01, None, ALU.mult))
                    link(tt(rootc[:, :], small[:, 26:28], ps[:, 6, 0:KT], ALU.max))
                else:
                    link(cp(rootc[:, :], ps[:, 6, 0:KT]))
                for k in range(KT):
                    link.mark(ts(rootb[:, k, :], ones[:, 0:Q], rootc[:, k:k + 1], None, ALU.mult))
                link.join()
                dve.sem_inc(S(bname), 1)

            def plain_product(j, nj, n, p_):
                cp(Bn[0:Q, j:j + nj, :], p_).then_inc(S("ring_ev"), 1)

            mixed_out("m1", plain_product)
            root_column("root1", "rootb1", True)
            v_.memset(racc, 0.0).then_inc(S("root_acc"), 1)

            def evac(name, u, du, g):
                ring = (du * NG + g) % RING
                w = GROUPS[g][1] * Q
                dve.wait_ge(S(name + "tr"), u * NG + (g + 1 + CREDIT * NG))
                dve.wait_ge(S(name + "mm"), u * NG + (g + 1))
                cp(PT[0:Q, ring, 0:w], ps[0:Q, ring, 0:w]).then_inc(S(name + "evD"), 1)

            def plain_pass(name, out_unit, beside=None):
                dve.sem_inc(S(name + "out"), CREDIT)

                def unit(u, du, v, first=False):
                    for g in range(1, NG, 2):
                        evac(name, u, du, g)
                        if g == 1 and not first:
                            dve.wait_ge(S(name + "mm"), u * NG + RING)
                            out_unit(u - 1, 1 - du % 2)
                        if beside:
                            beside(g, u, du, v)

                unit(0, 0, 0, True)
                with dve.Fori(0, NB // 4) as v:
                    for k in range(1, 5):
                        unit(v * 4 + k, k % 4, v)
                dve.wait_ge(S(name + "mm"), NB * NG + RING)
                out_unit(NB - 1, 0)

            def out_bias(bias, name):
                def f(i, s):
                    tt(H[0:Q, bass.ds(i, 1), :].rearrange("p o f -> p (o f)"), acc[s], bcs[0:Q, bias, :], ALU.add)\
                        .then_inc(S(name + "out"), 1)
                return f

            def out_f2(i, s):
                out_bias(0, "L1a")(i, s)
                dve.wait_ge(S("L1aout"), i + (1 + CREDIT))
                dve.wait_ge(S("root_acc"), i + 1)
                stt(racc[0:Q, :], H[0:Q, bass.ds(i, 1), :].rearrange("p o f -> p (o f)"), pick[0:Q, bass.ds(i, 1)],
                    racc[0:Q, :], ALU.mult, ALU.add).then_inc(S("root_acc"), 1)
                leaky_row(i, "f2_leaky")

            def leaky_row(i, name):
                hi = H[0:Q, bass.ds(i, 1), :].rearrange("p o f -> p (o f)")
                stt(hi, hi, 0.01, hi, ALU.mult, ALU.max).then_inc(S(name), 1)

            def out_f3(i, s):
                out_bias(1, "L1b")(i, s)
                dve.wait_ge(S("L1bout"), i + (1 + CREDIT))
                leaky_row(i, "f3_leaky")

            def counts(g, u, du, v):
                s = du % 2
                if g == 1:
                    dve.wait_ge(S("deg_made"), u + 1)
                    dg = Rp[s][0:Q, bass.ds(u * Q, Q), 1]
                    tt(dg, dg, ident[0:Q, 0:Q], ALU.add).then_inc(S("diag_in"), 1)
                    dve.wait_ge(S("lnc_free"), u + 1)
                    dve.wait_ge(S("diag_in"), u + 1)
                    ts(lncW[s], Rp[s][:, :, 1], 0.5, NEG, ALU.is_lt, ALU.mult).then_inc(S("self_added"), 1)
                if g == 5:
                    dve.wait_ge(S("ln_made"), u + 1)
                    tt(lncW[s], lncW[s], Rp[s][:, :, 1], ALU.add).then_inc(S("lnc_read"), 1)

            dve.wait_ge(S("ring_ev"), base["m1"] + len(MIX))
            plain_pass("L1a", out_f2, counts)

            dve.wait_ge(S("lnc_read"), NB + CREDIT)
            dve.sem_inc(S("L1a_done"), 1)
            dve.wait_ge(S("rootr1"), 1)
            cp(rootr[0:Q, :], ps[0:Q, 7, 0:D]).then_inc(S("rootr_used"), 1)
            root_column("root2", "rootb2", False)
            rb2 = rootr[0:Q, :].unsqueeze(1)

            def root_product(j, nj, n, p_):
                tt(Bn[0:Q, j:j + nj, :], p_, rb2.to_broadcast([Q, nj, D]), ALU.add).then_inc(S("ring_ev"), 1)

            dve.wait_ge(S("rootr_used"), 1)
            dve.wait_ge(S("lnc_free"), NB + CREDIT)
            mixed_out("m2", root_product)
            plain_pass("L1b", out_f3)
            dve.wait_ge(S("ring_ev"), base["m2"] + len(MIX))
            dve.sem_inc(S("L1b_done"), 1)
            dve.wait_ge(S("deg_made"), NB)
            ts(norm[0:Q, :], norm[0:Q, :], 1.0, None, ALU.max).then_inc(S("deg_max"), 1)
            dve.wait_ge(S("rootr2"), 1)
            tt(rootr[0:Q, :], ps[0:Q, 7, 0:D], bcs[0:Q, 2, :], ALU.add).then_inc(S("rootr_used"), 1)
            dve.wait_ge(S("rootr_used"), 2)

            def residual_product(j, nj, n, p_):
                bb = Bn[0:Q, j:j + nj, :]
                tt(bb, p_, rb2.to_broadcast([Q, nj, D]), ALU.add).then_inc(S("ring_ev"), 1)
                dve.wait_ge(S("ring_ev"), base["m3"] + n + 1)
                link(stt(bb, bb, 0.01, bb, ALU.mult, ALU.max))
                xx = X[0:Q, j:j + nj, :]
                link(tt(xx, xx, bb, ALU.add))
                for m in range(nj):
                    stats_of(j + m)

            mixed_out("m3", residual_product)
            ln_scale(2)
            dve.wait_ge(S("w2T_pe"), 1)
            cp(w2T[:, :, :].rearrange("p k n -> p (k n)"), ps[:, 7, :]).then_inc(S("w2T_made"), 1)

            dve.wait_ge(S("deg_std"), 1)
            link(v_.reciprocal(norm[0:Q, :], norm[0:Q, :]))

            def normed_product(j, nj, n, p_):
                bb = Bn[0:Q, j:j + nj, :]
                link(tt(bb, p_, bcs[0:Q, 3, :].unsqueeze(1).to_broadcast([Q, nj, D]), ALU.add))
                tt(bb, bb, norm[0:Q, j:j + nj].unsqueeze(2).to_broadcast([Q, nj, D]), ALU.mult)\
                    .then_inc(S("ring_ev"), 1)

            mixed_out("m4", normed_product)

            def out_residual(name, col):
                def f(i, s):
                    xi = X[0:Q, bass.ds(i, 1), :].rearrange("p o f -> p (o f)")
                    stt(xi, acc[s], col(i, s), xi, ALU.mult, ALU.add).then_inc(S(name + "out"), 1)
                    dve.wait_ge(S(name + "out"), i + (1 + CREDIT))
                    stats_of(i)
                return f

            plain_pass("L2", out_residual("L2", lambda i, s: norm[0:Q, bass.ds(i, 1)]))
            dve.wait_ge(S("L2out"), NB + CREDIT)

            dve.sem_inc(S("L3alnc_used"), CREDIT)
            ln_scale(3)
            features_out("h5")
            dve.wait_ge(S("ald_mm"), 1)
            cols8 = ps[0:Q, 6, 0:NB * 2 * HEADS].rearrange("p (j w h) -> p w h j", w=2, h=HEADS)
            cp(alsc[0:Q, 0:HEADS * NB].rearrange("p (h j) -> p h j", h=HEADS), cols8[:, 0]).then_inc(S("alsc_made"), 1)
            cp(ald[0:Q, :, :].rearrange("p j h -> p h j"), cols8[:, 1]).then_inc(S("ald_made"), 1)
            dve.wait_ge(S("alsT_pe"), 1)
            cp(alsr[0:HEADS * NB, 0:Q], ps[0:HEADS * NB, 7, 0:Q]).then_inc(S("alsrow_made"), 1)
            tt(X[0:Q, :, :], X[0:Q, :, :], bcs[0:Q, 4, :].unsqueeze(1).to_broadcast([Q, NB, D]), ALU.add)\
                .then_inc(S("bias_in_x"), 1)

            def leaky(name, t, u, du):
                dve.wait_ge(S(name + "score"), u + 1)
                link(stt(t[0:Q, :], t[0:Q, :], 0.2, t[0:Q, :], ALU.mult, ALU.max))

            def mask(name, t, du, rs, klnc, last_use):
                if klnc is not None:
                    dve.wait_ge(S(f"{name}lnc{rs}"), klnc)
                dve.sem_inc(S("masks_begun"), 1)
                link(v_.tensor_tensor_reduce(t[0:Q, :], t[0:Q, :], lncR[rs][0:Q, :], 1.0, 2.0 * NEG,
                                             ALU.add, ALU.max, accum_out=mx[0:Q, 0, du:du + 1]))
                ts(mx[0:Q, 1, du:du + 1], mx[0:Q, 0, du:du + 1], -1.0, None, ALU.mult).then_inc(S(name + "max"), 1)
                if last_use:
                    dve.sem_inc(S(name + "lnc_used"), 1)

            def inverse(u, du):
                link(v_.reciprocal(mx[0:Q, 3, du:du + 1], mx[0:Q, 2, du:du + 1]))

            def attention_out(u, du):
                inverse(u, du)
                dve.wait_ge(S("L3amm"), u * NG + (NG + RING))
                ts(ag[0:Q, du % 2, :], acc[du % 2], mx[0:Q, 3, du:du + 1], None, ALU.mult).then_inc(S("L3aout"), 1)

            def wide_in(u):
                dve.wait_ge(S("agT_pe"), u + 1)
                cp(agT[:, :, :].rearrange("p t q -> p (t q)"), ps[:, 6, 0:KT * Q]).then_inc(S("agT_made"), 1)

            def wide_out(u, hd, ys, i):
                if hd == 0:
                    dve.wait_ge(S("y_free"), i + 1)
                dve.wait_ge(S("y_pe"), u + 1)
                for c in range(KT):
                    t = hd * KT + c
                    link.mark(ts(yT[:, ys, t, :], ps[:, 7, c * Q:(c + 1) * Q], colw[:, 0, t:t + 1], None, ALU.add))
                link.join()
                if hd == HEADS - 1:
                    for t in range(CT):
                        last = v_.bn_stats(gst[:, t, bass.ds(i * 6, 6)], yT[:, ys, t, :])
                    last.then_inc(S("y_made"), 1)

            U = 4 * NB

            def step(t, dt8, i8, v):
                def unit(d):
                    return t + d, (dt8 + d) % 4
                done = dt8 == 0 and isinstance(t, int) and t == 0
                ahead = not (isinstance(t, int) and t + 2 >= U)
                u2, d2 = unit(2)
                blk = (dt8 + 2) // 4
                evac("L3a", t, dt8 % 4, 1)
                if ahead:
                    leaky("L3a", scr[0][d2], u2, d2)
                if not done:
                    attention_out(*unit(-1))
                evac("L3a", t, dt8 % 4, 3)
                if ahead:
                    mask("L3a", scr[0][d2], d2, blk % 2, (v + blk // 2 + 1) * 16 if d2 == 0 else None, d2 == 3)
                if not done:
                    wide_in(t - 1)
                evac("L3a", t, dt8 % 4, 5)
                if not done:
                    b1 = (dt8 - 1) // 4
                    wide_out(t - 1, (dt8 - 1) % 4, b1 % 2, i8 + b1)

            dve.sem_inc(S("L3aout"), CREDIT)
            for u in range(2):
                leaky("L3a", scr[0][u], u, u)
                mask("L3a", scr[0][u], u, 0, 16, False)
            step(0, 0, 0, 0)
            for v in link.loop(U // 8, 8 * 5):
                for k in range(1, 9):
                    step(v * 8 + k, k, v * 2, v)
            v = U // 8
            for k in range(1, 4):
                step(8 * v + k, k, 2 * v, v)
            attention_out(U - 1, 3)
            wide_in(U - 1)
            wide_out(U - 1, 3, 0, NB - 1)
            dve.wait_ge(S("y_made"), NB)

            for t in range(CT):
                link.mark(v_.bn_aggr(mv[:, t, :], gst[:, t, :]))
            link.join()
            link(ts(aff[:, 4, :], colw[:, 3, :], -1.0, 1.0, ALU.mult, ALU.add))
            link(tt(aff[:, 4, :], aff[:, 4, :], mv[:, :, 0], ALU.mult))
            link(tt(aff[:, 4, :], aff[:, 4, :], aff[:, 4, :], ALU.mult))
            stt(aff[:, 0, :], mv[:, :, 1], BN_EPS, aff[:, 4, :], ALU.add, ALU.add).then_inc(S("gn_var"), 1)
            dve.wait_ge(S("gn_std"), 1)
            link(v_.reciprocal(aff[:, 1, :], aff[:, 1, :]))
            link(tt(aff[:, 2, :], aff[:, 1, :], colw[:, 1, :], ALU.mult))
            link(tt(aff[:, 4, :], colw[:, 3, :], mv[:, :, 0], ALU.mult))
            link(tt(aff[:, 4, :], aff[:, 4, :], aff[:, 2, :], ALU.mult))
            tt(aff[:, 3, :], colw[:, 2, :], aff[:, 4, :], ALU.subtract).then_inc(S("gn_aff"), 1)

            dve.sem_inc(S("L3blnc_used"), CREDIT)
            for n in range(NB):
                dve.wait_ge(S("ring_pe"), base["z3"] + n + 1)
                cp(Bn[0:Q, n, :], ps[0:Q, n % 4, 0:D])
                cp(ald[0:Q, n, 0:2], ps[0:Q, n % 4, D:D + 2]).then_inc(S("ring_ev"), 1)
            dve.wait_ge(S("als2_pe"), 1)
            cp(alsr[0:NB, 0:Q], ps[0:NB, 6, 0:Q]).then_inc(S("row2_made"), 1)
            dve.wait_ge(S("row2_out"), 16)

            dve.sem_inc(S("L3bout"), CREDIT)
            dve.wait_ge(S("x_back"), 16)

            def last_out(u, du):
                inverse(u, du)
                dve.wait_ge(S("L3bmm"), u * NG + (NG + RING))
                xi = X[0:Q, bass.ds(u, 1), :].rearrange("p o f -> p (o f)")
                stt(xi, acc[du % 2], mx[0:Q, 3, du:du + 1], xi, ALU.mult, ALU.add).then_inc(S("L3bout"), 1)

            def last_step(t, dt, v):
                ahead = not (isinstance(t, int) and t + 2 >= NB)
                d2 = (dt + 2) % 4
                evac("L3b", t, dt % 4, 1)
                if ahead:
                    leaky("L3b", scr[1][d2], t + 2, d2)
                if not (isinstance(t, int) and t == 0):
                    last_out(t - 1, (dt - 1) % 4)
                evac("L3b", t, dt % 4, 3)
                if ahead:
                    mask("L3b", scr[1][d2], d2, dt % 2, (v * 2 + (dt + 2) // 2 + 1) * 16, True)
                evac("L3b", t, dt % 4, 5)

            for u in range(2):
                leaky("L3b", scr[1][u], u, u)
                mask("L3b", scr[1][u], u, u, 16, True)
            last_step(0, 0, 0)
            for v in link.loop(NB // 4 - 1, 4 * 3):
                for k in range(1, 5):
                    last_step(v * 4 + k, k, v)
            v = NB // 4 - 1
            for k in range(1, 5):
                last_step(v * 4 + k, k, v)
            last_out(NB - 1, 0)


_INS = ["x", "src", "dst", "edge_weight", "L0_gnn_eps", "L0_gnn_W1", "L0_gnn_b1", "L0_gnn_g1", "L0_gnn_be1",
        "L0_gnn_W2", "L0_gnn_b2", "L0_gnn_g2", "L0_gnn_be2", "L1_gnn_W1", "L1_gnn_b1", "L1_gnn_W2", "L1_gnn_b2",
        "L1_gnn_Wl", "L1_gnn_bl", "L1_gnn_root_idx", "L2_gnn_W", "L2_gnn_b", "L3_gnn_W1", "L3_gnn_att_src1",
        "L3_gnn_att_dst1", "L3_gnn_b1", "L3_gnn_gn_w", "L3_gnn_gn_b", "L3_gnn_gn_ms", "L3_gnn_W2",
        "L3_gnn_att_src2", "L3_gnn_att_dst2", "L3_gnn_b2"]


def kernel(**inputs):
    import numpy as _np
    import concourse.bacc as _bacc
    from concourse import mybir as _mybir
    from concourse.bass_utils import run_bass_kernel_spmd as _run

    nc = _bacc.Bacc("TRN2", target_bir_lowering=False, num_devices=1)
    arrays, args = {}, []
    for name in _INS:
        a = _np.ascontiguousarray(inputs[name])
        arrays["in_" + name] = a
        args.append(nc.dram_tensor("in_" + name, a.shape, _mybir.dt.from_np(a.dtype), kind="ExternalInput").ap())
    args.append(nc.dram_tensor("out_0", (N, D), F32, kind="ExternalOutput").ap())
    gnn_stack(nc, *args)
    r = _run(nc, [arrays], core_ids=[0])
    return r.results[0]["out_0"]
```
